# Optimizing a Trainium2 kernel written in Bass

```python
import numpy as np
import jax
import jax.numpy as jnp

def _softmax(x, axis=-1):
    return jax.nn.softmax(x, axis=axis)
def _gelu(x):
    return jax.nn.gelu(x, approximate=True)
def _silu(x):
    return jax.nn.silu(x)
def _sigmoid(x):
    return jax.nn.sigmoid(x)
def _layernorm(x, axis=-1, eps=1e-5):
    m = jnp.mean(x, axis=axis, keepdims=True)
    v = jnp.var(x, axis=axis, keepdims=True)
    return (x - m) / jnp.sqrt(v + eps)
def _scatter_add(tgt, idx, src, axis=0):
    return tgt.at[idx].add(src)
def _segment_sum(src, seg, n):
    return jax.ops.segment_sum(src, seg, n)

kernel_name = 'mk_conv_preact_d4_conv_nhwc128_23178b'

def setup_inputs(seed: int = 0):
    np.random.seed(seed)
    _w = jnp.asarray
    def _rec_inputs():
        import jax
        import jax.numpy as jnp
        _gk = jax.random.key(seed)
        x = 7.22e-05 + 1 * jax.random.normal(jax.random.fold_in(_gk, 1), (1, 256, 256, 128), jnp.float32)
        return x
    x = _rec_inputs()
    def _L0_conv_setup():
        import jax, jax.numpy as jnp
        import numpy as np
        C_Z = 128
        N_HEADS = 4
        HEAD_DIM = 32
        TOTAL = N_HEADS * HEAD_DIM
        B, N = (1, 256)
        key = jax.random.key(seed)
        ks = jax.random.split(key, 10)
        s = lambda k, sh: jax.random.normal(k, sh, dtype=jnp.float32) * 0.02
        return {'pair_representation': jax.random.normal(ks[0], (B, N, N, C_Z), dtype=jnp.float32), 'ln_gamma': jnp.ones((C_Z,), jnp.float32), 'ln_beta': jnp.zeros((C_Z,), jnp.float32), 'Wq': s(ks[1], (C_Z, TOTAL)), 'Wk': s(ks[2], (C_Z, TOTAL)), 'Wv': s(ks[3], (C_Z, TOTAL)), 'Wb': s(ks[4], (C_Z, N_HEADS)), 'Wg': s(ks[5], (C_Z, TOTAL)), 'bg': jnp.zeros((TOTAL,), jnp.float32), 'Wo': s(ks[6], (TOTAL, C_Z)), 'bo': jnp.zeros((C_Z,), jnp.float32)}
    _L0_conv_all = _L0_conv_setup()
    _L0_conv_in = {k: v for k, v in _L0_conv_all.items() if k in ('ln_gamma', 'ln_beta', 'Wq', 'Wk', 'Wv', 'Wb', 'Wg', 'bg', 'Wo', 'bo', )}
    del _L0_conv_all

    def _L1_conv_setup():
        import jax, jax.numpy as jnp
        import numpy as np
        B, H, W_DIM, C = (8, 128, 256, 128)
        K = 9

        def conv1d_same(y, W):
            return jax.lax.conv_general_dilated(y, W, window_strides=(1,), padding='SAME', dimension_numbers=('NWC', 'WIO', 'NWC'))
        key = jax.random.key(seed)
        kx, kw = jax.random.split(key)
        x = jax.random.normal(kx, (B, H, W_DIM, C), dtype=jnp.float32)
        W = jax.random.normal(kw, (K, C, C), dtype=jnp.float32) * 0.02
        return {'x': x, 'W': W}
    _L1_conv_all = _L1_conv_setup()
    _L1_conv_in = {k: v for k, v in _L1_conv_all.items() if k in ('W', )}
    del _L1_conv_all

    def _L2_conv_setup():
        import jax, jax.numpy as jnp
        import numpy as np
        EPS = 1e-05

        def _layernorm(x, g, b):
            mu = jnp.mean(x, axis=-1, keepdims=True)
            var = jnp.var(x, axis=-1, keepdims=True)
            return (x - mu) * jax.lax.rsqrt(var + EPS) * g + b
        key = jax.random.key(seed)
        ks = jax.random.split(key, 16)
        B, N, C, H = (1, 512, 128, 128)

        def xavier(k, shape):
            fan_out, fan_in = shape
            std = (2.0 / (fan_in + fan_out)) ** 0.5
            return jax.random.normal(k, shape, dtype=jnp.float32) * std
        return {'pair': jax.random.normal(ks[0], (B, N, N, C), dtype=jnp.float32), 'ln_g': jnp.ones((C,), jnp.float32), 'ln_b': jnp.zeros((C,), jnp.float32), 'lnh_g': jnp.ones((H,), jnp.float32), 'lnh_b': jnp.zeros((H,), jnp.float32), 'Wa': xavier(ks[1], (H, C)), 'ba': jnp.zeros((H,), jnp.float32), 'Ga': xavier(ks[2], (H, C)), 'bga': jnp.zeros((H,), jnp.float32), 'Wb': xavier(ks[3], (H, C)), 'bb': jnp.zeros((H,), jnp.float32), 'Gb': xavier(ks[4], (H, C)), 'bgb': jnp.zeros((H,), jnp.float32), 'Wo': xavier(ks[5], (C, H)), 'bo': jnp.zeros((C,), jnp.float32), 'Wg': xavier(ks[6], (C, C)), 'bg': jnp.zeros((C,), jnp.float32)}
    _L2_conv_all = _L2_conv_setup()
    _L2_conv_in = {k: v for k, v in _L2_conv_all.items() if k in ('ln_g', 'ln_b', 'lnh_g', 'lnh_b', 'Wa', 'ba', 'Ga', 'bga', 'Wb', 'bb', 'Gb', 'bgb', 'Wo', 'bo', 'Wg', 'bg', )}
    del _L2_conv_all

    def _L3_conv_setup():
        import jax, jax.numpy as jnp
        import numpy as np
        B, H, W, C, K, T = (16, 128, 128, 64, 7, 16)
        C2 = 2 * C

        def _pad_and_fft(kr, ki, h, w, k):
            kern = kr + 1j * ki
            ph = (h - k) // 2
            pw = (w - k) // 2
            padded = jnp.pad(kern, ((0, 0), (ph, h - k - ph), (pw, w - k - pw)))
            return jnp.fft.fft2(padded, axes=(-2, -1))
        key = jax.random.key(seed)
        ks = jax.random.split(key, 12)
        d = {'x_ri': jax.random.normal(ks[0], (B, H, W, C2), jnp.float32), 'Wf': jax.random.normal(ks[1], (C2, C2), jnp.float32) * 0.05, 'bf': jnp.zeros((C2,), jnp.float32), 'Wi': jax.random.normal(ks[2], (C2, C2), jnp.float32) * 0.05, 'bi': jnp.zeros((C2,), jnp.float32), 'Wd': jax.random.normal(ks[3], (C2, C2), jnp.float32) * 0.05, 'bd': jnp.zeros((C2,), jnp.float32), 'A_real': jax.random.normal(ks[4], (C, K, K), jnp.float32) * 0.02, 'A_imag': jax.random.normal(ks[5], (C, K, K), jnp.float32) * 0.02, 'B_real': jax.random.normal(ks[6], (C, K, K), jnp.float32) * 0.02, 'B_imag': jax.random.normal(ks[7], (C, K, K), jnp.float32) * 0.02}
        return d
    _L3_conv_all = _L3_conv_setup()
    _L3_conv_in = {k: v for k, v in _L3_conv_all.items() if k in ('Wf', 'bf', 'Wi', 'bi', 'Wd', 'bd', 'A_real', 'A_imag', 'B_real', 'B_imag', )}
    del _L3_conv_all

    return {
        "x": x,
        "L0_conv_ln_gamma": _L0_conv_in["ln_gamma"],
        "L0_conv_ln_beta": _L0_conv_in["ln_beta"],
        "L0_conv_Wq": _L0_conv_in["Wq"],
        "L0_conv_Wk": _L0_conv_in["Wk"],
        "L0_conv_Wv": _L0_conv_in["Wv"],
        "L0_conv_Wb": _L0_conv_in["Wb"],
        "L0_conv_Wg": _L0_conv_in["Wg"],
        "L0_conv_bg": _L0_conv_in["bg"],
        "L0_conv_Wo": _L0_conv_in["Wo"],
        "L0_conv_bo": _L0_conv_in["bo"],
        "L1_conv_W": _L1_conv_in["W"],
        "L2_conv_ln_g": _L2_conv_in["ln_g"],
        "L2_conv_ln_b": _L2_conv_in["ln_b"],
        "L2_conv_lnh_g": _L2_conv_in["lnh_g"],
        "L2_conv_lnh_b": _L2_conv_in["lnh_b"],
        "L2_conv_Wa": _L2_conv_in["Wa"],
        "L2_conv_ba": _L2_conv_in["ba"],
        "L2_conv_Ga": _L2_conv_in["Ga"],
        "L2_conv_bga": _L2_conv_in["bga"],
        "L2_conv_Wb": _L2_conv_in["Wb"],
        "L2_conv_bb": _L2_conv_in["bb"],
        "L2_conv_Gb": _L2_conv_in["Gb"],
        "L2_conv_bgb": _L2_conv_in["bgb"],
        "L2_conv_Wo": _L2_conv_in["Wo"],
        "L2_conv_bo": _L2_conv_in["bo"],
        "L2_conv_Wg": _L2_conv_in["Wg"],
        "L2_conv_bg": _L2_conv_in["bg"],
        "L3_conv_Wf": _L3_conv_in["Wf"],
        "L3_conv_bf": _L3_conv_in["bf"],
        "L3_conv_Wi": _L3_conv_in["Wi"],
        "L3_conv_bi": _L3_conv_in["bi"],
        "L3_conv_Wd": _L3_conv_in["Wd"],
        "L3_conv_bd": _L3_conv_in["bd"],
        "L3_conv_A_real": _L3_conv_in["A_real"],
        "L3_conv_A_imag": _L3_conv_in["A_imag"],
        "L3_conv_B_real": _L3_conv_in["B_real"],
        "L3_conv_B_imag": _L3_conv_in["B_imag"],
    }

def reference(x, L0_conv_ln_gamma, L0_conv_ln_beta, L0_conv_Wq, L0_conv_Wk, L0_conv_Wv, L0_conv_Wb, L0_conv_Wg, L0_conv_bg, L0_conv_Wo, L0_conv_bo, L1_conv_W, L2_conv_ln_g, L2_conv_ln_b, L2_conv_lnh_g, L2_conv_lnh_b, L2_conv_Wa, L2_conv_ba, L2_conv_Ga, L2_conv_bga, L2_conv_Wb, L2_conv_bb, L2_conv_Gb, L2_conv_bgb, L2_conv_Wo, L2_conv_bo, L2_conv_Wg, L2_conv_bg, L3_conv_Wf, L3_conv_bf, L3_conv_Wi, L3_conv_bi, L3_conv_Wd, L3_conv_bd, L3_conv_A_real, L3_conv_A_imag, L3_conv_B_real, L3_conv_B_imag):
    import jax
    import jax.numpy as jnp
    def _L0_conv_ref(pair_representation, ln_gamma, ln_beta, Wq, Wk, Wv, Wb, Wg, bg, Wo, bo):
        import jax, jax.numpy as jnp
        import numpy as np
        C_Z = 128
        N_HEADS = 4
        HEAD_DIM = 32
        TOTAL = N_HEADS * HEAD_DIM
        B, N = (1, 256)
        x = pair_representation
        mu = jnp.mean(x, axis=-1, keepdims=True)
        var = jnp.mean((x - mu) ** 2, axis=-1, keepdims=True)
        x = (x - mu) * jax.lax.rsqrt(var + 1e-05) * ln_gamma + ln_beta
        b, n, _, _ = x.shape
        split = lambda t: t.reshape(b, n, n, N_HEADS, HEAD_DIM)
        Q = split(x @ Wq)
        K = split(x @ Wk)
        V = split(x @ Wv)
        G = jax.nn.sigmoid(split(x @ Wg + bg))
        Bias = x @ Wb
        scores = jnp.einsum('bijhd,bikhd->bijkh', Q, K) / np.float32(np.sqrt(HEAD_DIM))
        scores = scores + Bias[:, None]
        attn = jax.nn.softmax(scores, axis=3)
        vals = jnp.einsum('bijkh,bikhd->bijhd', attn, V)
        vals = (G * vals).reshape(b, n, n, TOTAL)
        return vals @ Wo + bo

    def _L1_conv_ref(x, W):
        import jax, jax.numpy as jnp
        import numpy as np
        B, H, W_DIM, C = (8, 128, 256, 128)
        K = 9

        def conv1d_same(y, W):
            return jax.lax.conv_general_dilated(y, W, window_strides=(1,), padding='SAME', dimension_numbers=('NWC', 'WIO', 'NWC'))
        rows = jnp.moveaxis(x, 1, 0)
        row0 = rows[0]

        def step(carry, row):
            new = row + jax.nn.relu(conv1d_same(carry, W))
            return (new, new)
        _, outs = jax.lax.scan(step, row0, rows[1:])
        out = jnp.concatenate([row0[None], outs], axis=0)
        return jnp.moveaxis(out, 0, 1)

    def _L2_conv_ref(pair, ln_g, ln_b, lnh_g, lnh_b, Wa, ba, Ga, bga, Wb, bb, Gb, bgb, Wo, bo, Wg, bg):
        import jax, jax.numpy as jnp
        import numpy as np
        EPS = 1e-05

        def _layernorm(x, g, b):
            mu = jnp.mean(x, axis=-1, keepdims=True)
            var = jnp.var(x, axis=-1, keepdims=True)
            return (x - mu) * jax.lax.rsqrt(var + EPS) * g + b
        z = _layernorm(pair, ln_g, ln_b)
        a = (z @ Wa.T + ba) * jax.nn.sigmoid(z @ Ga.T + bga)
        b = (z @ Wb.T + bb) * jax.nn.sigmoid(z @ Gb.T + bgb)
        g_o = jax.nn.sigmoid(z @ Wg.T + bg)
        t = jnp.einsum('bikh,bjkh->bijh', a, b)
        t = _layernorm(t, lnh_g, lnh_b)
        out = (t @ Wo.T + bo) * g_o
        return out

    def _L3_conv_ref(x_ri, Wf, bf, Wi, bi, Wd, bd, A_real, A_imag, B_real, B_imag):
        import jax, jax.numpy as jnp
        import numpy as np
        B, H, W, C, K, T = (16, 128, 128, 64, 7, 16)
        C2 = 2 * C

        def _pad_and_fft(kr, ki, h, w, k):
            kern = kr + 1j * ki
            ph = (h - k) // 2
            pw = (w - k) // 2
            padded = jnp.pad(kern, ((0, 0), (ph, h - k - ph), (pw, w - k - pw)))
            return jnp.fft.fft2(padded, axes=(-2, -1))
        b, h, w, c2 = x_ri.shape
        c = c2 // 2
        k = A_real.shape[-1]
        forget_gate = jax.nn.sigmoid(x_ri @ Wf + bf + 2.0)
        input_gate = jax.nn.sigmoid(x_ri @ Wi + bi)
        delta = jax.nn.softplus(x_ri @ Wd + bd) * 0.1
        A_f = _pad_and_fft(A_real, A_imag, h, w, k)
        B_f = _pad_and_fft(B_real, B_imag, h, w, k)
        A_ri = jnp.concatenate([A_f.real, A_f.imag], 0).transpose(1, 2, 0)[None]
        B_ri = jnp.concatenate([B_f.real, B_f.imag], 0).transpose(1, 2, 0)[None]
        Ar, Ai = (A_ri[..., :c], A_ri[..., c:])
        mag = jnp.sqrt(Ar ** 2 + Ai ** 2 + 1e-08)
        scale = 0.95 * jax.nn.sigmoid(mag) / (mag + 1e-08)
        Ar = Ar * scale
        Ai = Ai * scale
        Br, Bi_ = (B_ri[..., :c], B_ri[..., c:])
        x_r, x_i = (x_ri[..., :c], x_ri[..., c:])
        Bx_r = Br * x_r - Bi_ * x_i
        Bx_i = Br * x_i + Bi_ * x_r
        inp_r = delta[..., :c] * input_gate[..., :c] * Bx_r
        inp_i = delta[..., c:] * input_gate[..., c:] * Bx_i
        fg_r, fg_i = (forget_gate[..., :c], forget_gate[..., c:])

        def step(h_state, _):
            h_r, h_i = h_state
            Ah_r = Ar * h_r - Ai * h_i
            Ah_i = Ar * h_i + Ai * h_r
            return ((fg_r * Ah_r + inp_r, fg_i * Ah_i + inp_i), None)
        h0 = (jnp.zeros_like(x_r), jnp.zeros_like(x_i))
        (h_r, h_i), _ = jax.lax.scan(step, h0, None, length=T)
        return jnp.concatenate([h_r, h_i], axis=-1)

    def _gn(v, G=32, eps=1e-5):
        B_, H_, W_, C_ = v.shape
        g = v.reshape(B_, H_, W_, G, C_ // G)
        m = jnp.mean(g, axis=(1, 2, 4), keepdims=True)
        s = jnp.var(g, axis=(1, 2, 4), keepdims=True)
        return ((g - m) / jnp.sqrt(s + eps)).reshape(v.shape)

    def _ln_c(v, eps=1e-6):
        m = jnp.mean(v, axis=-1, keepdims=True)
        s = jnp.var(v, axis=-1, keepdims=True)
        return (v - m) / jnp.sqrt(s + eps)

    def _ln_t(v, eps=1e-5):
        m = jnp.mean(v, axis=-1, keepdims=True)
        s = jnp.var(v, axis=-1, keepdims=True)
        return (v - m) / jnp.sqrt(s + eps)

    def _to_tokens(v):
        B_, H_, W_, C_ = v.shape
        return v.reshape(B_, H_ * W_, C_)
    def _from_tokens(t, like):
        return t.reshape(like.shape)

    x = x + _L0_conv_ref(_gn(x), L0_conv_ln_gamma, L0_conv_ln_beta, L0_conv_Wq, L0_conv_Wk, L0_conv_Wv, L0_conv_Wb, L0_conv_Wg, L0_conv_bg, L0_conv_Wo, L0_conv_bo)
    x = x + _L1_conv_ref(_gn(x), L1_conv_W)
    x = x + _L2_conv_ref(_gn(x), L2_conv_ln_g, L2_conv_ln_b, L2_conv_lnh_g, L2_conv_lnh_b, L2_conv_Wa, L2_conv_ba, L2_conv_Ga, L2_conv_bga, L2_conv_Wb, L2_conv_bb, L2_conv_Gb, L2_conv_bgb, L2_conv_Wo, L2_conv_bo, L2_conv_Wg, L2_conv_bg)
    x = x + _L3_conv_ref(_gn(x), L3_conv_Wf, L3_conv_bf, L3_conv_Wi, L3_conv_bi, L3_conv_Wd, L3_conv_bd, L3_conv_A_real, L3_conv_A_imag, L3_conv_B_real, L3_conv_B_imag)
    return x


_drawn_inputs = setup_inputs


def setup_inputs(seed=0):
    import zlib

    import numpy as np

    out = dict(_drawn_inputs(seed))
    spreads = {'L0_conv_ln_gamma': (1.0, 0.6),
     'L0_conv_ln_beta': (0.0, 0.8),
     'L0_conv_bg': (0.0, 0.8),
     'L0_conv_bo': (0.0, 0.1),
     'L2_conv_ln_g': (1.0, 0.2),
     'L2_conv_ln_b': (0.0, 0.1),
     'L2_conv_lnh_g': (1.0, 0.6),
     'L2_conv_lnh_b': (0.0, 0.317),
     'L2_conv_ba': (0.0, 0.305),
     'L2_conv_bga': (0.0, 0.794),
     'L2_conv_bb': (0.0, 0.319),
     'L2_conv_bgb': (0.0, 0.8),
     'L2_conv_bo': (0.0, 0.313),
     'L2_conv_bg': (0.0, 0.723),
     'L3_conv_bf': (0.0, 2.0),
     'L3_conv_bi': (0.0, 2.0),
     'L3_conv_bd': (0.0, 2.0)}
    factors = {'L0_conv_Wq': 8.0,
     'L0_conv_Wk': 8.0,
     'L0_conv_Wv': 8.0,
     'L0_conv_Wb': 8.0,
     'L0_conv_Wg': 8.0,
     'L0_conv_Wo': 8.0,
     'L3_conv_Wf': 8.0,
     'L3_conv_Wi': 8.0,
     'L3_conv_Wd': 8.0,
     'L3_conv_A_real': 8.0,
     'L3_conv_A_imag': 8.0,
     'L3_conv_B_real': 8.0,
     'L3_conv_B_imag': 8.0}
    for name, (base, spread) in spreads.items():
        noise = np.random.default_rng([zlib.crc32(name.encode()), seed]).standard_normal(out[name].shape)
        drawn = base * np.exp(spread * noise) if base else spread * noise
        out[name] = jnp.asarray(drawn.astype(out[name].dtype))
    for name, factor in factors.items():
        out[name] = (out[name] * factor).astype(out[name].dtype)
    return out
```

```python
import concourse.bass as bass
from concourse import mybir
from contextlib import ExitStack, contextmanager

F32 = mybir.dt.float32
BF16 = mybir.dt.bfloat16
ALU = mybir.AluOpType
ACT = mybir.ActivationFunctionType

P = 128
N = 256
TOK = N * N
HEADS, HD = 4, 32
CH = 512
NCH = TOK // CH
HALF = N // P
EPS = 1e-5


def wait_count(eng, sem, value):
    if isinstance(value, int) and value <= 0:
        return
    eng.wait_ge(sem, value)


def wait_counts(eng, passed, *counts):
    for sem, value in counts:
        wait_count(eng, sem, value)
    eng.sem_inc(passed, 1)


LOG_EXP_SET = 6


def load_log_exp(nc, act):
    act.add_instruction(mybir.InstLoadActFuncSet(
        name=nc.get_next_instruction_name(), act_func_set_id=LOG_EXP_SET, engine=mybir.EngineType.Activation))


def looped(eng, first, last, peel, body, tail=0):
    for i in range(first, first + peel):
        body(i)
    with eng.Fori(first + peel, last - tail) as i:
        body(i)
    for i in range(last - tail, last):
        body(i)


@contextmanager
def phase_semaphores(nc):
    given = []

    def sem(name):
        given.append(nc.alloc_semaphore(name))
        return given[-1]

    yield sem
    nc.clear_and_free_semaphores(given)
    nc.all_engine_barrier()


def linker(eng, sem):
    done = [0]

    def link(ins):
        done[0] += 1
        ins.then_inc(sem, 1)
        eng.wait_ge(sem, done[0])

    return link


class Schedule:
    def __init__(self, rounds, first_slot, steps):
        self.rounds, self.first_slot = rounds, first_slot
        self.ahead = {step: ahead for one in steps.values() for step, ahead in one}
        self.per_slot = {step: len(one) for one in steps.values() for step, _ in one}
        self.place = {step: n + 1 for one in steps.values() for n, (step, _) in enumerate(one)}

    def run(self, eng, slot):
        for s in range(self.first_slot, 2):
            slot(s // 2, s % 2)
        with eng.Fori(1, self.rounds // 2 - 2) as i:
            for r in range(2):
                slot(i, r)
        for s in range(self.rounds - 4, self.rounds):
            slot(s // 2, s % 2)


class Slot:
    def __init__(self, schedule, eng, done, i, r):
        self.schedule, self.eng, self.done, self.i, self.r = schedule, eng, done, i, r

    def runs(self, step, lag=0):
        return not isinstance(self.i, int) or 0 <= 2 * self.i + self.r + self.schedule.ahead[step] - lag < self.schedule.rounds

    def at(self, step, other, lag=0):
        S = self.schedule
        slots = self.r + S.ahead[step] - lag - S.ahead[other] - S.first_slot
        return self.i * (2 * S.per_slot[other]) + (slots * S.per_slot[other] + S.place[other])

    def on(self, step):
        self.parity = (self.r + self.schedule.ahead[step]) % 2
        if self.runs(step):
            return True
        wait_count(self.eng, self.done, self.at(step, step) - 1)
        self.eng.sem_inc(self.done, 1)
        return False

    def moved(self, sems, step, count, lag=0):
        ahead = self.r + self.schedule.ahead[step] - lag
        return sems[ahead % 2], (self.i * count + (ahead // 2 + 1) * count) if self.runs(step, lag) else 0


def group_norm_affine(nc, name, stats, const, affine, ps):
    with ExitStack() as ctx:
        sb = lambda n, s: ctx.enter_context(nc.sbuf_tensor(f"{name}_{n}", s, F32))
        new_sem = ctx.enter_context(phase_semaphores(nc))
        sem = lambda n: new_sem(f"{name}_" + n)
        mv, diff, spread, sd = sb("mv", [P, 2]), sb("diff", [P, 1]), sb("spread", [P, 1]), sb("sd", [P, 2])
        aggregated, group_mean_done, spread_done, group_var_done = (
            sem("aggregated"), sem("group_mean_done"), sem("spread_done"), sem("group_var_done"))
        var_ready, sd_ready, affine_ready, cen_offset_done, chain = (
            sem("var_ready"), sem("sd_ready"), sem("affine_ready"), sem("cen_offset_done"), sem("chain"))
        block = ctx.enter_context(nc.Block())

        @block.vector
        def _(dve):
            link = linker(dve, chain)
            nc.vector.bn_aggr(mv[:, :], stats).then_inc(aggregated, 1)
            dve.wait_ge(aggregated, 1)
            dve.wait_ge(group_mean_done, 1)
            link(nc.vector.tensor_tensor(diff[:, :], mv[:, 0:1], ps[:, 0, 0:1], ALU.subtract))
            nc.vector.scalar_tensor_tensor(spread[:, :], diff[:, :], diff[:, :], mv[:, 1:2],
                                           ALU.mult, ALU.add).then_inc(spread_done, 1)
            dve.wait_ge(group_var_done, 1)
            nc.vector.tensor_scalar(sd[:, 0:1], ps[:, 1, 0:1], EPS, None, ALU.add).then_inc(var_ready, 1)
            dve.wait_ge(sd_ready, 1)
            link(nc.vector.reciprocal(affine[:, 0:1], sd[:, 1:2]))
            nc.vector.scalar_tensor_tensor(affine[:, 1:2], ps[:, 0, 0:1], -1.0, affine[:, 0:1],
                                           ALU.mult, ALU.mult).then_inc(affine_ready, 1)
            link(nc.vector.tensor_scalar(affine[:, 2:2 + P], const["center"][:, :], affine[:, 0:1], None, ALU.mult))
            dve.wait_ge(cen_offset_done, 1)
            link(nc.vector.tensor_copy(affine[:, 2 + P:3 + P], ps[:, 2, 0:1]))

        @block.tensor
        def _(pe):
            pe.wait_ge(aggregated, 1)
            nc.tensor.matmul(ps[:, 0, 0:1], const["group_mean"][:, :], mv[:, 0:1],
                             start=True, stop=True).then_inc(group_mean_done, 1)
            pe.wait_ge(spread_done, 1)
            nc.tensor.matmul(ps[:, 1, 0:1], const["group_mean"][:, :], spread[:, :],
                             start=True, stop=True).then_inc(group_var_done, 1)
            pe.wait_ge(affine_ready, 1)
            nc.tensor.matmul(ps[:, 2, 0:1], const["center"][:, :], affine[:, 1:2],
                             start=True, stop=True).then_inc(cen_offset_done, 1)

        @block.scalar
        def _(act):
            act.wait_ge(var_ready, 1)
            nc.scalar.activation(sd[:, 1:2], sd[:, 0:1], ACT.Sqrt).then_inc(sd_ready, 1)


def input_statistics(nc, x_t, stats):
    PIECE = 4 * CH
    with ExitStack() as ctx:
        buf = ctx.enter_context(nc.sbuf_tensor("a_buf", [P, 2, PIECE], F32))
        sem = ctx.enter_context(phase_semaphores(nc))
        loaded = [sem(f"a_loaded{b}") for b in range(2)]
        counted = sem("a_counted")
        block = ctx.enter_context(nc.Block())

        @block.sync
        def _(sp):
            def body(i):
                for b in range(2):
                    wait_count(sp, counted, i * 8 + 4 * b - 4)
                    sp.dma_start(buf[:, b, :], x_t[:, bass.ds(i * (2 * PIECE) + b * PIECE, PIECE)]).then_inc(loaded[b], 16)
            looped(sp, 0, TOK // PIECE // 2, 1, body)

        @block.vector
        def _(dve):
            def body(i):
                for b in range(2):
                    wait_count(dve, loaded[b], i * 16 + 16)
                    for q in range(4):
                        nc.vector.bn_stats(stats[:, bass.ds(i * 48 + (b * 4 + q) * 6, 6)],
                                           buf[:, b, q * CH:(q + 1) * CH]).then_inc(counted, 1)
            looped(dve, 0, TOK // PIECE // 2, 1, body)


def attention_weights(nc, d, W, ps):
    with ExitStack() as ctx:
        raw = {n: ctx.enter_context(nc.sbuf_tensor(f"b_raw_{n}", [P, w], F32))
               for n, w in (("Wq", P), ("Wk", P), ("Wv", P), ("Wg", P), ("Wb", HEADS), ("Wo", P),
                            ("ln_gamma", 1), ("ln_beta", 1), ("bg", 1))}
        beta_rep = ctx.enter_context(nc.sbuf_tensor("b_beta_rep", [P, P], F32))
        sem = ctx.enter_context(phase_semaphores(nc))
        loaded, beta_ready, offsets_done, chain = (
            sem("b_w_loaded"), sem("b_beta_ready"), sem("b_offsets_done"), sem("b_w_chain"))
        block = ctx.enter_context(nc.Block())
        scale = HD ** -0.5

        @block.sync
        def _(sp):
            for n, t in raw.items():
                sp.dma_start(t[:, :], d["L0_conv_" + n]).then_inc(loaded, 16)
            sp.dma_start(W["bo"][:, :], d["L0_conv_bo"]).then_inc(loaded, 16)
            sp.wait_ge(loaded, 16 * (len(raw) + 1))

        @block.vector
        def _(dve):
            link = linker(dve, chain)
            dve.wait_ge(loaded, 16 * (len(raw) + 1))
            link(nc.vector.memset(beta_rep[:, :], 1.0))
            nc.vector.tensor_scalar(beta_rep[:, :], beta_rep[:, :], raw["ln_beta"][:, 0:1], None,
                                    ALU.mult).then_inc(beta_ready, 1)
            for n in ("Wq", "Wk", "Wv", "Wg", "Wb"):
                link(nc.vector.tensor_scalar(W[n][:, :], raw[n][:, :], raw["ln_gamma"][:, 0:1], None, ALU.mult))
            link(nc.vector.tensor_scalar(W["Wo"][:, :], raw["Wo"][:, :], 0.5, None, ALU.mult))
            dve.wait_ge(offsets_done, 5)
            link(nc.vector.tensor_scalar(W["q_off"][:, :], ps[:, 0, 0:1], -scale, None, ALU.mult))
            link(nc.vector.tensor_copy(W["k_off"][:, :], ps[:, 1, 0:1]))
            link(nc.vector.tensor_scalar(W["g_off"][:, :], ps[:, 2, 0:1], raw["bg"][:, 0:1], 0.5, ALU.add, ALU.mult))
            link(nc.vector.tensor_scalar(W["b_off"][0:HEADS, :], ps[0:HEADS, 3, 0:1], -1.0, None, ALU.mult))
            for kc in range(HALF):
                link(nc.vector.tensor_copy(W["v_off"][:, kc, :], ps[:, 4, 0:P]))

        @block.tensor
        def _(pe):
            pe.wait_ge(loaded, 16 * (len(raw) + 1))
            pe.wait_ge(beta_ready, 1)
            for n, w in enumerate(("Wq", "Wk", "Wg", "Wb")):
                m = raw[w].shape[1]
                nc.tensor.matmul(ps[0:m, n, 0:1], raw[w][:, :], raw["ln_beta"][:, 0:1],
                                 start=True, stop=True).then_inc(offsets_done, 1)
            nc.tensor.matmul(ps[:, 4, 0:P], beta_rep[:, :], raw["Wv"][:, :],
                             start=True, stop=True).then_inc(offsets_done, 1)


def attention_norm(nc, x_t, z_t, bias_d, W, const, affine, ps):
    Q = 4
    cen, cenb = affine[:, 2:2 + P], affine[:, 2 + P:3 + P]
    with ExitStack() as ctx:
        sb = lambda n, s: ctx.enter_context(nc.sbuf_tensor("b_" + n, s, F32))
        new_sem = ctx.enter_context(phase_semaphores(nc))
        sem = lambda n: new_sem("b_" + n)
        xin, sq, lnv, rstd, z = sb("xin", [P, Q, CH]), sb("sq", [P, 2, CH]), sb("lnv", [P, 2, CH]), sb("rstd", [P, 2, CH]), sb("z", [P, Q, CH])
        bsb = sb("bsb", [HEADS, Q, CH])
        eps = sb("eps", [P, 1])
        x_in = [sem(f"x_in{q}") for q in range(Q)]
        z_out = [sem(f"z_out{q}") for q in range(Q)]
        b_out = [sem(f"b_out{q}") for q in range(Q)]
        centred, squared, var_done, ln_done, rstd_done, z_done, bias_done, bias_copied, eps_set = (
            sem("centred"), sem("squared"), sem("var_done"), sem("ln_done"), sem("rstd_done"),
            sem("z_done"), sem("bias_done"), sem("bias_copied"), sem("eps_set"))
        pool_passed = sem("pool_passed")
        block = ctx.enter_context(nc.Block())
        CEN = [ps[:, q, :] for q in range(4)]
        VAR = [ps[:, 4 + q, :] for q in range(2)]
        BIA = [ps[0:HEADS, 6 + q, :] for q in range(2)]

        @block.sync
        def _(sp):
            def body(i):
                for q in range(Q):
                    wait_count(sp, centred, i * Q + q - 3)
                    sp.dma_start(xin[:, q, :], x_t[:, bass.ds(i * (Q * CH) + q * CH, CH)]).then_inc(x_in[q], 16)
            looped(sp, 0, NCH // Q, 1, body)

        @block.gpsimd
        def _(pool):
            nc.gpsimd.memset(eps[:, :], EPS).then_inc(eps_set, 1)
            def body(i):
                for q in range(Q):
                    wait_counts(pool, pool_passed, (z_done, i * Q + q + 1))
                    pool.dma_start(z_t[:, bass.ds(i * (Q * CH) + q * CH, CH)], z[:, q, :]).then_inc(z_out[q], 16)
                    if q:
                        wait_counts(pool, pool_passed, (bias_copied, i * Q + q))
                        pool.dma_start(bias_d[:, bass.ds(i * (Q * CH) + (q - 1) * CH, CH)], bsb[:, q - 1, :]).then_inc(b_out[q - 1], 16)
                wait_counts(pool, pool_passed, (bias_copied, i * Q + Q))
                pool.dma_start(bias_d[:, bass.ds(i * (Q * CH) + (Q - 1) * CH, CH)], bsb[:, Q - 1, :]).then_inc(b_out[Q - 1], 16)
            looped(pool, 0, NCH // Q, 1, body)
            for q in range(Q):
                pool.wait_ge(z_out[q], NCH // Q * 16)
                pool.wait_ge(b_out[q], NCH // Q * 16)

        @block.tensor
        def _(pe):
            def body(i):
                def centre(q):
                    wait_count(pe, x_in[q], i * 16 + 16)
                    wait_count(pe, z_done, i * Q + q - 3)
                    nc.tensor.matmul(CEN[q], cen, xin[:, q, :], start=True, stop=True).then_inc(centred, 1)

                def variance(q):
                    wait_count(pe, squared, i * Q + q + 1)
                    wait_count(pe, ln_done, i * Q + q - 1)
                    nc.tensor.matmul(VAR[q % 2], const["mean"][:, :], sq[:, q % 2, :], start=True, stop=True).then_inc(var_done, 1)

                def bias(q):
                    wait_count(pe, z_done, i * Q + q + 1)
                    wait_count(pe, bias_copied, i * Q + q - 1)
                    nc.tensor.matmul(BIA[q % 2], W["Wb"][:, :], z[:, q, :], start=True, stop=True).then_inc(bias_done, 1)

                centre(0), centre(1), variance(0), centre(2), variance(1), centre(3), variance(2)
                bias(0), variance(3), bias(1), bias(2), bias(3)
            looped(pe, 0, NCH // Q, 1, body)

        @block.scalar
        def _(act):
            act.wait_ge(eps_set, 1)
            load_log_exp(nc, act)
            def body(i):
                def square(q):
                    wait_count(act, centred, i * Q + q + 1)
                    wait_count(act, var_done, i * Q + q - 1)
                    nc.scalar.activation(sq[:, q % 2, :], CEN[q], ACT.Square, bias=cenb).then_inc(squared, 1)

                def inverse_deviation(q):
                    wait_count(act, var_done, i * Q + q + 1)
                    nc.scalar.activation(lnv[:, q % 2, :], VAR[q % 2], ACT.Ln, bias=eps[:, 0:1]).then_inc(ln_done, 1)
                    wait_count(act, ln_done, i * Q + q + 1)
                    wait_count(act, z_done, i * Q + q - 1)
                    nc.scalar.activation(rstd[:, q % 2, :], lnv[:, q % 2, :], ACT.Exp, scale=-0.5).then_inc(rstd_done, 1)

                square(0), square(1), inverse_deviation(0), square(2), inverse_deviation(1), square(3)
                inverse_deviation(2), inverse_deviation(3)
            looped(act, 0, NCH // Q, 1, body)

        @block.vector
        def _(dve):
            def body(i):
                for q in range(Q):
                    wait_count(dve, rstd_done, i * Q + q + 1)
                    wait_count(dve, z_out[q], i * 16)
                    wait_count(dve, bias_done, i * Q + q - 3)
                    nc.vector.scalar_tensor_tensor(z[:, q, :], CEN[q], cenb, rstd[:, q % 2, :],
                                                   ALU.add, ALU.mult).then_inc(z_done, 1)
                    if q:
                        copy_bias(i, q - 1)
                copy_bias(i, Q - 1)

            def copy_bias(i, q):
                wait_count(dve, bias_done, i * Q + q + 1)
                wait_count(dve, b_out[q], i * 16)
                nc.vector.tensor_scalar(bsb[:, q, :], BIA[q % 2], -1.0, W["b_off"][0:HEADS, 0:1],
                                        ALU.mult, ALU.add).then_inc(bias_copied, 1)
            looped(dve, 0, NCH // Q, 1, body)


ATTENTION_STEPS = {
    "pe": [("mKQ", 2), ("PV2", 0), ("PV3", 0), ("mV", 1), ("PV1", 0), ("T0", 1), ("QK3", 1), ("mO", 0), ("QK0", 2),
        ("mG", 2), ("PV0", 1), ("T1", 1), ("QK1", 2), ("T2", 1), ("QK2", 2), ("T3", 1)],
    "act": [("ex10", 1), ("kT", 2), ("qT", 2), ("ex21", 1), ("ex11", 1), ("ex20", 1), ("ex31", 1), ("ex30", 1), ("cp1",
        1), ("ex00", 2), ("tg", 2), ("ex01", 2), ("cp3", 1)],
    "pool": [("km0", 2), ("km2", 2), ("nm11", 1), ("km1", 2), ("nm10", 1), ("nm21", 1), ("nm20", 1), ("nm01", 2),
        ("km3", 2)],
    "dve": [("lo20", 1), ("v", 1), ("gated", 0), ("rec1", 1), ("cp0", 1), ("lo30", 1), ("lo31", 1), ("rec2", 1), ("xo",
        0), ("lo01", 2), ("rec3", 1), ("lo00", 2), ("nm31", 1), ("nm30", 1), ("lo11", 2), ("cp2", 1), ("lo10", 2),
        ("rec0", 2), ("nm00", 2), ("bn", 0), ("lo21", 2)],
    "sp": [("z", 3), ("x", 1), ("st", 0)],
}
ATTENTION = Schedule(N, -3, ATTENTION_STEPS)


def row_attention(nc, x_t, z_t, bias_d, x1_t, W, const, stats, ps):
    scale = HD ** -0.5
    with ExitStack() as ctx:
        sb = lambda n, s: ctx.enter_context(nc.sbuf_tensor("c_" + n, s, F32))
        new_sem = ctx.enter_context(phase_semaphores(nc))
        sem = lambda n: new_sem("c_" + n)
        bias = sb("bias", [P, HALF, HEADS, N])
        z, x = sb("z", [P, 2, N]), sb("x", [P, 2, N])
        qT, kT, km = sb("qT", [P, 2, N]), sb("kT", [P, 2, N]), sb("km", [P, 2, HEADS, N])
        tg, v = sb("tg", [P, 2, N]), sb("v", [P, 2, HALF, P])
        sc = sb("sc", [P, HEADS, HALF, N])
        pr = sb("pr", [P, 2, HEADS, HALF, N])
        pT = sb("pT", [P, 2, HEADS, HALF, N])
        low, tot, rec = [sb(n, [P, 2, HEADS, HALF]) for n in ("low", "tot", "rec")]
        gated, xo = sb("gated", [P, N]), sb("xo", [P, 2, N])
        z_in, x_in, x_out = [[sem(f"{n}{r}") for r in range(2)] for n in ("z_in", "x_in", "x_out")]
        bias_in, masks_zero = sem("bias_in"), sem("masks_zero")
        pe_done, act_done, pool_done, dve_done = sem("pe_done"), sem("act_done"), sem("pool_done"), sem("dve_done")
        pool_passed, dve_passed, sp_passed = sem("pool_passed"), sem("dve_passed"), sem("sp_passed")
        block = ctx.enter_context(nc.Block())
        SC = [ps[:, b, :].rearrange("p (c k) -> p c k", c=HALF) for b in range(2)]
        PT = [ps[:, 2 + b, :].rearrange("p (c k) -> p c k", c=HALF) for b in range(2)]
        PV = [ps[:, 4 + b, 0:N] for b in range(2)]
        PQ, PK, PG = ps[:, 6, 0:N], ps[:, 6, N:2 * N], ps[:, 6, 0:N]
        PWO, PVV = ps[:, 7, 0:N], ps[:, 7, N:2 * N]

        @block.sync
        def _(sp):
            for c in range(HALF):
                sp.dma_start(bias[:, c, :, :], bias_d[:, c * P * N:(c + 1) * P * N].rearrange("h (j k) -> j h k", k=N)).then_inc(bias_in, 16)

            def slot(half, r):
                s = Slot(ATTENTION, sp, None, half, r)
                at = s.at
                wait_counts(sp, sp_passed, (pe_done, at("z", "mV", 2)))
                if s.runs("z"):
                    sp.dma_start(z[:, (r + ATTENTION.ahead["z"]) % 2, :], z_t[:, bass.ds(half * (2 * N) + (r + ATTENTION.ahead["z"]) * N, N)]).then_inc(z_in[(r + ATTENTION.ahead["z"]) % 2], 16)
                wait_counts(sp, sp_passed, (dve_done, at("x", "xo", 2)))
                if s.runs("x"):
                    sp.dma_start(x[:, (r + ATTENTION.ahead["x"]) % 2, :], x_t[:, bass.ds(half * (2 * N) + (r + ATTENTION.ahead["x"]) * N, N)]).then_inc(x_in[(r + ATTENTION.ahead["x"]) % 2], 16)
                wait_counts(sp, sp_passed, (dve_done, at("st", "xo")))
                if s.runs("st"):
                    sp.dma_start(x1_t[:, bass.ds(half * (2 * N) + (r + ATTENTION.ahead["st"]) * N, N)], xo[:, (r + ATTENTION.ahead["st"]) % 2, :]).then_inc(x_out[(r + ATTENTION.ahead["st"]) % 2], 16)
            ATTENTION.run(sp, slot)
            for r in range(2):
                sp.wait_ge(x_out[r], 16 * N // 2)

        @block.tensor
        def _(pe):
            def transposes(bank, h, parity):
                for kc in range(HALF):
                    for jc in range(HALF):
                        mm = nc.tensor.transpose(bank[:, kc, jc * P:(jc + 1) * P], pr[:, parity, h, jc, kc * P:(kc + 1) * P],
                                                 const["ident"][:, :])
                return mm

            def values(h, parity):
                for kc in range(HALF):
                    mm = nc.tensor.matmul(PV[parity][h * HD:(h + 1) * HD, :], v[:, parity, kc, h * HD:(h + 1) * HD],
                                          pT[:, parity, h, kc, :], start=kc == 0, stop=kc == HALF - 1)
                return mm

            def slot(half, r):
                s = Slot(ATTENTION, pe, pe_done, half, r)
                at, on = s.at, s.on
                wait_count(pe, act_done, at("mKQ", "tg", 1))
                wait_count(pe, *s.moved(z_in, "mKQ", 16))
                if on("mKQ"):
                    nc.tensor.matmul(PK, W["Wk"][:, :], z[:, s.parity, :], start=True, stop=True)
                    nc.tensor.matmul(PQ, W["Wq"][:, :], z[:, s.parity, :], start=True, stop=True).then_inc(pe_done, 1)
                wait_count(pe, dve_done, at("PV2", "cp2"))
                if on("PV2"):
                    values(2, s.parity).then_inc(pe_done, 1)
                wait_count(pe, act_done, at("PV3", "cp3"))
                if on("PV3"):
                    values(3, s.parity).then_inc(pe_done, 1)
                wait_count(pe, *s.moved(z_in, "mV", 16))
                if on("mV"):
                    nc.tensor.matmul(PVV[:, 0:128], z[:, s.parity, 0:128], W["Wv"][:, :], start=True, stop=True)
                    nc.tensor.matmul(PVV[:, 128:256], z[:, s.parity, 128:256], W["Wv"][:, :], start=True, stop=True).then_inc(pe_done, 1)
                if on("PV1"):
                    values(1, s.parity).then_inc(pe_done, 1)
                wait_count(pe, dve_done, at("T0", "nm00"))
                wait_count(pe, pool_done, at("T0", "nm01"))
                if on("T0"):
                    transposes(PT[0], 0, s.parity).then_inc(pe_done, 1)
                wait_count(pe, pool_done, at("QK3", "km3"))
                if on("QK3"):
                    nc.tensor.matmul(SC[1][:, 0, :], qT[:, s.parity, 0:128], km[:, s.parity, 3, :], start=True, stop=True)
                    nc.tensor.matmul(SC[1][:, 1, :], qT[:, s.parity, 128:256], km[:, s.parity, 3, :], start=True, stop=True).then_inc(pe_done, 1)
                wait_count(pe, dve_done, at("mO", "gated"))
                if on("mO"):
                    nc.tensor.matmul(PWO, W["Wo"][:, :], gated[:, :], start=True, stop=True).then_inc(pe_done, 1)
                wait_count(pe, act_done, at("QK0", "qT"))
                wait_count(pe, pool_done, at("QK0", "km0"))
                if on("QK0"):
                    nc.tensor.matmul(SC[0][:, 0, :], qT[:, s.parity, 0:128], km[:, s.parity, 0, :], start=True, stop=True)
                    nc.tensor.matmul(SC[0][:, 1, :], qT[:, s.parity, 128:256], km[:, s.parity, 0, :], start=True, stop=True).then_inc(pe_done, 1)
                wait_count(pe, *s.moved(z_in, "mG", 16))
                if on("mG"):
                    nc.tensor.matmul(PG, W["Wg"][:, :], z[:, s.parity, :], start=True, stop=True).then_inc(pe_done, 1)
                wait_count(pe, dve_done, at("PV0", "cp0"))
                if on("PV0"):
                    values(0, s.parity).then_inc(pe_done, 1)
                wait_count(pe, pool_done, at("T1", "nm10"))
                if on("T1"):
                    transposes(PT[1], 1, s.parity).then_inc(pe_done, 1)
                wait_count(pe, dve_done, at("QK1", "lo31", 1))
                if on("QK1"):
                    nc.tensor.matmul(SC[1][:, 0, :], qT[:, s.parity, 0:128], km[:, s.parity, 1, :], start=True, stop=True)
                    nc.tensor.matmul(SC[1][:, 1, :], qT[:, s.parity, 128:256], km[:, s.parity, 1, :], start=True, stop=True).then_inc(pe_done, 1)
                wait_count(pe, pool_done, at("T2", "nm20"))
                if on("T2"):
                    transposes(PT[0], 2, s.parity).then_inc(pe_done, 1)
                wait_count(pe, dve_done, at("QK2", "lo00"))
                if on("QK2"):
                    nc.tensor.matmul(SC[0][:, 0, :], qT[:, s.parity, 0:128], km[:, s.parity, 2, :], start=True, stop=True)
                    nc.tensor.matmul(SC[0][:, 1, :], qT[:, s.parity, 128:256], km[:, s.parity, 2, :], start=True, stop=True).then_inc(pe_done, 1)
                wait_count(pe, dve_done, at("T3", "nm30"))
                wait_count(pe, act_done, at("T3", "cp1"))
                if on("T3"):
                    transposes(PT[1], 3, s.parity).then_inc(pe_done, 1)
            ATTENTION.run(pe, slot)

        @block.scalar
        def _(act):
            def exponential(h, jc, parity):
                return nc.scalar.activation(pr[:, parity, h, jc, :], sc[:, h, jc, :], ACT.Exp, bias=low[:, parity, h, jc:jc + 1],
                                            scale=-1.0, accum_out=tot[:, parity, h, jc:jc + 1])

            def slot(half, r):
                s = Slot(ATTENTION, act, act_done, half, r)
                at, on = s.at, s.on
                wait_count(act, dve_done, at("ex10", "lo10"))
                wait_count(act, pool_done, at("ex10", "nm10", 2))
                wait_count(act, pe_done, at("ex10", "T1", 2))
                if on("ex10"):
                    exponential(1, 0, s.parity).then_inc(act_done, 1)
                wait_count(act, pe_done, at("kT", "mKQ"))
                wait_count(act, pool_done, at("kT", "km3", 2))
                if on("kT"):
                    nc.scalar.activation(kT[:, s.parity, :], PK, ACT.Identity, bias=W["k_off"][:, 0:1]).then_inc(act_done, 1)
                if on("qT"):
                    nc.scalar.activation(qT[:, s.parity, :], PQ, ACT.Identity, bias=W["q_off"][:, 0:1], scale=-scale).then_inc(act_done, 1)
                wait_count(act, dve_done, at("ex21", "lo21"))
                if on("ex21"):
                    exponential(2, 1, s.parity).then_inc(act_done, 1)
                if on("ex11"):
                    exponential(1, 1, s.parity).then_inc(act_done, 1)
                wait_count(act, dve_done, at("ex20", "lo20"))
                if on("ex20"):
                    exponential(2, 0, s.parity).then_inc(act_done, 1)
                wait_count(act, dve_done, at("ex31", "lo31"))
                if on("ex31"):
                    exponential(3, 1, s.parity).then_inc(act_done, 1)
                if on("ex30"):
                    exponential(3, 0, s.parity).then_inc(act_done, 1)
                wait_count(act, pe_done, at("cp1", "T1"))
                if on("cp1"):
                    nc.scalar.activation(pT[:, s.parity, 1, :, :], PT[1], ACT.Identity).then_inc(act_done, 1)
                wait_count(act, dve_done, at("ex00", "lo00"))
                if on("ex00"):
                    exponential(0, 0, s.parity).then_inc(act_done, 1)
                if on("tg"):
                    nc.scalar.activation(tg[:, s.parity, :], PG, ACT.Tanh, bias=W["g_off"][:, 0:1], scale=0.5).then_inc(act_done, 1)
                if on("ex01"):
                    exponential(0, 1, s.parity).then_inc(act_done, 1)
                wait_count(act, pe_done, at("cp3", "T3"))
                if on("cp3"):
                    nc.scalar.activation(pT[:, s.parity, 3, :, :], PT[1], ACT.Identity).then_inc(act_done, 1)
            ATTENTION.run(act, slot)

        @block.gpsimd
        def _(pool):
            nc.gpsimd.memset(km[:, :, :, :], 0.0).then_inc(masks_zero, 1)
            pool.wait_ge(masks_zero, 1)

            def slot(half, r):
                s = Slot(ATTENTION, pool, pool_done, half, r)
                at, on = s.at, s.on
                wait_counts(pool, pool_passed, (pool_done, at("km0", "km0") - 1), (act_done, at("km0", "kT")), (pe_done, at("km0", "QK0", 2)))
                if on("km0"):
                    nc.gpsimd.tensor_scalar(km[0:32, s.parity, 0, :], kT[0:32, s.parity, :], 1.0, 0.0, ALU.mult, ALU.add).then_inc(pool_done, 1)
                wait_counts(pool, pool_passed, (pool_done, at("km2", "km2") - 1), (pe_done, at("km2", "QK2", 2)))
                if on("km2"):
                    nc.gpsimd.tensor_scalar(km[64:96, s.parity, 2, :], kT[64:96, s.parity, :], 1.0, 0.0, ALU.mult, ALU.add).then_inc(pool_done, 1)
                wait_counts(pool, pool_passed, (pool_done, at("nm11", "nm11") - 1), (act_done, at("nm11", "ex11")), (dve_done, at("nm11", "rec1")))
                if on("nm11"):
                    nc.gpsimd.tensor_scalar(pr[:, s.parity, 1, 1, :], pr[:, s.parity, 1, 1, :], rec[:, s.parity, 1, 1:2], 0.0, ALU.mult, ALU.add).then_inc(pool_done, 1)
                wait_counts(pool, pool_passed, (pool_done, at("km1", "km1") - 1))
                if on("km1"):
                    nc.gpsimd.tensor_scalar(km[32:64, s.parity, 1, :], kT[32:64, s.parity, :], 1.0, 0.0, ALU.mult, ALU.add).then_inc(pool_done, 1)
                wait_counts(pool, pool_passed, (pool_done, at("nm10", "nm10") - 1))
                if on("nm10"):
                    nc.gpsimd.tensor_scalar(pr[:, s.parity, 1, 0, :], pr[:, s.parity, 1, 0, :], rec[:, s.parity, 1, 0:1], 0.0, ALU.mult, ALU.add).then_inc(pool_done, 1)
                wait_counts(pool, pool_passed, (pool_done, at("nm21", "nm21") - 1), (dve_done, at("nm21", "rec2")))
                if on("nm21"):
                    nc.gpsimd.tensor_scalar(pr[:, s.parity, 2, 1, :], pr[:, s.parity, 2, 1, :], rec[:, s.parity, 2, 1:2], 0.0, ALU.mult, ALU.add).then_inc(pool_done, 1)
                wait_counts(pool, pool_passed, (pool_done, at("nm20", "nm20") - 1), (act_done, at("nm20", "ex20")))
                if on("nm20"):
                    nc.gpsimd.tensor_scalar(pr[:, s.parity, 2, 0, :], pr[:, s.parity, 2, 0, :], rec[:, s.parity, 2, 0:1], 0.0, ALU.mult, ALU.add).then_inc(pool_done, 1)
                wait_counts(pool, pool_passed, (pool_done, at("nm01", "nm01") - 1), (act_done, at("nm01", "ex01")), (dve_done, at("nm01", "rec0")))
                if on("nm01"):
                    nc.gpsimd.tensor_scalar(pr[:, s.parity, 0, 1, :], pr[:, s.parity, 0, 1, :], rec[:, s.parity, 0, 1:2], 0.0, ALU.mult, ALU.add).then_inc(pool_done, 1)
                wait_counts(pool, pool_passed, (pool_done, at("km3", "km3") - 1), (pe_done, at("km3", "QK3", 2)))
                if on("km3"):
                    nc.gpsimd.tensor_scalar(km[96:128, s.parity, 3, :], kT[96:128, s.parity, :], 1.0, 0.0, ALU.mult, ALU.add).then_inc(pool_done, 1)
            ATTENTION.run(pool, slot)

        @block.vector
        def _(dve):
            dve.wait_ge(bias_in, 16 * HALF)

            def lowest(scores, h, jc, parity):
                return nc.vector.tensor_tensor_reduce(out=sc[:, h, jc, :], in0=scores[:, jc, :], in1=bias[:, jc, h, :], scale=1.0,
                                                      scalar=3.0e38, op0=ALU.add, op1=ALU.min,
                                                      accum_out=low[:, parity, h, jc:jc + 1])

            def slot(half, r):
                s = Slot(ATTENTION, dve, dve_done, half, r)
                at, on = s.at, s.on
                wait_counts(dve, dve_passed, (pe_done, at("lo20", "QK2")), (act_done, at("lo20", "ex20", 1)))
                if on("lo20"):
                    lowest(SC[0], 2, 0, s.parity).then_inc(dve_done, 1)
                wait_count(dve, pe_done, at("v", "mV"))
                if on("v"):
                    nc.vector.tensor_tensor(v[:, s.parity, :, :].rearrange("p c d -> p (c d)"), PVV,
                                             W["v_off"][:, :, :].rearrange("p c d -> p (c d)"), ALU.add).then_inc(dve_done, 1)
                wait_count(dve, pe_done, at("gated", "PV1"))
                if on("gated"):
                    nc.vector.scalar_tensor_tensor(gated[:, :], tg[:, s.parity, :], 1.0, PV[s.parity], ALU.add, ALU.mult).then_inc(dve_done, 1)
                wait_count(dve, act_done, at("rec1", "ex11"))
                wait_count(dve, pool_done, at("rec1", "nm10", 2))
                if on("rec1"):
                    nc.vector.reciprocal(rec[:, s.parity, 1, :], tot[:, s.parity, 1, :]).then_inc(dve_done, 1)
                wait_count(dve, pe_done, at("cp0", "T0"))
                if on("cp0"):
                    nc.vector.tensor_copy(pT[:, s.parity, 0, :, :], PT[0]).then_inc(dve_done, 1)
                wait_counts(dve, dve_passed, (pe_done, at("lo30", "QK3")))
                if on("lo30"):
                    lowest(SC[1], 3, 0, s.parity).then_inc(dve_done, 1)
                if on("lo31"):
                    lowest(SC[1], 3, 1, s.parity).then_inc(dve_done, 1)
                wait_count(dve, act_done, at("rec2", "ex20"))
                wait_count(dve, pool_done, at("rec2", "nm20", 2))
                if on("rec2"):
                    nc.vector.reciprocal(rec[:, s.parity, 2, :], tot[:, s.parity, 2, :]).then_inc(dve_done, 1)
                wait_count(dve, pe_done, at("xo", "mO"))
                wait_count(dve, *s.moved(x_in, "xo", 16))
                wait_count(dve, *s.moved(x_out, "xo", 16, 2))
                if on("xo"):
                    nc.vector.scalar_tensor_tensor(xo[:, s.parity, :], PWO, W["bo"][:, 0:1], x[:, s.parity, :], ALU.add, ALU.add).then_inc(dve_done, 1)
                wait_counts(dve, dve_passed, (pe_done, at("lo01", "QK0")))
                if on("lo01"):
                    lowest(SC[0], 0, 1, s.parity).then_inc(dve_done, 1)
                wait_count(dve, act_done, at("rec3", "ex30"))
                if on("rec3"):
                    nc.vector.reciprocal(rec[:, s.parity, 3, :], tot[:, s.parity, 3, :]).then_inc(dve_done, 1)
                if on("lo00"):
                    lowest(SC[0], 0, 0, s.parity).then_inc(dve_done, 1)
                wait_count(dve, dve_done, at("nm31", "rec3"))
                if on("nm31"):
                    nc.vector.tensor_scalar(pr[:, s.parity, 3, 1, :], pr[:, s.parity, 3, 1, :], rec[:, s.parity, 3, 1:2], None, ALU.mult).then_inc(dve_done, 1)
                if on("nm30"):
                    nc.vector.tensor_scalar(pr[:, s.parity, 3, 0, :], pr[:, s.parity, 3, 0, :], rec[:, s.parity, 3, 0:1], None, ALU.mult).then_inc(dve_done, 1)
                wait_counts(dve, dve_passed, (pe_done, at("lo11", "QK1")))
                if on("lo11"):
                    lowest(SC[1], 1, 1, s.parity).then_inc(dve_done, 1)
                wait_count(dve, pe_done, at("cp2", "T2"))
                if on("cp2"):
                    nc.vector.tensor_copy(pT[:, s.parity, 2, :, :], PT[0]).then_inc(dve_done, 1)
                if on("lo10"):
                    lowest(SC[1], 1, 0, s.parity).then_inc(dve_done, 1)
                wait_count(dve, act_done, at("rec0", "ex01"))
                wait_count(dve, pool_done, at("rec0", "nm01", 2))
                if on("rec0"):
                    nc.vector.reciprocal(rec[:, s.parity, 0, :], tot[:, s.parity, 0, :]).then_inc(dve_done, 1)
                wait_count(dve, dve_done, at("nm00", "rec0"))
                if on("nm00"):
                    nc.vector.tensor_scalar(pr[:, s.parity, 0, 0, :], pr[:, s.parity, 0, 0, :], rec[:, s.parity, 0, 0:1], None, ALU.mult).then_inc(dve_done, 1)
                if on("bn"):
                    nc.vector.bn_stats(stats[:, bass.ds(half * 12 + (r + ATTENTION.ahead["bn"]) * 6, 6)], xo[:, s.parity, :]).then_inc(dve_done, 1)
                wait_counts(dve, dve_passed, (pe_done, at("lo21", "QK2")))
                if on("lo21"):
                    lowest(SC[0], 2, 1, s.parity).then_inc(dve_done, 1)
            ATTENTION.run(dve, slot)


TAPS = 9
PAD = TAPS // 2


def row_scan(nc, d, x1_t, x2_t, affine, stats, ps):
    with ExitStack() as ctx:
        sb = lambda n, s: ctx.enter_context(nc.sbuf_tensor("d_" + n, s, F32))
        new_sem = ctx.enter_context(phase_semaphores(nc))
        sem = lambda n: new_sem("d_" + n)
        taps = sb("taps", [P, TAPS, P])
        x1, g, x2 = sb("x1", [P, 2, N]), sb("g", [P, 2, N]), sb("x2", [P, 2, N])
        new = sb("new", [P, 2, N + 2 * PAD])
        taps_in, pads_zero = sem("taps_in"), sem("pads_zero")
        x_in, x_out = [sem(f"x_in{r}") for r in range(2)], [sem(f"x_out{r}") for r in range(2)]
        g_done, left_conv, right_conv, left_new, right_new, x2_done, x2_counted = (
            sem("g_done"), sem("left_conv"), sem("right_conv"), sem("left_new"), sem("right_new"),
            sem("x2_done"), sem("x2_counted"))
        pool_passed = sem("pool_passed")
        block = ctx.enter_context(nc.Block())
        LEFT = [ps[:, r, 0:P] for r in range(2)]
        RIGHT = [ps[:, 2 + r, 0:P] for r in range(2)]

        def nth(half, r, c=0):
            return half * 2 + (r + c)

        def rows(eng, row):
            for R in range(4):
                row(R // 2, R % 2, R)
            with eng.Fori(2, N // 2 - 1) as half:
                for r in range(2):
                    row(half, r, None)
            for R in range(N - 2, N):
                row(R // 2, R % 2, R)

        @block.sync
        def _(sp):
            sp.dma_start(taps[:, :, :], d["L1_conv_W"]).then_inc(taps_in, 16)
            for r in range(2):
                sp.dma_start(x1[:, r, :], x1_t[:, r * N:(r + 1) * N]).then_inc(x_in[r], 16)

            def row(half, r, R):
                wait_count(sp, x2_done, nth(half, r, 1))
                sp.dma_start(x2_t[:, bass.ds(half * (2 * N) + r * N, N)], x2[:, r, :]).then_inc(x_out[r], 16)
                if R is None or R + 2 < N:
                    sp.dma_start(x1[:, r, :], x1_t[:, bass.ds(half * (2 * N) + (r + 2) * N, N)]).then_inc(x_in[r], 16)
            rows(sp, row)
            for r in range(2):
                sp.wait_ge(x_out[r], 16 * N // 2)

        @block.scalar
        def _(act):
            act.wait_ge(pads_zero, 1)

            def row(half, r, R):
                wait_count(act, x_in[r], half * 16 + 16)
                wait_count(act, right_new, nth(half, r, -2))
                if R == 0:
                    nc.scalar.activation(g[:, 0, :], x1[:, 0, :], ACT.Identity, bias=affine[:, 1:2], scale=affine[:, 0:1]).then_inc(g_done, 1)
                    act.wait_ge(g_done, 1)
                    nc.scalar.activation(new[:, 0, PAD:PAD + N], g[:, 0, :], ACT.Identity).then_inc(g_done, 1)
                    return
                nc.scalar.activation(g[:, r, :], x1[:, r, :], ACT.Identity, bias=affine[:, 1:2], scale=affine[:, 0:1]).then_inc(g_done, 1)
            rows(act, row)

        @block.tensor
        def _(pe):
            pe.wait_ge(taps_in, 16)

            def row(half, r, R):
                if R == 0:
                    return
                last = new[:, 1 - r, :]

                def tap(to, k, at, **flags):
                    return nc.tensor.matmul(to, taps[:, k, :], last[:, at + k:at + k + P], **flags)

                if R == 1:
                    pe.wait_ge(g_done, 2)
                wait_count(pe, left_new, nth(half, r, -1))
                for k in range(PAD + 1):
                    tap(LEFT[r], k, 0, start=k == 0, stop=False)
                wait_count(pe, right_new, nth(half, r, -1))
                for k in range(PAD + 1, TAPS):
                    mm = tap(LEFT[r], k, 0, start=False, stop=k == TAPS - 1)
                mm.then_inc(left_conv, 1)
                for k in range(TAPS):
                    mm = tap(RIGHT[r], k, P, start=k == 0, stop=k == TAPS - 1)
                mm.then_inc(right_conv, 1)
            rows(pe, row)

        @block.vector
        def _(dve):
            nc.vector.memset(new[:, :, :], 0.0).then_inc(pads_zero, 1)

            def row(half, r, R):
                if R == 0:
                    return
                wait_count(dve, g_done, nth(half, r, 2))
                wait_count(dve, x2_done, nth(half, r, -1))
                wait_count(dve, left_conv, nth(half, r))
                nc.vector.scalar_tensor_tensor(new[:, r, PAD:PAD + P], LEFT[r], 0.0, g[:, r, 0:P],
                                               ALU.max, ALU.add).then_inc(left_new, 1)
                wait_count(dve, x2_done, nth(half, r))
                nc.vector.bn_stats(stats[:, bass.ds(half * 12 + (r - 1) * 6, 6)], x2[:, 1 - r, :]).then_inc(x2_counted, 1)
                wait_count(dve, right_conv, nth(half, r))
                nc.vector.scalar_tensor_tensor(new[:, r, PAD + P:PAD + N], RIGHT[r], 0.0, g[:, r, P:N],
                                               ALU.max, ALU.add).then_inc(right_new, 1)
            rows(dve, row)
            dve.wait_ge(x2_done, N)
            nc.vector.bn_stats(stats[:, (N - 1) * 6:N * 6], x2[:, 1, :]).then_inc(x2_counted, 1)

        @block.gpsimd
        def _(pool):
            def row(half, r, R):
                if R == 0:
                    pool.wait_ge(g_done, 2)
                wait_count(pool, right_new, nth(half, r))
                wait_count(pool, x_in[r], half * 16 + 16)
                wait_count(pool, x_out[r], half * 16)
                wait_counts(pool, pool_passed, (x2_counted, nth(half, r, -1)))
                nc.gpsimd.tensor_tensor(x2[:, r, :], x1[:, r, :], new[:, r, PAD:PAD + N], ALU.add).then_inc(x2_done, 1)
            rows(pool, row)


HC, HW = 8, 16
W4 = ("Wa", "Wb", "Ga", "Gb")
B4 = ("ba", "bb", "bga", "bgb")


def triangle_weights(nc, d, W, ps):
    with ExitStack() as ctx:
        sb = lambda n, s, t=F32: ctx.enter_context(nc.sbuf_tensor("e_raw_" + n, s, t))
        raw4, rawg, rawo = sb("raw4", [P, 4, P]), sb("rawg", [P, P]), sb("rawo", [P, P])
        cols = {n: sb(n, [P, 1]) for n in ("ln_g", "ln_b", "lnh_g", "lnh_b", "bg", "bo")}
        row4, beta_rep = sb("row4", [P, 4, P]), sb("beta_rep", [P, P])
        part = [sb(f"part{n}", [P, CH], BF16) for n in range(3)]
        rest = [sb(f"rest{n}", [P, CH]) for n in range(3)]
        new_sem = ctx.enter_context(phase_semaphores(nc))
        sem = lambda n: new_sem("e_w_" + n)
        loaded, beta_ready, offsets_done, chain = sem("loaded"), sem("beta_ready"), sem("offsets_done"), sem("chain")
        block = ctx.enter_context(nc.Block())
        LOADS = 4 + 4 + 2 + len(cols)

        @block.sync
        def _(sp):
            for n in range(4):
                sp.dma_start(raw4[:, n, :], d["L2_conv_" + W4[n]]).then_inc(loaded, 16)
                sp.dma_start(row4[:, n, :], d["L2_conv_" + B4[n]].rearrange("a b -> b a").broadcast_to([P, P])).then_inc(loaded, 16)
            sp.dma_start(rawg[:, :], d["L2_conv_Wg"]).then_inc(loaded, 16)
            sp.dma_start(rawo[:, :], d["L2_conv_Wo"]).then_inc(loaded, 16)
            for n, t in cols.items():
                sp.dma_start(t[:, :], d["L2_conv_" + n]).then_inc(loaded, 16)
            sp.wait_ge(loaded, 16 * LOADS)

        @block.vector
        def _(dve):
            link = linker(dve, chain)
            dve.wait_ge(loaded, 16 * LOADS)
            link(nc.vector.memset(beta_rep[:, :], 1.0))
            nc.vector.tensor_scalar(beta_rep[:, :], beta_rep[:, :], cols["ln_b"][:, 0:1], None, ALU.mult).then_inc(beta_ready, 1)
            link(nc.vector.tensor_scalar(W["W4"][:, :], raw4[:, :, :].rearrange("p a b -> p (a b)"), cols["ln_g"][:, 0:1], None, ALU.mult))
            link(nc.vector.tensor_scalar(W["Wg"][:, :], rawg[:, :], cols["ln_g"][:, 0:1], None, ALU.mult))
            link(nc.vector.tensor_scalar(W["Wo"][:, :], rawo[:, :], cols["lnh_g"][:, 0:1], None, ALU.mult))
            link(nc.vector.memset(W["ones"][:, :], 1.0))
            link(nc.vector.memset(W["bias_parts"][:, :], 0.0))
            dve.wait_ge(offsets_done, 3)
            link(nc.vector.tensor_tensor(W["g_off"][:, :], ps[:, 1, 0:1], cols["bg"][:, :], ALU.add))
            link(nc.vector.tensor_tensor(W["o_off"][:, :], ps[:, 2, 0:1], cols["bo"][:, :], ALU.add))
            link(nc.vector.tensor_tensor(rest[0][:, :], ps[:, 0, :], row4[:, :, :].rearrange("p a b -> p (a b)"), ALU.add))
            for n in range(3):
                link(nc.vector.tensor_copy(part[n][:, :], rest[n][:, :]))
                if n < 2:
                    link(nc.vector.tensor_tensor(rest[n + 1][:, :], rest[n][:, :], part[n][:, :], ALU.subtract))
                link(nc.vector.tensor_copy(W["bias_parts"][32 * n:32 * n + 1, :], part[n][32 * n:32 * n + 1, :]))

        @block.tensor
        def _(pe):
            pe.wait_ge(loaded, 16 * LOADS)
            pe.wait_ge(beta_ready, 1)
            nc.tensor.matmul(ps[:, 0, :], beta_rep[:, :], raw4[:, :, :].rearrange("p a b -> p (a b)"), start=True, stop=True).then_inc(offsets_done, 1)
            nc.tensor.matmul(ps[:, 1, 0:1], rawg[:, :], cols["ln_b"][:, :], start=True, stop=True).then_inc(offsets_done, 1)
            nc.tensor.matmul(ps[:, 2, 0:1], rawo[:, :], cols["lnh_b"][:, :], start=True, stop=True).then_inc(offsets_done, 1)


def triangle_projections(nc, x2_t, ab_d, go_t, W, const, affine, ps):
    Q, GROUPS, TILES = 4, NCH // 4, 4
    cen, cenb = affine[:, 2:2 + P], affine[:, 2 + P:3 + P]
    with ExitStack() as ctx:
        sb = lambda n, s: ctx.enter_context(nc.sbuf_tensor("e_" + n, s, F32))
        new_sem = ctx.enter_context(phase_semaphores(nc))
        sem = lambda n: new_sem("e_" + n)
        xin, z, go = sb("xin", [P, Q, CH]), sb("z", [P, Q, CH]), sb("go", [P, Q, CH])
        sq, lnv, rstd, sg = sb("sq", [P, 2, CH]), sb("lnv", [P, 2, CH]), sb("rstd", [P, 2, CH]), sb("sg", [P, 2, N])
        stage = sb("stage", [P, 2, HALF, 2 * HC, 8, HW])
        eps = sb("eps", [P, 1])
        x_in, go_out = [sem(f"x_in{q}") for q in range(Q)], [sem(f"go_out{q}") for q in range(Q)]
        ab_out = [sem(f"ab_out{p}") for p in range(2)]
        centred, squared, var_done, ln_done, rstd_done, z_done = (
            sem("centred"), sem("squared"), sem("var_done"), sem("ln_done"), sem("rstd_done"), sem("z_done"))
        go_mm, go_done, ab_mm, gate_done, ab_done, eps_set, pool_passed = (
            sem("go_mm"), sem("go_done"), sem("ab_mm"), sem("gate_done"), sem("ab_done"), sem("eps_set"), sem("pool_passed"))
        block = ctx.enter_context(nc.Block())
        CEN = [ps[:, q, :] for q in range(Q)]
        VAR, GO = ps[:, 4, :], ps[:, 5, :]
        AB = [ps[:, 6 + b, :] for b in range(2)]

        def chunk(i, p, q, per=1, c=0):
            return i * (2 * Q * per) + ((p * Q + q) * per + c)

        def groups(eng, group):
            looped(eng, 0, GROUPS // 2, 1, lambda i: [group(i, p) for p in range(2)])

        @block.sync
        def _(sp):
            def store(i, p):
                wait_count(sp, ab_done, chunk(i, p, Q - 1, TILES, TILES))
                for kc in range(HALF):
                    for ab in range(2):
                        sp.dma_start(ab_d[ab, :, kc, :, bass.ds(i * (16 * HW) + p * (8 * HW), 8 * HW)].rearrange("c k x -> k c x"),
                                     stage[:, p, kc, ab * HC:(ab + 1) * HC, :, :].rearrange("k c i h -> k c (i h)")).then_inc(ab_out[p], 16)

            def group(i, p):
                for q in range(Q):
                    wait_count(sp, centred, chunk(i, p, q, 1, -3))
                    sp.dma_start(xin[:, q, :], x2_t[:, bass.ds(chunk(i, p, q, CH), CH)]).then_inc(x_in[q], 16)
                if p == 1:
                    store(i, 0)
                elif not (isinstance(i, int) and i == 0):
                    store(i - 1, 1)
            groups(sp, group)
            store(GROUPS // 2 - 1, 1)
            for p in range(2):
                sp.wait_ge(ab_out[p], GROUPS // 2 * 64)

        @block.gpsimd
        def _(pool):
            nc.gpsimd.memset(eps[:, :], EPS).then_inc(eps_set, 1)
            def group(i, p):
                for q in range(Q):
                    wait_counts(pool, pool_passed, (go_done, chunk(i, p, q, 1, 1)))
                    pool.dma_start(go_t[:, bass.ds(chunk(i, p, q, CH), CH)], go[:, q, :]).then_inc(go_out[q], 16)
            groups(pool, group)
            for q in range(Q):
                pool.wait_ge(go_out[q], GROUPS * 16)

        @block.tensor
        def _(pe):
            def group(i, p):
                def centre(q):
                    wait_count(pe, x_in[q], i * 32 + (16 * p + 16))
                    wait_count(pe, z_done, chunk(i, p, q, 1, -3))
                    nc.tensor.matmul(CEN[q], cen, xin[:, q, :], start=True, stop=True).then_inc(centred, 1)

                def variance(q):
                    wait_count(pe, squared, chunk(i, p, q, 1, 1))
                    wait_count(pe, ln_done, chunk(i, p, q))
                    nc.tensor.matmul(VAR, const["mean"][:, :], sq[:, q % 2, :], start=True, stop=True).then_inc(var_done, 1)

                centre(0), centre(1), variance(0), centre(2), variance(1), centre(3), variance(2), variance(3)
                for q in range(Q):
                    wait_count(pe, z_done, chunk(i, p, q, 1, 1))
                    wait_count(pe, go_done, chunk(i, p, q))
                    nc.tensor.matmul(GO, W["Wg"][:, :], z[:, q, :], start=True, stop=True).then_inc(go_mm, 1)
                    for t in range(TILES):
                        wait_count(pe, ab_done, chunk(i, p, q, TILES, t - 1))
                        nc.tensor.matmul(AB[t % 2], W["ones"][:, :], W["bias_parts"][:, :], start=True, stop=False)
                        nc.tensor.matmul(AB[t % 2], z[:, q, t * P:(t + 1) * P], W["W4"][:, :], start=False, stop=True).then_inc(ab_mm, 1)
            groups(pe, group)

        @block.scalar
        def _(act):
            act.wait_ge(eps_set, 1)

            def group(i, p):
                def square(q):
                    wait_count(act, centred, chunk(i, p, q, 1, 1))
                    wait_count(act, var_done, chunk(i, p, q, 1, -1))
                    nc.scalar.activation(sq[:, q % 2, :], CEN[q], ACT.Square, bias=cenb).then_inc(squared, 1)

                def inverse_deviation(q):
                    wait_count(act, var_done, chunk(i, p, q, 1, 1))
                    nc.scalar.activation(lnv[:, q % 2, :], VAR, ACT.Ln, bias=eps[:, 0:1]).then_inc(ln_done, 1)
                    wait_count(act, ln_done, chunk(i, p, q, 1, 1))
                    wait_count(act, z_done, chunk(i, p, q, 1, -1))
                    nc.scalar.activation(rstd[:, q % 2, :], lnv[:, q % 2, :], ACT.Exp, scale=-0.5).then_inc(rstd_done, 1)

                load_log_exp(nc, act)
                square(0), square(1), inverse_deviation(0), square(2), inverse_deviation(1), square(3)
                inverse_deviation(2), inverse_deviation(3)
                for q in range(Q):
                    wait_count(act, go_mm, chunk(i, p, q, 1, 1))
                    wait_count(act, go_out[q], i * 32 + 16 * p)
                    nc.scalar.activation(go[:, q, :], GO, ACT.Sigmoid, bias=W["g_off"][:, 0:1]).then_inc(go_done, 1)
                    for t in range(TILES):
                        wait_count(act, ab_mm, chunk(i, p, q, TILES, t + 1))
                        wait_count(act, ab_done, chunk(i, p, q, TILES, t - 1))
                        nc.scalar.activation(sg[:, t % 2, :], AB[t % 2][:, N:2 * N], ACT.Sigmoid).then_inc(gate_done, 1)
            groups(act, group)

        @block.vector
        def _(dve):
            def group(i, p):
                for q in range(Q):
                    wait_count(dve, rstd_done, chunk(i, p, q, 1, 1))
                    wait_count(dve, ab_mm, chunk(i, p, q, TILES, -3 * TILES))
                    nc.vector.scalar_tensor_tensor(z[:, q, :], CEN[q], cenb, rstd[:, q % 2, :], ALU.add, ALU.mult).then_inc(z_done, 1)
                wait_count(dve, ab_out[p], i * 64)
                for q in range(Q):
                    for t in range(TILES):
                        wait_count(dve, gate_done, chunk(i, p, q, TILES, t + 1))
                        nc.vector.tensor_tensor(stage[:, p, t % HALF, :, q * 2 + t // HALF, :],
                                                AB[t % 2][:, 0:N].rearrange("k (c h) -> k c h", h=HW),
                                                sg[:, t % 2, :].rearrange("k (c h) -> k c h", h=HW), ALU.mult).then_inc(ab_done, 1)
            groups(dve, group)


def triangle_products(nc, ab_d, t_t, ps):
    SLOTS = 4
    with ExitStack() as ctx:
        sb = lambda n, s: ctx.enter_context(nc.sbuf_tensor("f_" + n, s, F32))
        new_sem = ctx.enter_context(phase_semaphores(nc))
        sem = lambda n: new_sem("f_" + n)
        ab = sb("ab", [P, 2, 2, HALF, N, HW])
        t = sb("t", [P, SLOTS, 2, HALF * N])
        ab_in = [sem(f"ab_in{b}") for b in range(2)]
        t_out = [sem(f"t_out{s}") for s in range(SLOTS)]
        product, even_copied, odd_copied = sem("product"), sem("even_copied"), sem("odd_copied")
        block = ctx.enter_context(nc.Block())
        T = [ps[:, b, :] for b in range(SLOTS)]

        def chunks(eng, chunk):
            looped(eng, 0, HC // 2, 1, lambda i: [chunk(i, b) for b in range(2)], tail=1)

        def h_count(i, b, c, per=HW):
            return i * (2 * per) + (b * per + c)

        def load(sp, i, b):
            for which in range(2):
                sp.dma_start(ab[:, b, which, :, :, :].rearrange("k c i h -> k c (i h)"),
                             (ab_d[which, bass.ds(i * 2 + b, 1), :, :, :]).rearrange("o c k x -> k (o c) x")).then_inc(ab_in[b], 16)

        @block.sync
        def _(sp):
            load(sp, 0, 0)

            def chunk(i, b):
                if b == 0:
                    wait_count(sp, product, h_count(i, 0, 0))
                    load(sp, i, 1)
                elif not (isinstance(i, int) and i == HC // 2 - 1):
                    wait_count(sp, product, h_count(i, 1, 0))
                    load(sp, i + 1, 0)
                for m in range(HW // 2):
                    wait_count(sp, even_copied, h_count(i, b, m + 1, HW // 2))
                    wait_count(sp, odd_copied, h_count(i, b, m + 1, HW // 2))
                    sp.dma_start(t_t[bass.ds(i * (2 * HW) + (b * HW + 2 * m), 2), :].rearrange("h (c p j) -> p h c j", c=HALF, p=P),
                                 t[:, m % SLOTS, :, :].rearrange("p h (c j) -> p h c j", c=HALF)).then_inc(t_out[m % SLOTS], 16)
            chunks(sp, chunk)
            for s in range(SLOTS):
                sp.wait_ge(t_out[s], P // 2 // SLOTS * 16)

        @block.tensor
        def _(pe):
            def chunk(i, b):
                wait_count(pe, ab_in[b], i * 32 + 32)
                for h in range(HW):
                    wait_count(pe, odd_copied if h % 2 else even_copied, h_count(i, b, h // 2 - 1, HW // 2))
                    for ic in range(HALF):
                        for kc in range(HALF):
                            mm = nc.tensor.matmul(T[h % SLOTS][:, ic * N:(ic + 1) * N], ab[:, b, 0, kc, ic * P:(ic + 1) * P, h],
                                                  ab[:, b, 1, kc, :, h], start=kc == 0, stop=kc == HALF - 1)
                    mm.then_inc(product, 1)
            chunks(pe, chunk)

        def copier(eng, copy, parity, copied):
            def chunk(i, b):
                for m in range(HW // 2):
                    h = 2 * m + parity
                    wait_count(eng, product, h_count(i, b, h + 1))
                    wait_count(eng, t_out[m % SLOTS], h_count(i, b, m // SLOTS, HW // 2 // SLOTS) * 16)
                    copy(t[:, m % SLOTS, parity, :], T[h % SLOTS]).then_inc(copied, 1)
            chunks(eng, chunk)

        @block.vector
        def _(dve):
            copier(dve, nc.vector.tensor_copy, 0, even_copied)

        @block.scalar
        def _(act):
            copier(act, lambda o, i: nc.scalar.activation(o, i, ACT.Identity), 1, odd_copied)


def triangle_output(nc, t_t, go_t, x2_t, x3_t, W, const, stats, ps):
    Q = 4
    with ExitStack() as ctx:
        sb = lambda n, s: ctx.enter_context(nc.sbuf_tensor("g_" + n, s, F32))
        new_sem = ctx.enter_context(phase_semaphores(nc))
        sem = lambda n: new_sem("g_" + n)
        tin, gin, xin = sb("tin", [P, Q, CH]), sb("gin", [P, Q, CH]), sb("xin", [P, Q, CH])
        tn, y, x3 = sb("tn", [P, Q, CH]), sb("y", [P, Q, CH]), sb("x3", [P, Q, CH])
        sq, lnv, rstd = sb("sq", [P, 2, CH]), sb("lnv", [P, 2, CH]), sb("rstd", [P, 2, CH])
        eps = sb("eps", [P, 1])
        t_in, gx_in, x_out = [[sem(f"{n}{q}") for q in range(Q)] for n in ("t_in", "gx_in", "x_out")]
        centred, squared, var_done, ln_done, rstd_done, tn_done = (
            sem("centred"), sem("squared"), sem("var_done"), sem("ln_done"), sem("rstd_done"), sem("tn_done"))
        out_mm, y_done, x3_done, x3_counted, eps_set, pool_passed = (
            sem("out_mm"), sem("y_done"), sem("x3_done"), sem("x3_counted"), sem("eps_set"), sem("pool_passed"))
        block = ctx.enter_context(nc.Block())
        CEN = [ps[:, q, :] for q in range(Q)]
        VAR = [ps[:, 4 + b, :] for b in range(2)]
        OUT = [ps[:, 6 + b, :] for b in range(2)]

        def nth(i, q, c=0):
            return i * Q + (q + c)

        @block.sync
        def _(sp):
            def store(i, q):
                wait_count(sp, x3_done, nth(i, q, 1))
                sp.dma_start(x3_t[:, bass.ds(i * (Q * CH) + q * CH, CH)], x3[:, q, :]).then_inc(x_out[q], 16)

            def body(i):
                for q in range(Q):
                    at = bass.ds(i * (Q * CH) + q * CH, CH)
                    wait_count(sp, centred, nth(i, q, -3))
                    sp.dma_start(tin[:, q, :], t_t[:, at]).then_inc(t_in[q], 16)
                for q in range(Q):
                    at = bass.ds(i * (Q * CH) + q * CH, CH)
                    wait_count(sp, x3_done, nth(i, q, -3))
                    sp.dma_start(gin[:, q, :], go_t[:, at]).then_inc(gx_in[q], 16)
                    sp.dma_start(xin[:, q, :], x2_t[:, at]).then_inc(gx_in[q], 16)
                    if not (isinstance(i, int) and i == 0):
                        store(i - 1, q)
            looped(sp, 0, NCH // Q, 1, body)
            for q in range(Q):
                store(NCH // Q - 1, q)
            for q in range(Q):
                sp.wait_ge(x_out[q], NCH // Q * 16)

        @block.tensor
        def _(pe):
            def body(i):
                def centre(q):
                    wait_count(pe, t_in[q], i * 16 + 16)
                    wait_count(pe, tn_done, nth(i, q, -3))
                    nc.tensor.matmul(CEN[q], const["center"][:, :], tin[:, q, :], start=True, stop=True).then_inc(centred, 1)

                def variance(q):
                    wait_count(pe, squared, nth(i, q, 1))
                    wait_count(pe, ln_done, nth(i, q, -1))
                    nc.tensor.matmul(VAR[q % 2], const["mean"][:, :], sq[:, q % 2, :], start=True, stop=True).then_inc(var_done, 1)

                def output(q):
                    wait_count(pe, tn_done, nth(i, q, 1))
                    wait_count(pe, y_done, nth(i, q, -1))
                    nc.tensor.matmul(OUT[q % 2], W["Wo"][:, :], tn[:, q, :], start=True, stop=True).then_inc(out_mm, 1)

                centre(0), centre(1), variance(0), centre(2), variance(1), centre(3), variance(2)
                output(0), variance(3), output(1), output(2), output(3)
            looped(pe, 0, NCH // Q, 1, body)

        @block.scalar
        def _(act):
            act.wait_ge(eps_set, 1)
            load_log_exp(nc, act)

            def body(i):
                def square(q):
                    wait_count(act, centred, nth(i, q, 1))
                    wait_count(act, var_done, nth(i, q, -1))
                    nc.scalar.activation(sq[:, q % 2, :], CEN[q], ACT.Square).then_inc(squared, 1)

                def inverse_deviation(q):
                    wait_count(act, var_done, nth(i, q, 1))
                    nc.scalar.activation(lnv[:, q % 2, :], VAR[q % 2], ACT.Ln, bias=eps[:, 0:1]).then_inc(ln_done, 1)
                    wait_count(act, ln_done, nth(i, q, 1))
                    wait_count(act, tn_done, nth(i, q, -1))
                    nc.scalar.activation(rstd[:, q % 2, :], lnv[:, q % 2, :], ACT.Exp, scale=-0.5).then_inc(rstd_done, 1)

                square(0), square(1), inverse_deviation(0), square(2), inverse_deviation(1), square(3)
                inverse_deviation(2), inverse_deviation(3)
            looped(act, 0, NCH // Q, 1, body)

        @block.vector
        def _(dve):
            def body(i):
                def normalise(q):
                    wait_count(dve, rstd_done, nth(i, q, 1))
                    wait_count(dve, out_mm, nth(i, q, -3))
                    nc.vector.tensor_tensor(tn[:, q, :], CEN[q], rstd[:, q % 2, :], ALU.mult).then_inc(tn_done, 1)

                def gate(q):
                    wait_count(dve, out_mm, nth(i, q, 1))
                    wait_count(dve, gx_in[q], i * 32 + 32)
                    wait_count(dve, x3_done, nth(i, q, -3))
                    nc.vector.scalar_tensor_tensor(y[:, q, :], OUT[q % 2], W["o_off"][:, 0:1], gin[:, q, :], ALU.add, ALU.mult).then_inc(y_done, 1)

                def count(q):
                    wait_count(dve, x3_done, nth(i, q, 1))
                    nc.vector.bn_stats(stats[:, bass.ds(i * (Q * 6) + q * 6, 6)], x3[:, q, :]).then_inc(x3_counted, 1)

                normalise(0), normalise(1), normalise(2), gate(0), normalise(3), gate(1), gate(2)
                count(0), gate(3), count(1), count(2), count(3)
            looped(dve, 0, NCH // Q, 1, body)

        @block.gpsimd
        def _(pool):
            nc.gpsimd.memset(eps[:, :], EPS).then_inc(eps_set, 1)

            def body(i):
                for q in range(Q):
                    wait_counts(pool, pool_passed, (y_done, nth(i, q, 1)), (x_out[q], i * 16), (x3_counted, nth(i, q, -3)),
                                (gx_in[q], i * 32 + 32))
                    nc.gpsimd.tensor_tensor(x3[:, q, :], y[:, q, :], xin[:, q, :], ALU.add).then_inc(x3_done, 1)
            looped(pool, 0, NCH // Q, 1, body)


PARTS3 = ("r", "i")
C2 = P // 2
GATES = ("f", "i", "d")
KAREA = 49
STEPS = {
    "pe": [("mi_r", 1), ("mi_i", 1), ("mf_r", 1), ("mf_i", 1), ("mA_r", 2), ("mB_r", 2), ("mA_i", 2), ("mB_i", 2),
        ("md_r", 2), ("md_i", 2)],
    "act": [("tau8sq", 0), ("det8", 0), ("lnw", 1), ("scale", 1), ("lnd", 0), ("abs_r", 1), ("relu_r", 1), ("rd", 0),
        ("abs_i", 1), ("exp_r", 1), ("log_r", 1), ("relu_i", 1), ("exp_i", 1), ("scale2", 1), ("i_i", 1), ("f_r", 1),
        ("i_r", 1), ("f_i", 1), ("log_i", 1), ("sq_i", 2), ("sq_r", 2), ("tausq", 1), ("det2", 1), ("lnA", 2),
        ("tau2sq", 1), ("mag", 2), ("expm", 2), ("det4", 1), ("tau4sq", 1), ("g_r", 2), ("g_i", 2)],
    "pool": [("P3", 0), ("P4", 0), ("P2", 0), ("v", 0), ("Ah_i", 0), ("Bx_i", 1), ("y_i", 0), ("y_r", 0), ("h1_i", 0),
        ("h1_r", 0), ("fsum", 1), ("A2f", 1), ("A2", 2), ("sp_i", 1), ("u4", 1), ("inp_r", 1), ("u8", 1)],
    "dve": [("magexp", 1), ("inp_i", 0), ("tau8", 0), ("w", 1), ("Bx4", 1), ("u16", 0), ("P1", 0), ("tau16", 0), ("tu",
        0), ("As_r", 1), ("Bx3", 1), ("Bx1", 1), ("num", 0), ("As_i", 1), ("alpha", 0), ("Ah_r", 0), ("ad", 0), ("sp_r",
        1), ("beta", 0), ("Bx2", 1), ("h2_i", 0), ("h2_r", 0), ("Bx_r", 1), ("h_i", 0), ("fprod", 1), ("h_r", 0),
        ("tau", 1), ("out_r", 0), ("det", 1), ("out_i", 0), ("tau2", 1), ("dif", 1), ("gate_r", 1), ("tau4", 1),
        ("gate_i", 1)],
    "sp": [("table", 2), ("x_r", 2), ("x_i", 2), ("st_i", 0), ("st_r", 0)],
}
RECURRENCE = Schedule(TOK // 2 // CH, -2, STEPS)
AHEAD = RECURRENCE.ahead


def recurrence_weights(nc, d, W, affine):
    with ExitStack() as ctx:
        sb = lambda n, s: ctx.enter_context(nc.sbuf_tensor("h_raw_" + n, s, F32))
        new_sem = ctx.enter_context(phase_semaphores(nc))
        sem = lambda n: new_sem("h_w_" + n)
        ri, ir = sb("ri", [2 * KAREA, 2, C2]), sb("ir", [2 * KAREA, 2, C2])
        sign = sb("sign", [2 * KAREA, 2])
        zeroed, loaded, chain = sem("zeroed"), sem("loaded"), sem("chain")
        block = ctx.enter_context(nc.Block())
        count = [0]

        @block.sync
        def _(sp):
            def load(to, of):
                sp.dma_start(to, of).then_inc(loaded, 16)
                count[0] += 16
            with nc.allow_non_contiguous_dma(reason="columns of one element"):
                load(sign[:, :], d["c_sign"])
                for k, name in enumerate("AB"):
                    re, im = d[f"L3_conv_{name}_real"], d[f"L3_conv_{name}_imag"]
                    load(ri[0:KAREA, k, :], re), load(ri[KAREA:2 * KAREA, k, :], im)
                    load(ir[0:KAREA, k, :], im), load(ir[KAREA:2 * KAREA, k, :], re)
                sp.wait_ge(zeroed, 1)
                for blk in range(2):
                    to = slice(blk * C2, (blk + 1) * C2)
                    for o in range(2):
                        of = slice(o * C2, (o + 1) * C2)
                        for g, gate in enumerate(GATES):
                            for s in range(2):
                                load(W["gates"][to, g, o, s, to], d["L3_conv_W" + gate][s * C2:(s + 1) * C2, of])
                            load(W["g_off"][to, 2 * g + o:2 * g + o + 1], d["L3_conv_b" + gate][of, :])
                        load(W["gn"][to, 2 * o:2 * o + 2], affine[of, 0:2])
            sp.wait_ge(loaded, count[0])

        @block.vector
        def _(dve):
            link = linker(dve, chain)
            nc.vector.memset(W["gates"][:, :, :, :, :], 0.0).then_inc(zeroed, 1)
            dve.wait_ge(loaded, count[0])
            link(nc.vector.tensor_scalar(W["g_off"][:, 0:2], W["g_off"][:, 0:2], 2.0, None, ALU.add))
            link(nc.vector.memset(W["tiny"][:, :], 1e-8))
            for k in range(2):
                for part, raw in enumerate((ri, ir)):
                    own, far = W["kern"][:, 2 * k + part, 0:C2], W["kern"][:, 2 * k + part, C2:P]
                    link(nc.vector.tensor_scalar(own, raw[:, k, :], sign[:, 0:1] if part else 1.0, None, ALU.mult))
                    link(nc.vector.tensor_scalar(far, own, sign[:, 1:2], None, ALU.mult))
            link(nc.vector.tensor_scalar(W["kern"][:, 2:4, :], W["kern"][:, 2:4, :], 0.1, None, ALU.mult))


def recurrence(nc, d, x3_t, out, W, ps):
    F = CH
    HALFTOK = TOK // 2
    ITERS = RECURRENCE.rounds
    MUL, ADD, SUB = ALU.mult, ALU.add, ALU.subtract
    with ExitStack() as ctx:
        new_sem = ctx.enter_context(phase_semaphores(nc))
        sem = lambda n: new_sem("h_" + n)
        sb = lambda n, depth: ctx.enter_context(nc.sbuf_tensor("h_" + n, [P, depth, F], F32))
        two = ("x_r x_i g_r g_i f_r f_i i_r i_i sq_r expm As_r As_i inp_r inp_i fsum fprod tau det out_r out_i").split()
        one = ("sq_i lnA scale abs_r relu_r abs_i relu_i Bx1 Bx2 Bx3 Bx4 tausq tau2sq det2 det4 tau4sq det8 tau8sq "
               "u4 tu num dif ad P1 P2 P3 P4 h2_r h2_i").split()
        T = {n: sb(n, 2) for n in two} | {n: sb(n, 1) for n in one}
        for value, place in (("A2", "sq_r"), ("mag", "lnA"), ("magexp", "expm"), ("w", "expm"), ("lnw", "expm"), ("scale2",
                             "expm"), ("exp_r", "abs_r"), ("log_r", "abs_r"), ("sp_r", "relu_r"),
                             ("gate_r", "relu_r"), ("exp_i", "abs_i"), ("log_i", "abs_i"), ("sp_i",
                             "relu_i"), ("gate_i", "relu_i"), ("Bx_r", "Bx1"), ("Bx_i", "Bx3"),
                             ("A2f", "fprod"), ("tau2", "tausq"), ("tau4", "tau2sq"), ("tau8",
                             "tau4sq"), ("tau16", "tau8sq"), ("u8", "u4"), ("u16", "u4"), ("v",
                             "tu"), ("lnd", "dif"), ("rd", "dif"), ("alpha", "num"), ("beta", "ad"),
                             ("Ah_r", "P1"), ("Ah_i", "P3"), ("y_r", "P1"), ("h1_r", "P1"), ("h_r",
                             "P1"), ("y_i", "P3"), ("h1_i", "P3"), ("h_i", "P3")):
            T[value] = T[place]
        T["table"] = ctx.enter_context(nc.sbuf_tensor("h_table", [2 * KAREA, 2, F], F32))
        BANK = {"bd_r": 0, "bf_r": 0, "bd_i": 1, "bf_i": 1, "bi_r": 2, "bi_i": 3, "bA_r": 4, "bA_i": 5, "bB_r": 6,
                "bB_i": 7}
        pe_done, act_done, pool_done, dve_done = sem("pe_done"), sem("act_done"), sem("pool_done"), sem("dve_done")
        x_in, table_in, out_st = [[sem(f"{n}{r}") for r in range(2)] for n in ("x_in", "table_in", "out_st")]
        pool_passed, sp_passed = sem("pool_passed"), sem("sp_passed")
        block = ctx.enter_context(nc.Block())

        def place(slot, name):
            if name in BANK:
                return ps[:, BANK[name], :]
            return T[name][:, slot.parity if T[name].shape[1] == 2 else 0, :]

        def gate_off(g, o):
            return W["g_off"][:, 2 * g + o:2 * g + o + 1]

        @block.sync
        def _(sp):
            def slot(i, r):
                s = Slot(RECURRENCE, sp, None, i, r)
                at = s.at

                def load_x(step, o):
                    if s.runs(step):
                        for blk in range(2):
                            sp.dma_start(T[step][blk * C2:(blk + 1) * C2, (r + AHEAD[step]) % 2, :],
                                         x3_t[o * C2:(o + 1) * C2, bass.ds(i * (2 * F) + (blk * HALFTOK + (r + AHEAD[step]) * F), F)]
                                         ).then_inc(x_in[(r + AHEAD[step]) % 2], 16)

                def load_table(step):
                    if s.runs(step):
                        sp.dma_start(T["table"][:, (r + AHEAD[step]) % 2, :],
                                     d["c_table"][:, bass.ds(i * (2 * F) + (r + AHEAD[step]) * F, F)]).then_inc(table_in[(r + AHEAD[step]) % 2], 16)

                def store(step, value, o):
                    if s.runs(step):
                        for blk in range(2):
                            sp.dma_start(out[o * C2:(o + 1) * C2, bass.ds(i * (2 * F) + (blk * HALFTOK + (r + AHEAD[step]) * F), F)],
                                         T[value][blk * C2:(blk + 1) * C2, (r + AHEAD[step]) % T[value].shape[1], :]
                                         ).then_inc(out_st[(r + AHEAD[step]) % 2], 16)

                wait_counts(sp, sp_passed, (pe_done, at("table", "mB_i", 2)))
                load_table("table")
                wait_counts(sp, sp_passed, (act_done, at("x_r", "g_r", 2)))
                wait_counts(sp, sp_passed, (dve_done, at("x_r", "out_r", 2)))
                load_x("x_r", 0)
                wait_counts(sp, sp_passed, (act_done, at("x_i", "g_i", 2)))
                wait_counts(sp, sp_passed, (dve_done, at("x_i", "out_i", 2)))
                load_x("x_i", 1)
                store("st_i", "out_i", 1)
                store("st_r", "out_r", 0)
            RECURRENCE.run(sp, slot)
            for r in range(2):
                sp.wait_ge(out_st[r], ITERS // 2 * 64)

        @block.tensor
        def _(pe):
            def slot(i, r):
                s = Slot(RECURRENCE, pe, pe_done, i, r)
                at, on, t = s.at, s.on, lambda name: place(s, name)
                wait_count(pe, act_done, at("mi_r", "g_i"))
                if on("mi_r"):
                    nc.tensor.matmul(t("bi_r"), W["gates"][:, 1, 0, 0, :], t("g_r"), start=True, stop=False)
                    nc.tensor.matmul(t("bi_r"), W["gates"][:, 1, 0, 1, :], t("g_i"), start=False, stop=True).then_inc(pe_done, 1)
                if on("mi_i"):
                    nc.tensor.matmul(t("bi_i"), W["gates"][:, 1, 1, 0, :], t("g_r"), start=True, stop=False)
                    nc.tensor.matmul(t("bi_i"), W["gates"][:, 1, 1, 1, :], t("g_i"), start=False, stop=True).then_inc(pe_done, 1)
                wait_count(pe, act_done, at("mf_r", "relu_r"))
                if on("mf_r"):
                    nc.tensor.matmul(t("bf_r"), W["gates"][:, 0, 0, 0, :], t("g_r"), start=True, stop=False)
                    nc.tensor.matmul(t("bf_r"), W["gates"][:, 0, 0, 1, :], t("g_i"), start=False, stop=True).then_inc(pe_done, 1)
                wait_count(pe, act_done, at("mf_i", "relu_i"))
                if on("mf_i"):
                    nc.tensor.matmul(t("bf_i"), W["gates"][:, 0, 1, 0, :], t("g_r"), start=True, stop=False)
                    nc.tensor.matmul(t("bf_i"), W["gates"][:, 0, 1, 1, :], t("g_i"), start=False, stop=True).then_inc(pe_done, 1)
                wait_count(pe, dve_done, at("mA_r", "As_r", 1))
                wait_count(pe, *s.moved(table_in, "mA_r", 16))
                if on("mA_r"):
                    nc.tensor.matmul(t("bA_r"), W["kern"][:, 0, :], t("table"), start=True, stop=True).then_inc(pe_done, 1)
                wait_count(pe, dve_done, at("mB_r", "Bx1", 1))
                wait_count(pe, *s.moved(table_in, "mB_r", 16))
                if on("mB_r"):
                    nc.tensor.matmul(t("bB_r"), W["kern"][:, 2, :], t("table"), start=True, stop=True).then_inc(pe_done, 1)
                wait_count(pe, dve_done, at("mA_i", "As_i", 1))
                wait_count(pe, *s.moved(table_in, "mA_i", 16))
                if on("mA_i"):
                    nc.tensor.matmul(t("bA_i"), W["kern"][:, 1, :], t("table"), start=True, stop=True).then_inc(pe_done, 1)
                wait_count(pe, dve_done, at("mB_i", "Bx2", 1))
                wait_count(pe, *s.moved(table_in, "mB_i", 16))
                if on("mB_i"):
                    nc.tensor.matmul(t("bB_i"), W["kern"][:, 3, :], t("table"), start=True, stop=True).then_inc(pe_done, 1)
                wait_count(pe, act_done, at("md_r", "g_i"))
                if on("md_r"):
                    nc.tensor.matmul(t("bd_r"), W["gates"][:, 2, 0, 0, :], t("g_r"), start=True, stop=False)
                    nc.tensor.matmul(t("bd_r"), W["gates"][:, 2, 0, 1, :], t("g_i"), start=False, stop=True).then_inc(pe_done, 1)
                if on("md_i"):
                    nc.tensor.matmul(t("bd_i"), W["gates"][:, 2, 1, 0, :], t("g_r"), start=True, stop=False)
                    nc.tensor.matmul(t("bd_i"), W["gates"][:, 2, 1, 1, :], t("g_i"), start=False, stop=True).then_inc(pe_done, 1)
            RECURRENCE.run(pe, slot)

        @block.scalar
        def _(act):
            def slot(i, r):
                s = Slot(RECURRENCE, act, act_done, i, r)
                at, on, t = s.at, s.on, lambda name: place(s, name)
                wait_count(act, dve_done, at("tau8sq", "tau8"))
                wait_count(act, pool_done, at("tau8sq", "v", 1))
                if on("tau8sq"):
                    nc.scalar.activation(t("tau8sq"), t("tau8"), ACT.Square).then_inc(act_done, 1)
                wait_count(act, act_done, at("det8", "det4"))
                if on("det8"):
                    nc.scalar.activation(t("det8"), t("det4"), ACT.Square).then_inc(act_done, 1)
                wait_count(act, dve_done, at("lnw", "w"))
                if on("lnw"):
                    nc.scalar.activation(t("lnw"), t("w"), ACT.Ln).then_inc(act_done, 1)
                wait_count(act, act_done, at("scale", "lnw"))
                if on("scale"):
                    nc.scalar.activation(t("scale"), t("lnw"), ACT.Exp, scale=-1.0).then_inc(act_done, 1)
                if on("lnd"):
                    nc.scalar.activation(t("lnd"), t("dif"), ACT.Ln, scale=-1.0, bias=1.0).then_inc(act_done, 1)
                wait_count(act, pe_done, at("abs_r", "md_r"))
                if on("abs_r"):
                    nc.scalar.activation(t("abs_r"), t("bd_r"), ACT.Abs, bias=gate_off(2, 0)).then_inc(act_done, 1)
                wait_count(act, pool_done, at("relu_r", "inp_r", 1))
                if on("relu_r"):
                    nc.scalar.activation(t("relu_r"), t("bd_r"), ACT.Relu, bias=gate_off(2, 0)).then_inc(act_done, 1)
                wait_count(act, act_done, at("rd", "lnd"))
                if on("rd"):
                    nc.scalar.activation(t("rd"), t("lnd"), ACT.Exp, scale=-1.0).then_inc(act_done, 1)
                wait_count(act, pe_done, at("abs_i", "md_i"))
                if on("abs_i"):
                    nc.scalar.activation(t("abs_i"), t("bd_i"), ACT.Abs, bias=gate_off(2, 1)).then_inc(act_done, 1)
                wait_count(act, act_done, at("exp_r", "abs_r"))
                if on("exp_r"):
                    nc.scalar.activation(t("exp_r"), t("abs_r"), ACT.Exp, scale=-1.0).then_inc(act_done, 1)
                wait_count(act, act_done, at("log_r", "exp_r"))
                if on("log_r"):
                    nc.scalar.activation(t("log_r"), t("exp_r"), ACT.Ln, bias=1.0).then_inc(act_done, 1)
                if on("relu_i"):
                    nc.scalar.activation(t("relu_i"), t("bd_i"), ACT.Relu, bias=gate_off(2, 1)).then_inc(act_done, 1)
                if on("exp_i"):
                    nc.scalar.activation(t("exp_i"), t("abs_i"), ACT.Exp, scale=-1.0).then_inc(act_done, 1)
                if on("scale2"):
                    nc.scalar.activation(t("scale2"), t("lnw"), ACT.Exp, scale=-2.0).then_inc(act_done, 1)
                wait_count(act, pe_done, at("i_i", "mi_i"))
                if on("i_i"):
                    nc.scalar.activation(t("i_i"), t("bi_i"), ACT.Sigmoid, bias=gate_off(1, 1)).then_inc(act_done, 1)
                wait_count(act, pe_done, at("f_r", "mf_r"))
                if on("f_r"):
                    nc.scalar.activation(t("f_r"), t("bf_r"), ACT.Sigmoid, bias=gate_off(0, 0)).then_inc(act_done, 1)
                if on("i_r"):
                    nc.scalar.activation(t("i_r"), t("bi_r"), ACT.Sigmoid, bias=gate_off(1, 0)).then_inc(act_done, 1)
                wait_count(act, pe_done, at("f_i", "mf_i"))
                if on("f_i"):
                    nc.scalar.activation(t("f_i"), t("bf_i"), ACT.Sigmoid, bias=gate_off(0, 1)).then_inc(act_done, 1)
                load_log_exp(nc, act)
                wait_count(act, act_done, at("log_i", "exp_i"))
                if on("log_i"):
                    nc.scalar.activation(t("log_i"), t("exp_i"), ACT.Ln, bias=1.0).then_inc(act_done, 1)
                wait_count(act, pe_done, at("sq_i", "mA_i"))
                if on("sq_i"):
                    nc.scalar.activation(t("sq_i"), t("bA_i"), ACT.Square).then_inc(act_done, 1)
                if on("sq_r"):
                    nc.scalar.activation(t("sq_r"), t("bA_r"), ACT.Square).then_inc(act_done, 1)
                wait_count(act, dve_done, at("tausq", "tau"))
                if on("tausq"):
                    nc.scalar.activation(t("tausq"), t("tau"), ACT.Square).then_inc(act_done, 1)
                wait_count(act, dve_done, at("det2", "det"))
                if on("det2"):
                    nc.scalar.activation(t("det2"), t("det"), ACT.Square).then_inc(act_done, 1)
                wait_count(act, pool_done, at("lnA", "A2"))
                if on("lnA"):
                    nc.scalar.activation(t("lnA"), t("A2"), ACT.Ln, bias=W["tiny"][:, 0:1]).then_inc(act_done, 1)
                wait_count(act, dve_done, at("tau2sq", "tau2"))
                if on("tau2sq"):
                    nc.scalar.activation(t("tau2sq"), t("tau2"), ACT.Square).then_inc(act_done, 1)
                wait_count(act, act_done, at("mag", "lnA"))
                if on("mag"):
                    nc.scalar.activation(t("mag"), t("lnA"), ACT.Exp, scale=0.5).then_inc(act_done, 1)
                wait_count(act, act_done, at("expm", "mag"))
                if on("expm"):
                    nc.scalar.activation(t("expm"), t("mag"), ACT.Exp, scale=-1.0).then_inc(act_done, 1)
                if on("det4"):
                    nc.scalar.activation(t("det4"), t("det2"), ACT.Square).then_inc(act_done, 1)
                wait_count(act, dve_done, at("tau4sq", "tau4"))
                if on("tau4sq"):
                    nc.scalar.activation(t("tau4sq"), t("tau4"), ACT.Square).then_inc(act_done, 1)
                wait_count(act, *s.moved(x_in, "g_r", 64))
                if on("g_r"):
                    nc.scalar.activation(t("g_r"), t("x_r"), ACT.Identity, bias=W["gn"][:, 1:2], scale=W["gn"][:, 0:1]).then_inc(act_done, 1)
                wait_count(act, *s.moved(x_in, "g_i", 64))
                if on("g_i"):
                    nc.scalar.activation(t("g_i"), t("x_i"), ACT.Identity, bias=W["gn"][:, 3:4], scale=W["gn"][:, 2:3]).then_inc(act_done, 1)
            RECURRENCE.run(act, slot)

        @block.gpsimd
        def _(pool):
            def slot(i, r):
                s = Slot(RECURRENCE, pool, pool_done, i, r)
                at, on, t = s.at, s.on, lambda name: place(s, name)
                wait_counts(pool, pool_passed, (dve_done, at("P3", "inp_i")))
                if on("P3"):
                    nc.gpsimd.tensor_tensor(t("P3"), t("As_r"), t("inp_i"), MUL).then_inc(pool_done, 1)
                wait_counts(pool, pool_passed, (pool_done, at("P4", "inp_r")))
                if on("P4"):
                    nc.gpsimd.tensor_tensor(t("P4"), t("As_i"), t("inp_r"), MUL).then_inc(pool_done, 1)
                if on("P2"):
                    nc.gpsimd.tensor_tensor(t("P2"), t("As_i"), t("inp_i"), MUL).then_inc(pool_done, 1)
                wait_counts(pool, pool_passed, (dve_done, at("v", "tu")))
                if on("v"):
                    nc.gpsimd.tensor_tensor(t("v"), t("tu"), t("tau16"), SUB).then_inc(pool_done, 1)
                wait_counts(pool, pool_passed, (pool_done, at("Ah_i", "P4")))
                if on("Ah_i"):
                    nc.gpsimd.tensor_tensor(t("Ah_i"), t("P3"), t("P4"), ADD).then_inc(pool_done, 1)
                wait_counts(pool, pool_passed, (dve_done, at("Bx_i", "Bx3")))
                if on("Bx_i"):
                    nc.gpsimd.tensor_tensor(t("Bx_i"), t("Bx3"), t("Bx4"), ADD).then_inc(pool_done, 1)
                wait_counts(pool, pool_passed, (pool_done, at("y_i", "Ah_i")), (act_done, at("y_i", "f_i")))
                if on("y_i"):
                    nc.gpsimd.tensor_tensor(t("y_i"), t("Ah_i"), t("f_i"), MUL).then_inc(pool_done, 1)
                wait_counts(pool, pool_passed, (dve_done, at("y_r", "Ah_r")))
                if on("y_r"):
                    nc.gpsimd.tensor_tensor(t("y_r"), t("Ah_r"), t("f_r"), MUL).then_inc(pool_done, 1)
                wait_counts(pool, pool_passed, (pool_done, at("h1_i", "y_i")))
                if on("h1_i"):
                    nc.gpsimd.tensor_tensor(t("h1_i"), t("y_i"), t("alpha"), MUL).then_inc(pool_done, 1)
                wait_counts(pool, pool_passed, (pool_done, at("h1_r", "y_r")))
                if on("h1_r"):
                    nc.gpsimd.tensor_tensor(t("h1_r"), t("y_r"), t("alpha"), MUL).then_inc(pool_done, 1)
                wait_counts(pool, pool_passed, (act_done, at("fsum", "f_i")))
                if on("fsum"):
                    nc.gpsimd.tensor_tensor(t("fsum"), t("f_r"), t("f_i"), ADD).then_inc(pool_done, 1)
                wait_counts(pool, pool_passed, (dve_done, at("A2f", "fprod")))
                if on("A2f"):
                    nc.gpsimd.tensor_tensor(t("A2f"), t("A2"), t("fprod"), MUL).then_inc(pool_done, 1)
                wait_counts(pool, pool_passed, (act_done, at("A2", "sq_r")))
                if on("A2"):
                    nc.gpsimd.tensor_tensor(t("A2"), t("sq_r"), t("sq_i"), ADD).then_inc(pool_done, 1)
                if on("sp_i"):
                    nc.gpsimd.tensor_tensor(t("sp_i"), t("relu_i"), t("log_i"), ADD).then_inc(pool_done, 1)
                wait_counts(pool, pool_passed, (dve_done, at("u4", "tau2")))
                if on("u4"):
                    nc.gpsimd.tensor_tensor(t("u4"), t("tau"), t("tau2"), MUL).then_inc(pool_done, 1)
                wait_counts(pool, pool_passed, (dve_done, at("inp_r", "gate_r")))
                if on("inp_r"):
                    nc.gpsimd.tensor_tensor(t("inp_r"), t("Bx_r"), t("gate_r"), MUL).then_inc(pool_done, 1)
                wait_counts(pool, pool_passed, (pool_done, at("u8", "u4")), (dve_done, at("u8", "tau4")))
                if on("u8"):
                    nc.gpsimd.tensor_tensor(t("u8"), t("u4"), t("tau4"), MUL).then_inc(pool_done, 1)
            RECURRENCE.run(pool, slot)

        @block.vector
        def _(dve):
            def slot(i, r):
                s = Slot(RECURRENCE, dve, dve_done, i, r)
                at, on, t = s.at, s.on, lambda name: place(s, name)
                wait_count(dve, act_done, at("magexp", "expm"))
                if on("magexp"):
                    nc.vector.scalar_tensor_tensor(t("magexp"), t("mag"), 1e-8, t("expm"), ADD, MUL).then_inc(dve_done, 1)
                wait_count(dve, pool_done, at("inp_i", "Bx_i"))
                wait_count(dve, dve_done, at("inp_i", "gate_i"))
                if on("inp_i"):
                    nc.vector.tensor_tensor(t("inp_i"), t("Bx_i"), t("gate_i"), MUL).then_inc(dve_done, 1)
                wait_count(dve, act_done, at("tau8", "tau4sq"))
                if on("tau8"):
                    nc.vector.scalar_tensor_tensor(t("tau8"), t("det4"), -2.0, t("tau4sq"), MUL, ADD).then_inc(dve_done, 1)
                wait_count(dve, dve_done, at("w", "magexp"))
                if on("w"):
                    nc.vector.scalar_tensor_tensor(t("w"), t("mag"), 1e-8, t("magexp"), ADD, ADD).then_inc(dve_done, 1)
                wait_count(dve, pe_done, at("Bx4", "mB_i"))
                wait_count(dve, act_done, at("Bx4", "g_r"))
                if on("Bx4"):
                    nc.vector.tensor_tensor(t("Bx4"), t("bB_i"), t("g_r"), MUL).then_inc(dve_done, 1)
                wait_count(dve, pool_done, at("u16", "u8"))
                wait_count(dve, dve_done, at("u16", "tau8"))
                if on("u16"):
                    nc.vector.tensor_tensor(t("u16"), t("u8"), t("tau8"), MUL).then_inc(dve_done, 1)
                if on("P1"):
                    nc.vector.tensor_tensor(t("P1"), t("As_r"), t("inp_r"), MUL).then_inc(dve_done, 1)
                wait_count(dve, act_done, at("tau16", "det8"))
                if on("tau16"):
                    nc.vector.scalar_tensor_tensor(t("tau16"), t("det8"), -2.0, t("tau8sq"), MUL, ADD).then_inc(dve_done, 1)
                wait_count(dve, dve_done, at("tu", "u16"))
                if on("tu"):
                    nc.vector.tensor_tensor(t("tu"), t("tau"), t("u16"), MUL).then_inc(dve_done, 1)
                wait_count(dve, act_done, at("As_r", "scale"))
                if on("As_r"):
                    nc.vector.scalar_tensor_tensor(t("As_r"), t("bA_r"), 0.95, t("scale"), MUL, MUL).then_inc(dve_done, 1)
                if on("Bx3"):
                    nc.vector.tensor_tensor(t("Bx3"), t("bB_r"), t("g_i"), MUL).then_inc(dve_done, 1)
                if on("Bx1"):
                    nc.vector.tensor_tensor(t("Bx1"), t("bB_r"), t("g_r"), MUL).then_inc(dve_done, 1)
                wait_count(dve, pool_done, at("num", "v"))
                if on("num"):
                    nc.vector.scalar_tensor_tensor(t("num"), t("v"), 0.5, t("u16"), MUL, SUB).then_inc(dve_done, 1)
                if on("As_i"):
                    nc.vector.scalar_tensor_tensor(t("As_i"), t("bA_i"), 0.95, t("scale"), MUL, MUL).then_inc(dve_done, 1)
                wait_count(dve, dve_done, at("alpha", "num"))
                wait_count(dve, act_done, at("alpha", "rd"))
                if on("alpha"):
                    nc.vector.scalar_tensor_tensor(t("alpha"), t("num"), 1.0, t("rd"), ADD, MUL).then_inc(dve_done, 1)
                if on("Ah_r"):
                    nc.vector.tensor_tensor(t("Ah_r"), t("P1"), t("P2"), SUB).then_inc(dve_done, 1)
                wait_count(dve, dve_done, at("ad", "alpha"))
                if on("ad"):
                    nc.vector.tensor_tensor(t("ad"), t("alpha"), t("det"), MUL).then_inc(dve_done, 1)
                wait_count(dve, act_done, at("sp_r", "log_r"))
                if on("sp_r"):
                    nc.vector.tensor_tensor(t("sp_r"), t("relu_r"), t("log_r"), ADD).then_inc(dve_done, 1)
                wait_count(dve, dve_done, at("beta", "ad"))
                if on("beta"):
                    nc.vector.scalar_tensor_tensor(t("beta"), t("v"), 0.5, t("ad"), MUL, SUB).then_inc(dve_done, 1)
                if on("Bx2"):
                    nc.vector.tensor_tensor(t("Bx2"), t("bB_i"), t("g_i"), MUL).then_inc(dve_done, 1)
                wait_count(dve, dve_done, at("h2_i", "beta"))
                if on("h2_i"):
                    nc.vector.scalar_tensor_tensor(t("h2_i"), t("beta"), 1.0, t("inp_i"), ADD, MUL).then_inc(dve_done, 1)
                if on("h2_r"):
                    nc.vector.scalar_tensor_tensor(t("h2_r"), t("beta"), 1.0, t("inp_r"), ADD, MUL).then_inc(dve_done, 1)
                wait_count(dve, dve_done, at("Bx_r", "Bx2"))
                if on("Bx_r"):
                    nc.vector.tensor_tensor(t("Bx_r"), t("Bx1"), t("Bx2"), SUB).then_inc(dve_done, 1)
                wait_count(dve, pool_done, at("h_i", "h1_i"))
                wait_count(dve, dve_done, at("h_i", "h2_i"))
                if on("h_i"):
                    nc.vector.tensor_tensor(t("h_i"), t("h1_i"), t("h2_i"), ADD).then_inc(dve_done, 1)
                wait_count(dve, act_done, at("fprod", "f_i"))
                if on("fprod"):
                    nc.vector.tensor_tensor(t("fprod"), t("f_r"), t("f_i"), MUL).then_inc(dve_done, 1)
                wait_count(dve, pool_done, at("h_r", "h1_r"))
                wait_count(dve, dve_done, at("h_r", "h2_r"))
                if on("h_r"):
                    nc.vector.tensor_tensor(t("h_r"), t("h1_r"), t("h2_r"), ADD).then_inc(dve_done, 1)
                wait_count(dve, pool_done, at("tau", "fsum"))
                if on("tau"):
                    nc.vector.tensor_tensor(t("tau"), t("fsum"), t("As_r"), MUL).then_inc(dve_done, 1)
                wait_count(dve, dve_done, at("out_r", "h_r"))
                wait_count(dve, *s.moved(x_in, "out_r", 64))
                wait_count(dve, *s.moved(out_st, "out_r", 64, 2))
                if on("out_r"):
                    nc.vector.tensor_tensor(t("out_r"), t("h_r"), t("x_r"), ADD).then_inc(dve_done, 1)
                wait_count(dve, pool_done, at("det", "A2f"))
                if on("det"):
                    nc.vector.scalar_tensor_tensor(t("det"), t("A2f"), 0.95 * 0.95, t("scale2"), MUL, MUL).then_inc(dve_done, 1)
                wait_count(dve, *s.moved(x_in, "out_i", 64))
                wait_count(dve, *s.moved(out_st, "out_i", 64, 2))
                if on("out_i"):
                    nc.vector.tensor_tensor(t("out_i"), t("h_i"), t("x_i"), ADD).then_inc(dve_done, 1)
                wait_count(dve, act_done, at("tau2", "tausq"))
                wait_count(dve, dve_done, at("tau2", "det"))
                if on("tau2"):
                    nc.vector.scalar_tensor_tensor(t("tau2"), t("det"), -2.0, t("tausq"), MUL, ADD).then_inc(dve_done, 1)
                if on("dif"):
                    nc.vector.tensor_tensor(t("dif"), t("tau"), t("det"), SUB).then_inc(dve_done, 1)
                if on("gate_r"):
                    nc.vector.tensor_tensor(t("gate_r"), t("sp_r"), t("i_r"), MUL).then_inc(dve_done, 1)
                wait_count(dve, act_done, at("tau4", "tau2sq"))
                if on("tau4"):
                    nc.vector.scalar_tensor_tensor(t("tau4"), t("det2"), -2.0, t("tau2sq"), MUL, ADD).then_inc(dve_done, 1)
                wait_count(dve, pool_done, at("gate_i", "sp_i"))
                if on("gate_i"):
                    nc.vector.tensor_tensor(t("gate_i"), t("sp_i"), t("i_i"), MUL).then_inc(dve_done, 1)
            RECURRENCE.run(dve, slot)


def layer0(nc, d, z_t, bias_d, x_t, x1_t, stats, const, affine, ps):
    input_statistics(nc, x_t, stats)
    group_norm_affine(nc, "gn0", stats[:, 0:NCH * 6], const, affine, ps)
    with ExitStack() as layer:
        wsb = lambda n, s: layer.enter_context(nc.sbuf_tensor("w0_" + n, s, F32))
        W = {n: wsb(n, [P, P]) for n in ("Wq", "Wk", "Wv", "Wg", "Wo")}
        W["Wb"] = wsb("Wb", [P, HEADS])
        W |= {n: wsb(n, [P, 1]) for n in ("q_off", "k_off", "g_off", "b_off", "bo")}
        W["v_off"] = wsb("v_off", [P, HALF, P])
        attention_weights(nc, d, W, ps)
        attention_norm(nc, x_t, z_t, bias_d, W, const, affine, ps)
        row_attention(nc, x_t, z_t, bias_d, x1_t, W, const, stats, ps)


def layer1(nc, d, x1_t, x2_t, stats, const, affine, ps):
    group_norm_affine(nc, "gn1", stats[:, :], const, affine, ps)
    row_scan(nc, d, x1_t, x2_t, affine, stats, ps)


def layer2(nc, d, ab_d, go_t, t_t, x2_t, x3_t, stats, const, affine, ps):
    with ExitStack() as layer:
        wsb = lambda n, s, t=F32: layer.enter_context(nc.sbuf_tensor("w2_" + n, s, t))
        W = {"W4": wsb("W4", [P, CH]), "Wg": wsb("Wg", [P, P]), "Wo": wsb("Wo", [P, P]), "g_off": wsb("g_off", [P, 1]),
             "o_off": wsb("o_off", [P, 1]), "ones": wsb("ones", [P, P], BF16), "bias_parts": wsb("bias_parts", [P, CH], BF16)}
        group_norm_affine(nc, "gn2", stats[:, :], const, affine, ps)
        triangle_weights(nc, d, W, ps)
        triangle_projections(nc, x2_t, ab_d, go_t, W, const, affine, ps)
        triangle_products(nc, ab_d, t_t, ps)
        triangle_output(nc, t_t, go_t, x2_t, x3_t, W, const, stats, ps)


def layer3(nc, d, x3_t, out, stats, const, affine, ps):
    with ExitStack() as layer:
        wsb = lambda n, s: layer.enter_context(nc.sbuf_tensor("w3_" + n, s, F32))
        W = {"gates": wsb("gates", [P, 3, 2, 2, P]), "g_off": wsb("g_off", [P, 6]), "gn": wsb("gn", [P, 4]),
             "kern": wsb("kern", [2 * KAREA, 4, P]), "tiny": wsb("tiny", [P, 1])}
        group_norm_affine(nc, "gn3", stats[:, 0:NCH * 6], const, affine, ps)
        recurrence_weights(nc, d, W, affine)
        recurrence(nc, d, x3_t, out, W, ps)


def layers_kernel(nc, d, out):
    scratch = lambda name, shape: nc.dram_tensor(name, shape, F32).ap()
    x_t, z_t, bias_d = d["x"], scratch("z_t", (P, TOK)), scratch("bias_d", (HEADS, TOK))
    x1_t, x2_t, x3_t, t_t, go_t = [scratch(n, (P, TOK)) for n in ("x1_t", "x2_t", "x3_t", "t_t", "go_t")]
    ab_d = scratch("ab_d", (2, HC, HALF, P, N * HW))
    with ExitStack() as ctx:
        sb = lambda n, s: ctx.enter_context(nc.sbuf_tensor(n, s, F32))
        ps = ctx.enter_context(nc.psum_tensor("ps", [P, 8, CH], F32))
        const = {n: sb("const_" + n, [P, P]) for n in ("ident", "center", "mean", "group_mean")}
        stats, affine = sb("stats", [P, N * 6]), sb("affine", [P, P + 3])
        const_in = nc.alloc_semaphore("const_in")
        with nc.Block() as block:
            @block.sync
            def _(sp):
                for n, t in const.items():
                    sp.dma_start(t[:, :], d["c_" + n]).then_inc(const_in, 16)
                sp.wait_ge(const_in, 16 * len(const))

        layer0(nc, d, z_t, bias_d, x_t, x1_t, stats, const, affine, ps)
        layer1(nc, d, x1_t, x2_t, stats, const, affine, ps)
        layer2(nc, d, ab_d, go_t, t_t, x2_t, x3_t, stats, const, affine, ps)
        layer3(nc, d, x3_t, out, stats, const, affine, ps)


def kernel(**inputs):
    import numpy as np
    import concourse.bacc as bacc
    from concourse import mybir as mb
    from concourse.bass_utils import run_bass_kernel_spmd

    nc = bacc.Bacc("TRN2", target_bir_lowering=False, num_devices=1)
    arrays, d = laid_out(inputs), {}
    for name, a in arrays.items():
        d[name] = nc.dram_tensor(name, a.shape, mb.dt.from_np(a.dtype), kind="ExternalInput").ap()
    out = nc.dram_tensor("out_t", (128, 65536), mb.dt.float32, kind="ExternalOutput").ap()
    layers_kernel(nc, d, out)
    r = run_bass_kernel_spmd(nc, [arrays], core_ids=[0])
    got = r.results[0]["out_t"]
    return np.ascontiguousarray(got.T).reshape(1, 256, 256, 128)


def laid_out(inputs):
    import numpy as np
    arrays = {}
    for name, a in inputs.items():
        a = np.asarray(a)
        if name == "x":
            a = a.reshape(-1, 128).T
        elif name == "L1_conv_W":
            a = a.transpose(1, 0, 2)
        elif a.ndim == 1:
            a = a.reshape(-1, 1)
        elif name.startswith("L2_conv_"):
            a = a.T
        elif name.startswith(("L3_conv_A", "L3_conv_B")):
            a = a.reshape(64, 49).T
        arrays[name] = np.ascontiguousarray(a)
    c = 128
    arrays["c_ident"] = np.eye(c, dtype=np.float32)
    arrays["c_center"] = (np.eye(c) - 1.0 / c).astype(np.float32)
    arrays["c_mean"] = np.full((c, c), 1.0 / c, np.float32)
    arrays["c_group_mean"] = (np.kron(np.eye(32), np.ones((4, 4))) / 4).astype(np.float32)
    k, pad, half = 7, (256 - 7) // 2, 128
    p, q = np.divmod(np.arange(k * k), k)
    turns = (p + pad)[:, None, None] * np.arange(half)[None, :, None] + (q + pad)[:, None, None] * np.arange(256)[None, None, :]
    angle = (2 * np.pi / 256) * (turns % 256).reshape(k * k, -1)
    arrays["c_table"] = np.concatenate([np.cos(angle), np.sin(angle)]).astype(np.float32)
    odd = np.tile((-1.0) ** p, 2)
    arrays["c_sign"] = np.stack([np.repeat([1.0, -1.0], k * k), odd], 1).astype(np.float32)
    return arrays
```

```python
import concourse.bass as bass
from concourse import mybir
from contextlib import ExitStack, contextmanager

F32 = mybir.dt.float32
ALU = mybir.AluOpType
ACT = mybir.ActivationFunctionType

P = 128
N = 256
TOK = N * N
HEADS, HD = 4, 32
CH = 512
NCH = TOK // CH
HALF = N // P
QUARTER = P // 4
EPS = 1e-5


def wait_count(eng, sem, value):
    if isinstance(value, int) and value <= 0:
        return
    eng.wait_ge(sem, value)


def wait_counts(eng, passed, *counts):
    for sem, value in counts:
        wait_count(eng, sem, value)
    eng.sem_inc(passed, 1)


LOG_EXP_SET = 6


def load_log_exp(nc, act):
    act.add_instruction(mybir.InstLoadActFuncSet(
        name=nc.get_next_instruction_name(), act_func_set_id=LOG_EXP_SET, engine=mybir.EngineType.Activation))


def looped(eng, first, last, peel, body, tail=0):
    for i in range(first, first + peel):
        body(i)
    with eng.Fori(first + peel, last - tail) as i:
        body(i)
    for i in range(last - tail, last):
        body(i)


@contextmanager
def phase_semaphores(nc):
    given = []

    def sem(name):
        given.append(nc.alloc_semaphore(name))
        return given[-1]

    yield sem
    nc.clear_and_free_semaphores(given)
    nc.all_engine_barrier()


def linker(eng, sem):
    done = [0]

    def link(ins):
        done[0] += 1
        ins.then_inc(sem, 1)
        eng.wait_ge(sem, done[0])

    return link


class Schedule:
    def __init__(self, rounds, first_slot, steps):
        self.rounds, self.first_slot = rounds, first_slot
        self.ahead = {step: ahead for one in steps.values() for step, ahead in one}
        self.per_slot = {step: len(one) for one in steps.values() for step, _ in one}
        self.place = {step: n + 1 for one in steps.values() for n, (step, _) in enumerate(one)}

    def run(self, eng, slot):
        for s in range(self.first_slot, 2):
            slot(s // 2, s % 2)
        with eng.Fori(1, self.rounds // 2 - 2) as i:
            for r in range(2):
                slot(i, r)
        for s in range(self.rounds - 4, self.rounds):
            slot(s // 2, s % 2)


class Slot:
    def __init__(self, schedule, eng, done, i, r):
        self.schedule, self.eng, self.done, self.i, self.r = schedule, eng, done, i, r

    def runs(self, step, lag=0):
        return not isinstance(self.i, int) or 0 <= 2 * self.i + self.r + self.schedule.ahead[step] - lag < self.schedule.rounds

    def at(self, step, other, lag=0):
        S = self.schedule
        slots = self.r + S.ahead[step] - lag - S.ahead[other] - S.first_slot
        count = self.i * (2 * S.per_slot[other]) + (slots * S.per_slot[other] + S.place[other] + 1)
        return max(count, 1) if isinstance(count, int) else count

    def on(self, step):
        self.parity = self.side(step)
        if self.runs(step):
            return True
        self.eng.wait_ge(self.done, self.at(step, step) - 1)
        self.eng.sem_inc(self.done, 1)
        return False

    def side(self, step, lag=0):
        return (self.r + self.schedule.ahead[step] - lag) % 2

    def moved(self, step, count, lag=0):
        return self.i * count + ((self.r + self.schedule.ahead[step] - lag) // 2 + 1) * count


def group_norm_affine(nc, name, stats, const, affine, ps):
    with ExitStack() as ctx:
        sb = lambda n, s: ctx.enter_context(nc.sbuf_tensor(f"{name}_{n}", s, F32))
        new_sem = ctx.enter_context(phase_semaphores(nc))
        sem = lambda n: new_sem(f"{name}_" + n)
        mv, diff, spread, sd = sb("mv", [P, 2]), sb("diff", [P, 1]), sb("spread", [P, 1]), sb("sd", [P, 2])
        aggregated, group_mean_done, spread_done, group_var_done = (
            sem("aggregated"), sem("group_mean_done"), sem("spread_done"), sem("group_var_done"))
        var_ready, sd_ready, affine_ready, cen_offset_done, chain = (
            sem("var_ready"), sem("sd_ready"), sem("affine_ready"), sem("cen_offset_done"), sem("chain"))
        block = ctx.enter_context(nc.Block())

        @block.vector
        def _(dve):
            link = linker(dve, chain)
            nc.vector.bn_aggr(mv[:, :], stats).then_inc(aggregated, 1)
            dve.wait_ge(aggregated, 1)
            dve.wait_ge(group_mean_done, 1)
            link(nc.vector.tensor_tensor(diff[:, :], mv[:, 0:1], ps[:, 0, 0:1], ALU.subtract))
            nc.vector.scalar_tensor_tensor(spread[:, :], diff[:, :], diff[:, :], mv[:, 1:2],
                                           ALU.mult, ALU.add).then_inc(spread_done, 1)
            dve.wait_ge(group_var_done, 1)
            nc.vector.tensor_scalar(sd[:, 0:1], ps[:, 1, 0:1], EPS, None, ALU.add).then_inc(var_ready, 1)
            dve.wait_ge(sd_ready, 1)
            link(nc.vector.reciprocal(affine[:, 0:1], sd[:, 1:2]))
            nc.vector.scalar_tensor_tensor(affine[:, 1:2], ps[:, 0, 0:1], -1.0, affine[:, 0:1],
                                           ALU.mult, ALU.mult).then_inc(affine_ready, 1)
            link(nc.vector.tensor_scalar(affine[:, 2:2 + P], const["center"][:, :], affine[:, 0:1], None, ALU.mult))
            dve.wait_ge(cen_offset_done, 1)
            link(nc.vector.tensor_copy(affine[:, 2 + P:3 + P], ps[:, 2, 0:1]))

        @block.tensor
        def _(pe):
            pe.wait_ge(aggregated, 1)
            nc.tensor.matmul(ps[:, 0, 0:1], const["group_mean"][:, :], mv[:, 0:1],
                             start=True, stop=True).then_inc(group_mean_done, 1)
            pe.wait_ge(spread_done, 1)
            nc.tensor.matmul(ps[:, 1, 0:1], const["group_mean"][:, :], spread[:, :],
                             start=True, stop=True).then_inc(group_var_done, 1)
            pe.wait_ge(affine_ready, 1)
            nc.tensor.matmul(ps[:, 2, 0:1], const["center"][:, :], affine[:, 1:2],
                             start=True, stop=True).then_inc(cen_offset_done, 1)

        @block.scalar
        def _(act):
            act.wait_ge(var_ready, 1)
            nc.scalar.activation(sd[:, 1:2], sd[:, 0:1], ACT.Sqrt).then_inc(sd_ready, 1)


def input_statistics(nc, x_t, stats):
    PIECE = 4 * CH
    with ExitStack() as ctx:
        buf = ctx.enter_context(nc.sbuf_tensor("a_buf", [P, 2, PIECE], F32))
        sem = ctx.enter_context(phase_semaphores(nc))
        loaded = [sem(f"a_loaded{b}") for b in range(2)]
        counted = sem("a_counted")
        block = ctx.enter_context(nc.Block())

        @block.sync
        def _(sp):
            def body(i):
                for b in range(2):
                    wait_count(sp, counted, i * 8 + 4 * b - 4)
                    sp.dma_start(buf[:, b, :], x_t[:, bass.ds(i * (2 * PIECE) + b * PIECE, PIECE)]).then_inc(loaded[b], 16)
            looped(sp, 0, TOK // PIECE // 2, 1, body)

        @block.vector
        def _(dve):
            def body(i):
                for b in range(2):
                    wait_count(dve, loaded[b], i * 16 + 16)
                    for q in range(4):
                        nc.vector.bn_stats(stats[:, bass.ds(i * 48 + (b * 4 + q) * 6, 6)],
                                           buf[:, b, q * CH:(q + 1) * CH]).then_inc(counted, 1)
            looped(dve, 0, TOK // PIECE // 2, 1, body)


def attention_weights(nc, d, W, ps):
    with ExitStack() as ctx:
        raw = {n: ctx.enter_context(nc.sbuf_tensor(f"b_raw_{n}", [P, w], F32))
               for n, w in (("Wq", P), ("Wk", P), ("Wv", P), ("Wg", P), ("Wb", HEADS), ("Wo", P),
                            ("ln_gamma", 1), ("ln_beta", 1), ("bg", 1))}
        beta_rep = ctx.enter_context(nc.sbuf_tensor("b_beta_rep", [P, P], F32))
        sem = ctx.enter_context(phase_semaphores(nc))
        loaded, beta_ready, offsets_done, chain = (
            sem("b_w_loaded"), sem("b_beta_ready"), sem("b_offsets_done"), sem("b_w_chain"))
        block = ctx.enter_context(nc.Block())
        scale = HD ** -0.5

        @block.sync
        def _(sp):
            for n, t in raw.items():
                sp.dma_start(t[:, :], d["L0_conv_" + n]).then_inc(loaded, 16)
            sp.dma_start(W["bo"][:, :], d["L0_conv_bo"]).then_inc(loaded, 16)
            sp.wait_ge(loaded, 16 * (len(raw) + 1))

        @block.vector
        def _(dve):
            link = linker(dve, chain)
            dve.wait_ge(loaded, 16 * (len(raw) + 1))
            link(nc.vector.memset(beta_rep[:, :], 1.0))
            nc.vector.tensor_scalar(beta_rep[:, :], beta_rep[:, :], raw["ln_beta"][:, 0:1], None,
                                    ALU.mult).then_inc(beta_ready, 1)
            for n in ("Wq", "Wk", "Wv", "Wg", "Wb"):
                link(nc.vector.tensor_scalar(W[n][:, :], raw[n][:, :], raw["ln_gamma"][:, 0:1], None, ALU.mult))
            link(nc.vector.tensor_scalar(W["Wo"][:, :], raw["Wo"][:, :], 0.5, None, ALU.mult))
            dve.wait_ge(offsets_done, 4 + P // QUARTER)
            link(nc.vector.tensor_scalar(W["q_off"][:, :], ps[:, 0, 0:1], -scale, None, ALU.mult))
            link(nc.vector.tensor_copy(W["k_off"][:, :], ps[:, 1, 0:1]))
            link(nc.vector.tensor_scalar(W["g_off"][:, :], ps[:, 2, 0:1], raw["bg"][:, 0:1], 0.5, ALU.add, ALU.mult))
            for at in range(0, P, QUARTER):
                link(nc.vector.tensor_scalar(W["b_off"][at:at + HEADS, :], ps[at:at + HEADS, 3, 0:1], -1.0, None, ALU.mult))
            for kc in range(HALF):
                link(nc.vector.tensor_copy(W["v_off"][:, kc, :], ps[:, 4, 0:P]))

        @block.tensor
        def _(pe):
            pe.wait_ge(loaded, 16 * (len(raw) + 1))
            pe.wait_ge(beta_ready, 1)
            for n, w in enumerate(("Wq", "Wk", "Wg")):
                nc.tensor.matmul(ps[:, n, 0:1], raw[w][:, :], raw["ln_beta"][:, 0:1],
                                 start=True, stop=True).then_inc(offsets_done, 1)
            for at in range(0, P, QUARTER):
                nc.tensor.matmul(ps[at:at + HEADS, 3, 0:1], raw["Wb"][:, :], raw["ln_beta"][:, 0:1],
                                 start=True, stop=True).then_inc(offsets_done, 1)
            nc.tensor.matmul(ps[:, 4, 0:P], beta_rep[:, :], raw["Wv"][:, :],
                             start=True, stop=True).then_inc(offsets_done, 1)


NORM_STEPS = {
    "pe": [("mC1", 2), ("mC3", 2), ("mM2", 2), ("mM1", 2), ("mB", 1), ("mC0", 3), ("mM3", 2), ("mC2", 3), ("mM0", 3)],
    "act": [("ln0", 2), ("sq1", 2), ("rs0", 2), ("ln2", 2), ("rs2", 2), ("ln1", 2), ("sq3", 2), ("rs1", 2),
        ("sq0", 3), ("ln3", 2), ("rs3", 2), ("sq2", 3)],
    "dve": [("bc1", 0), ("bc0", 0), ("z0", 2), ("bc2", 1), ("z2", 2), ("z1", 2), ("z3", 2), ("bc3", 1)],
    "sp": [("zs0", 1), ("x1", 3), ("zs1", 0), ("x0", 3), ("x2", 3), ("bs2", 0), ("zs2", 1), ("bs3", 0), ("bs0", 0),
        ("bs1", 0), ("zs3", 1), ("x3", 3)],
}
NORM = Schedule(NCH // 4, -3, NORM_STEPS)


def attention_norm(nc, x_t, z_t, bias_d, W, const, affine, ps):
    Q = 4
    cen, cenb = affine[:, 2:2 + P], affine[:, 2 + P:3 + P]
    with ExitStack() as ctx:
        sb = lambda n, s: ctx.enter_context(nc.sbuf_tensor("b_" + n, s, F32))
        new_sem = ctx.enter_context(phase_semaphores(nc))
        sem = lambda n: new_sem("b_" + n)
        xin, z, bsb = sb("xin", [P, 2, Q, CH]), sb("z", [P, 2, Q, CH]), sb("bsb", [P, 2, CH])
        sq, lnv, rstd = sb("sq", [P, 2, CH]), sb("lnv", [P, 2, CH]), sb("rstd", [P, 2, CH])
        eps = sb("eps", [P, 1])
        x_in, z_out, b_out = [[[sem(f"{n}{c}{r}") for r in range(2)] for c in range(Q)] for n in ("x_in", "z_out", "b_out")]
        pe_done, act_done, dve_done = sem("pe_done"), sem("act_done"), sem("dve_done")
        eps_set, sp_passed = sem("eps_set"), sem("sp_passed")
        block = ctx.enter_context(nc.Block())
        CEN = [ps[:, q, :] for q in range(Q)]
        VAR = [ps[:, 4 + b, :] for b in range(2)]
        BIA = [ps[:, 6 + b, :] for b in range(2)]

        @block.sync
        def _(sp):
            def slot(i, r):
                s = Slot(NORM, sp, None, i, r)
                at = s.at

                def load(step, buffer, array, c, arrived):
                    if s.runs(step):
                        ahead = r + NORM.ahead[step]
                        sp.dma_start(buffer[:, ahead % 2, c, :], array[:, bass.ds(i * (2 * Q * CH) + (ahead * Q + c) * CH, CH)]
                                     ).then_inc(arrived[c][ahead % 2], 16)

                def store(step, array, buffer, c, stored):
                    if s.runs(step):
                        ahead = r + NORM.ahead[step]
                        sp.dma_start(array[:, bass.ds(i * (2 * Q * CH) + (ahead * Q + c) * CH, CH)], buffer[:, ahead % 2, c, :]
                                     ).then_inc(stored[c][ahead % 2], 16)

                def store_bias(step, c):
                    if s.runs(step):
                        ahead = r + NORM.ahead[step]
                        sp.dma_start(bias_d[:, bass.ds(i * (2 * Q * CH) + (ahead * Q + c) * CH, CH)],
                                     bsb[c * QUARTER:c * QUARTER + HEADS, ahead % 2, :]).then_inc(b_out[c][ahead % 2], 16)

                sp.wait_ge(dve_done, at("zs0", "z0"))
                sp.sem_inc(sp_passed, 1)
                store("zs0", z_t, z, 0, z_out)
                sp.wait_ge(pe_done, at("x1", "mC1", 2))
                sp.sem_inc(sp_passed, 1)
                load("x1", xin, x_t, 1, x_in)
                store("zs1", z_t, z, 1, z_out)
                load("x0", xin, x_t, 0, x_in)
                load("x2", xin, x_t, 2, x_in)
                sp.wait_ge(dve_done, at("bs2", "bc2"))
                sp.sem_inc(sp_passed, 1)
                store_bias("bs2", 2)
                sp.wait_ge(dve_done, at("zs2", "z2"))
                sp.sem_inc(sp_passed, 1)
                store("zs2", z_t, z, 2, z_out)
                sp.wait_ge(dve_done, at("bs3", "bc3"))
                sp.sem_inc(sp_passed, 1)
                store_bias("bs3", 3)
                sp.wait_ge(dve_done, at("bs0", "bc0"))
                sp.sem_inc(sp_passed, 1)
                store_bias("bs0", 0)
                store_bias("bs1", 1)
                store("zs3", z_t, z, 3, z_out)
                sp.wait_ge(pe_done, at("x3", "mC3", 2))
                sp.sem_inc(sp_passed, 1)
                load("x3", xin, x_t, 3, x_in)
            NORM.run(sp, slot)
            for stored in (z_out, b_out):
                for c in range(Q):
                    for r in range(2):
                        sp.wait_ge(stored[c][r], NORM.rounds // 2 * 16)

        @block.tensor
        def _(pe):
            def biases(parity):
                for c in range(Q):
                    mm = nc.tensor.matmul(BIA[parity][c * QUARTER:c * QUARTER + HEADS, :], W["Wb"][:, :], z[:, parity, c, :],
                                          start=True, stop=True)
                return mm

            def slot(i, r):
                s = Slot(NORM, pe, pe_done, i, r)
                at, on = s.at, s.on
                pe.wait_ge(act_done, at("mC1", "sq1", 1))
                pe.wait_ge(dve_done, at("mC1", "z1", 1))
                if s.runs("mC1"):
                    pe.wait_ge(x_in[1][s.side("mC1")], s.moved("mC1", 16))
                if on("mC1"):
                    nc.tensor.matmul(CEN[1], cen, xin[:, s.parity, 1, :], start=True, stop=True).then_inc(pe_done, 1)
                pe.wait_ge(act_done, at("mC3", "sq3", 1))
                pe.wait_ge(dve_done, at("mC3", "z3", 1))
                if s.runs("mC3"):
                    pe.wait_ge(x_in[3][s.side("mC3")], s.moved("mC3", 16))
                if on("mC3"):
                    nc.tensor.matmul(CEN[3], cen, xin[:, s.parity, 3, :], start=True, stop=True).then_inc(pe_done, 1)
                pe.wait_ge(act_done, at("mM2", "ln0"))
                if on("mM2"):
                    nc.tensor.matmul(VAR[0], const["mean"][:, :], sq[:, 0, :], start=True, stop=True).then_inc(pe_done, 1)
                pe.wait_ge(act_done, at("mM1", "sq1"))
                if on("mM1"):
                    nc.tensor.matmul(VAR[1], const["mean"][:, :], sq[:, 1, :], start=True, stop=True).then_inc(pe_done, 1)
                if on("mB"):
                    biases(s.parity).then_inc(pe_done, 1)
                pe.wait_ge(dve_done, at("mC0", "z0", 1))
                if s.runs("mC0"):
                    pe.wait_ge(x_in[0][s.side("mC0")], s.moved("mC0", 16))
                if on("mC0"):
                    nc.tensor.matmul(CEN[0], cen, xin[:, s.parity, 0, :], start=True, stop=True).then_inc(pe_done, 1)
                pe.wait_ge(act_done, at("mM3", "sq3"))
                if on("mM3"):
                    nc.tensor.matmul(VAR[1], const["mean"][:, :], sq[:, 1, :], start=True, stop=True).then_inc(pe_done, 1)
                pe.wait_ge(dve_done, at("mC2", "z2", 1))
                if s.runs("mC2"):
                    pe.wait_ge(x_in[2][s.side("mC2")], s.moved("mC2", 16))
                if on("mC2"):
                    nc.tensor.matmul(CEN[2], cen, xin[:, s.parity, 2, :], start=True, stop=True).then_inc(pe_done, 1)
                pe.wait_ge(act_done, at("mM0", "sq0"))
                if on("mM0"):
                    nc.tensor.matmul(VAR[0], const["mean"][:, :], sq[:, 0, :], start=True, stop=True).then_inc(pe_done, 1)
            pe.sem_inc(pe_done, 1)
            NORM.run(pe, slot)

        @block.scalar
        def _(act):
            act.wait_ge(eps_set, 1)
            load_log_exp(nc, act)

            def slot(i, r):
                s = Slot(NORM, act, act_done, i, r)
                at, on = s.at, s.on
                act.wait_ge(pe_done, at("ln0", "mM0"))
                act.wait_ge(act_done, at("ln0", "rs2", 1))
                if on("ln0"):
                    nc.scalar.activation(lnv[:, 0, :], VAR[0], ACT.Ln, bias=eps[:, 0:1]).then_inc(act_done, 1)
                act.wait_ge(pe_done, at("sq1", "mC1"))
                if on("sq1"):
                    nc.scalar.activation(sq[:, 1, :], CEN[1], ACT.Square, bias=cenb).then_inc(act_done, 1)
                act.wait_ge(act_done, at("rs0", "ln0"))
                act.wait_ge(dve_done, at("rs0", "z2", 1))
                if on("rs0"):
                    nc.scalar.activation(rstd[:, 0, :], lnv[:, 0, :], ACT.Exp, scale=-0.5).then_inc(act_done, 1)
                act.wait_ge(pe_done, at("ln2", "mM2"))
                act.wait_ge(act_done, at("ln2", "rs0"))
                if on("ln2"):
                    nc.scalar.activation(lnv[:, 0, :], VAR[0], ACT.Ln, bias=eps[:, 0:1]).then_inc(act_done, 1)
                act.wait_ge(act_done, at("rs2", "ln2"))
                act.wait_ge(dve_done, at("rs2", "z0"))
                if on("rs2"):
                    nc.scalar.activation(rstd[:, 0, :], lnv[:, 0, :], ACT.Exp, scale=-0.5).then_inc(act_done, 1)
                act.wait_ge(pe_done, at("ln1", "mM1"))
                if on("ln1"):
                    nc.scalar.activation(lnv[:, 1, :], VAR[1], ACT.Ln, bias=eps[:, 0:1]).then_inc(act_done, 1)
                if on("sq3"):
                    nc.scalar.activation(sq[:, 1, :], CEN[3], ACT.Square, bias=cenb).then_inc(act_done, 1)
                act.wait_ge(act_done, at("rs1", "ln1"))
                if on("rs1"):
                    nc.scalar.activation(rstd[:, 1, :], lnv[:, 1, :], ACT.Exp, scale=-0.5).then_inc(act_done, 1)
                act.wait_ge(pe_done, at("sq0", "mC0"))
                if on("sq0"):
                    nc.scalar.activation(sq[:, 0, :], CEN[0], ACT.Square, bias=cenb).then_inc(act_done, 1)
                act.wait_ge(pe_done, at("ln3", "mM3"))
                act.wait_ge(act_done, at("ln3", "rs1"))
                if on("ln3"):
                    nc.scalar.activation(lnv[:, 1, :], VAR[1], ACT.Ln, bias=eps[:, 0:1]).then_inc(act_done, 1)
                act.wait_ge(act_done, at("rs3", "ln3"))
                act.wait_ge(dve_done, at("rs3", "z1"))
                if on("rs3"):
                    nc.scalar.activation(rstd[:, 1, :], lnv[:, 1, :], ACT.Exp, scale=-0.5).then_inc(act_done, 1)
                act.wait_ge(pe_done, at("sq2", "mM0"))
                if on("sq2"):
                    nc.scalar.activation(sq[:, 0, :], CEN[2], ACT.Square, bias=cenb).then_inc(act_done, 1)
            act.sem_inc(act_done, 1)
            NORM.run(act, slot)

        @block.vector
        def _(dve):
            nc.vector.memset(eps[:, :], EPS).then_inc(eps_set, 1)

            def taken(c, parity):
                at = slice(c * QUARTER, c * QUARTER + HEADS)
                return nc.vector.tensor_scalar(bsb[at, parity, :], BIA[parity][at, :], -1.0, W["b_off"][at, 0:1],
                                               ALU.mult, ALU.add)

            def slot(i, r):
                s = Slot(NORM, dve, dve_done, i, r)
                at, on = s.at, s.on
                dve.wait_ge(pe_done, at("bc1", "mB"))
                if s.runs("bc1", 2):
                    dve.wait_ge(b_out[1][s.side("bc1", 2)], s.moved("bc1", 16, 2))
                if on("bc1"):
                    taken(1, s.parity).then_inc(dve_done, 1)
                if s.runs("bc0", 2):
                    dve.wait_ge(b_out[0][s.side("bc0", 2)], s.moved("bc0", 16, 2))
                if on("bc0"):
                    taken(0, s.parity).then_inc(dve_done, 1)
                dve.wait_ge(pe_done, at("z0", "mC0"))
                dve.wait_ge(act_done, at("z0", "rs0"))
                if s.runs("z0", 2):
                    dve.wait_ge(z_out[0][s.side("z0", 2)], s.moved("z0", 16, 2))
                if on("z0"):
                    nc.vector.scalar_tensor_tensor(z[:, s.parity, 0, :], CEN[0], cenb, rstd[:, 0, :], ALU.add,
                                                   ALU.mult).then_inc(dve_done, 1)
                dve.wait_ge(pe_done, at("bc2", "mB"))
                if s.runs("bc2", 2):
                    dve.wait_ge(b_out[2][s.side("bc2", 2)], s.moved("bc2", 16, 2))
                if on("bc2"):
                    taken(2, s.parity).then_inc(dve_done, 1)
                dve.wait_ge(act_done, at("z2", "rs2"))
                if s.runs("z2", 2):
                    dve.wait_ge(z_out[2][s.side("z2", 2)], s.moved("z2", 16, 2))
                if on("z2"):
                    nc.vector.scalar_tensor_tensor(z[:, s.parity, 2, :], CEN[2], cenb, rstd[:, 0, :], ALU.add,
                                                   ALU.mult).then_inc(dve_done, 1)
                dve.wait_ge(act_done, at("z1", "rs1"))
                if s.runs("z1", 2):
                    dve.wait_ge(z_out[1][s.side("z1", 2)], s.moved("z1", 16, 2))
                if on("z1"):
                    nc.vector.scalar_tensor_tensor(z[:, s.parity, 1, :], CEN[1], cenb, rstd[:, 1, :], ALU.add,
                                                   ALU.mult).then_inc(dve_done, 1)
                dve.wait_ge(act_done, at("z3", "rs3"))
                if s.runs("z3", 2):
                    dve.wait_ge(z_out[3][s.side("z3", 2)], s.moved("z3", 16, 2))
                if on("z3"):
                    nc.vector.scalar_tensor_tensor(z[:, s.parity, 3, :], CEN[3], cenb, rstd[:, 1, :], ALU.add,
                                                   ALU.mult).then_inc(dve_done, 1)
                if s.runs("bc3", 2):
                    dve.wait_ge(b_out[3][s.side("bc3", 2)], s.moved("bc3", 16, 2))
                if on("bc3"):
                    taken(3, s.parity).then_inc(dve_done, 1)
            dve.sem_inc(dve_done, 1)
            NORM.run(dve, slot)


ATTENTION_STEPS = {
    "pe": [("QK2", 2), ("mKQ", 3), ("QK3", 2), ("mV", 2), ("T3", 1), ("mG", 3), ("T2", 1), ("QK0", 3), ("PV3", 1),
        ("PV2", 1), ("PV0", 1), ("T1", 2), ("PV1", 1), ("QK1", 3), ("T0", 2), ("mO", 1)],
    "act": [("tg", 2), ("ex01", 2), ("cp1", 1), ("ex10", 2), ("ex11", 2), ("qT", 3), ("kT", 3), ("cp3", 1),
        ("cp2", 1), ("ex21", 2), ("ex30", 2), ("ex00", 3), ("ex31", 2), ("ex20", 2)],
    "pool": [("nm31", 1), ("km3", 2), ("km0", 3), ("km1", 3), ("nm11", 2), ("nm10", 2), ("km2", 3)],
    "dve": [("lo10", 2), ("rec2", 1), ("xo", 0), ("lo11", 2), ("nm20", 1), ("lo20", 2), ("nm30", 1), ("rec1", 2),
        ("nm21", 1), ("rec0", 2), ("cp0", 1), ("lo21", 2), ("v", 2), ("lo31", 2), ("nm00", 2), ("lo30", 2),
        ("lo00", 3), ("bn", 0), ("nm01", 2), ("lo01", 3), ("gated", 1), ("rec3", 2)],
    "sp": [("x", 0), ("z", 3), ("st", 0)],
}
ATTENTION = Schedule(N, -3, ATTENTION_STEPS)


def row_attention(nc, x_t, z_t, bias_d, x1_t, W, const, stats, ps):
    scale = HD ** -0.5
    with ExitStack() as ctx:
        sb = lambda n, s: ctx.enter_context(nc.sbuf_tensor("c_" + n, s, F32))
        new_sem = ctx.enter_context(phase_semaphores(nc))
        sem = lambda n: new_sem("c_" + n)
        bias = sb("bias", [P, HALF, HEADS, N])
        z, x = sb("z", [P, 2, N]), sb("x", [P, 2, N])
        qT, kT, km = sb("qT", [P, 2, N]), sb("kT", [P, 2, N]), sb("km", [P, 2, HEADS, N])
        tg, v = sb("tg", [P, 2, N]), sb("v", [P, 2, HALF, P])
        sc = sb("sc", [P, HEADS, HALF, N])
        pr = sb("pr", [P, 2, HEADS, HALF, N])
        pT = sb("pT", [P, 2, HEADS, HALF, N])
        low, tot, rec = [sb(n, [P, 2, HEADS, HALF]) for n in ("low", "tot", "rec")]
        gated, xo = sb("gated", [P, N]), sb("xo", [P, 2, N])
        z_in, x_in, x_out = [[sem(f"{n}{r}") for r in range(2)] for n in ("z_in", "x_in", "x_out")]
        bias_in, masks_zero = sem("bias_in"), sem("masks_zero")
        pe_done, act_done, pool_done, dve_done = sem("pe_done"), sem("act_done"), sem("pool_done"), sem("dve_done")
        pool_passed, dve_passed, sp_passed = sem("pool_passed"), sem("dve_passed"), sem("sp_passed")
        block = ctx.enter_context(nc.Block())
        SC = [ps[:, b, :].rearrange("p (c k) -> p c k", c=HALF) for b in range(2)]
        PT = [ps[:, 2 + b, :].rearrange("p (c k) -> p c k", c=HALF) for b in range(2)]
        PV = [ps[:, 4 + b, 0:N] for b in range(2)]
        PQ, PK, PG = ps[:, 6, 0:N], ps[:, 6, N:2 * N], ps[:, 6, 0:N]
        PWO, PVV = ps[:, 7, 0:N], ps[:, 7, N:2 * N]

        @block.sync
        def _(sp):
            for c in range(HALF):
                sp.dma_start(bias[:, c, :, :], bias_d[:, c * P * N:(c + 1) * P * N].rearrange("h (j k) -> j h k",
                        k=N)).then_inc(bias_in, 16)

            def slot(half, r):
                s = Slot(ATTENTION, sp, None, half, r)
                at = s.at
                sp.wait_ge(dve_done, at("x", "xo", 2))
                sp.sem_inc(sp_passed, 1)
                if s.runs("x"):
                    sp.dma_start(x[:, (r + ATTENTION.ahead["x"]) % 2, :],
                                 x_t[:, bass.ds(half * (2 * N) + (r + ATTENTION.ahead["x"]) * N, N)]).then_inc(x_in[(r + ATTENTION.ahead["x"]) % 2], 16)
                sp.wait_ge(pe_done, at("z", "mV", 2))
                sp.sem_inc(sp_passed, 1)
                if s.runs("z"):
                    sp.dma_start(z[:, (r + ATTENTION.ahead["z"]) % 2, :],
                                 z_t[:, bass.ds(half * (2 * N) + (r + ATTENTION.ahead["z"]) * N, N)]).then_inc(z_in[(r + ATTENTION.ahead["z"]) % 2], 16)
                sp.wait_ge(dve_done, at("st", "xo"))
                sp.sem_inc(sp_passed, 1)
                if s.runs("st"):
                    sp.dma_start(x1_t[:, bass.ds(half * (2 * N) + (r + ATTENTION.ahead["st"]) * N, N)],
                                 xo[:, (r + ATTENTION.ahead["st"]) % 2, :]).then_inc(x_out[(r + ATTENTION.ahead["st"]) % 2], 16)
            ATTENTION.run(sp, slot)
            for r in range(2):
                sp.wait_ge(x_out[r], 16 * N // 2)

        @block.tensor
        def _(pe):
            def transposes(bank, h, parity):
                for kc in range(HALF):
                    for jc in range(HALF):
                        mm = nc.tensor.transpose(bank[:, kc, jc * P:(jc + 1) * P], pr[:, parity, h, jc, kc * P:(kc + 1) * P],
                                                 const["ident"][:, :])
                return mm

            def values(h, parity):
                for kc in range(HALF):
                    mm = nc.tensor.matmul(PV[parity][h * HD:(h + 1) * HD, :], v[:, parity, kc, h * HD:(h + 1) * HD],
                                          pT[:, parity, h, kc, :], start=kc == 0, stop=kc == HALF - 1)
                return mm

            def slot(half, r):
                s = Slot(ATTENTION, pe, pe_done, half, r)
                at, on = s.at, s.on
                pe.wait_ge(act_done, at("QK2", "qT"))
                pe.wait_ge(pool_done, at("QK2", "km2"))
                pe.wait_ge(dve_done, at("QK2", "lo01"))
                if on("QK2"):
                    nc.tensor.matmul(SC[0][:, 0, :], qT[:, s.parity, 0:P], km[:, s.parity, 2, :], start=True, stop=True)
                    nc.tensor.matmul(SC[0][:, 1, :], qT[:, s.parity, P:2 * P], km[:, s.parity, 2, :], start=True,
                                     stop=True).then_inc(pe_done, 1)
                pe.wait_ge(act_done, at("mKQ", "tg", 1))
                if s.runs("mKQ"):
                    pe.wait_ge(z_in[s.side("mKQ")], s.moved("mKQ", 16))
                if on("mKQ"):
                    nc.tensor.matmul(PK, W["Wk"][:, :], z[:, s.parity, :], start=True, stop=True)
                    nc.tensor.matmul(PQ, W["Wq"][:, :], z[:, s.parity, :], start=True, stop=True).then_inc(pe_done, 1)
                pe.wait_ge(pool_done, at("QK3", "km3"))
                pe.wait_ge(dve_done, at("QK3", "lo11"))
                if on("QK3"):
                    nc.tensor.matmul(SC[1][:, 0, :], qT[:, s.parity, 0:P], km[:, s.parity, 3, :], start=True, stop=True)
                    nc.tensor.matmul(SC[1][:, 1, :], qT[:, s.parity, P:2 * P], km[:, s.parity, 3, :], start=True,
                                     stop=True).then_inc(pe_done, 1)
                if s.runs("mV"):
                    pe.wait_ge(z_in[s.side("mV")], s.moved("mV", 16))
                if on("mV"):
                    nc.tensor.matmul(PVV[:, 0:P], z[:, s.parity, 0:P], W["Wv"][:, :], start=True, stop=True)
                    nc.tensor.matmul(PVV[:, P:2 * P], z[:, s.parity, P:2 * P], W["Wv"][:, :], start=True,
                                     stop=True).then_inc(pe_done, 1)
                pe.wait_ge(dve_done, at("T3", "nm30"))
                pe.wait_ge(act_done, at("T3", "cp1"))
                if on("T3"):
                    transposes(PT[1], 3, s.parity).then_inc(pe_done, 1)
                pe.wait_ge(act_done, at("mG", "kT"))
                if s.runs("mG"):
                    pe.wait_ge(z_in[s.side("mG")], s.moved("mG", 16))
                if on("mG"):
                    nc.tensor.matmul(PG, W["Wg"][:, :], z[:, s.parity, :], start=True, stop=True).then_inc(pe_done, 1)
                pe.wait_ge(dve_done, at("T2", "cp0"))
                if on("T2"):
                    transposes(PT[0], 2, s.parity).then_inc(pe_done, 1)
                pe.wait_ge(pool_done, at("QK0", "km0"))
                pe.wait_ge(dve_done, at("QK0", "lo21", 1))
                if on("QK0"):
                    nc.tensor.matmul(SC[0][:, 0, :], qT[:, s.parity, 0:P], km[:, s.parity, 0, :], start=True, stop=True)
                    nc.tensor.matmul(SC[0][:, 1, :], qT[:, s.parity, P:2 * P], km[:, s.parity, 0, :], start=True,
                                     stop=True).then_inc(pe_done, 1)
                pe.wait_ge(act_done, at("PV3", "cp3"))
                if on("PV3"):
                    values(3, s.parity).then_inc(pe_done, 1)
                pe.wait_ge(act_done, at("PV2", "cp2"))
                if on("PV2"):
                    values(2, s.parity).then_inc(pe_done, 1)
                if on("PV0"):
                    values(0, s.parity).then_inc(pe_done, 1)
                pe.wait_ge(pool_done, at("T1", "nm10"))
                if on("T1"):
                    transposes(PT[1], 1, s.parity).then_inc(pe_done, 1)
                if on("PV1"):
                    values(1, s.parity).then_inc(pe_done, 1)
                pe.wait_ge(dve_done, at("QK1", "lo30", 1))
                if on("QK1"):
                    nc.tensor.matmul(SC[1][:, 0, :], qT[:, s.parity, 0:P], km[:, s.parity, 1, :], start=True, stop=True)
                    nc.tensor.matmul(SC[1][:, 1, :], qT[:, s.parity, P:2 * P], km[:, s.parity, 1, :], start=True,
                                     stop=True).then_inc(pe_done, 1)
                pe.wait_ge(dve_done, at("T0", "nm01"))
                if on("T0"):
                    transposes(PT[0], 0, s.parity).then_inc(pe_done, 1)
                pe.wait_ge(dve_done, at("mO", "gated"))
                if on("mO"):
                    nc.tensor.matmul(PWO, W["Wo"][:, :], gated[:, :], start=True, stop=True).then_inc(pe_done, 1)
            pe.sem_inc(pe_done, 1)
            ATTENTION.run(pe, slot)

        @block.scalar
        def _(act):
            def exponential(h, jc, parity):
                return nc.scalar.activation(pr[:, parity, h, jc, :], sc[:, h, jc, :], ACT.Exp, bias=low[:, parity, h, jc:jc + 1],
                                            scale=-1.0, accum_out=tot[:, parity, h, jc:jc + 1])

            def slot(half, r):
                s = Slot(ATTENTION, act, act_done, half, r)
                at, on = s.at, s.on
                act.wait_ge(pe_done, at("tg", "mG"))
                act.wait_ge(dve_done, at("tg", "gated", 2))
                if on("tg"):
                    nc.scalar.activation(tg[:, s.parity, :], PG, ACT.Tanh, bias=W["g_off"][:, 0:1],
                                         scale=0.5).then_inc(act_done, 1)
                if on("ex01"):
                    exponential(0, 1, s.parity).then_inc(act_done, 1)
                act.wait_ge(pe_done, at("cp1", "T1"))
                if on("cp1"):
                    nc.scalar.activation(pT[:, s.parity, 1, :, :], PT[1], ACT.Identity).then_inc(act_done, 1)
                act.wait_ge(dve_done, at("ex10", "lo10"))
                act.wait_ge(pool_done, at("ex10", "nm10", 2))
                if on("ex10"):
                    exponential(1, 0, s.parity).then_inc(act_done, 1)
                act.wait_ge(dve_done, at("ex11", "lo11"))
                if on("ex11"):
                    exponential(1, 1, s.parity).then_inc(act_done, 1)
                act.wait_ge(pe_done, at("qT", "mKQ"))
                if on("qT"):
                    nc.scalar.activation(qT[:, s.parity, :], PQ, ACT.Identity, bias=W["q_off"][:, 0:1],
                                         scale=-scale).then_inc(act_done, 1)
                act.wait_ge(pool_done, at("kT", "km3", 2))
                if on("kT"):
                    nc.scalar.activation(kT[:, s.parity, :], PK, ACT.Identity, bias=W["k_off"][:, 0:1]).then_inc(act_done, 1)
                act.wait_ge(pe_done, at("cp3", "T3"))
                if on("cp3"):
                    nc.scalar.activation(pT[:, s.parity, 3, :, :], PT[1], ACT.Identity).then_inc(act_done, 1)
                act.wait_ge(pe_done, at("cp2", "T2"))
                if on("cp2"):
                    nc.scalar.activation(pT[:, s.parity, 2, :, :], PT[0], ACT.Identity).then_inc(act_done, 1)
                act.wait_ge(dve_done, at("ex21", "lo21"))
                if on("ex21"):
                    exponential(2, 1, s.parity).then_inc(act_done, 1)
                act.wait_ge(dve_done, at("ex30", "lo30"))
                if on("ex30"):
                    exponential(3, 0, s.parity).then_inc(act_done, 1)
                act.wait_ge(dve_done, at("ex00", "lo00"))
                if on("ex00"):
                    exponential(0, 0, s.parity).then_inc(act_done, 1)
                if on("ex31"):
                    exponential(3, 1, s.parity).then_inc(act_done, 1)
                if on("ex20"):
                    exponential(2, 0, s.parity).then_inc(act_done, 1)
            act.sem_inc(act_done, 1)
            ATTENTION.run(act, slot)

        @block.gpsimd
        def _(pool):
            nc.gpsimd.memset(km[:, :, :, :], 0.0).then_inc(masks_zero, 1)
            pool.wait_ge(masks_zero, 1)

            def slot(half, r):
                s = Slot(ATTENTION, pool, pool_done, half, r)
                at, on = s.at, s.on
                pool.wait_ge(pool_done, at("nm31", "nm31") - 1)
                pool.wait_ge(act_done, at("nm31", "ex31"))
                pool.wait_ge(dve_done, at("nm31", "rec3"))
                pool.sem_inc(pool_passed, 1)
                if on("nm31"):
                    nc.gpsimd.tensor_scalar(pr[:, s.parity, 3, 1, :], pr[:, s.parity, 3, 1, :],
                                            rec[:, s.parity, 3, 1:2], 0.0, ALU.mult, ALU.add).then_inc(pool_done, 1)
                pool.wait_ge(pool_done, at("km3", "km3") - 1)
                pool.wait_ge(pe_done, at("km3", "QK3", 2))
                pool.sem_inc(pool_passed, 1)
                if on("km3"):
                    nc.gpsimd.tensor_scalar(km[3 * HD:4 * HD, s.parity, 3, :], kT[3 * HD:4 * HD, s.parity, :], 1.0, 0.0, ALU.mult,
                                            ALU.add).then_inc(pool_done, 1)
                pool.wait_ge(pool_done, at("km0", "km0") - 1)
                pool.wait_ge(act_done, at("km0", "kT"))
                pool.wait_ge(pe_done, at("km0", "QK0", 2))
                pool.sem_inc(pool_passed, 1)
                if on("km0"):
                    nc.gpsimd.tensor_scalar(km[0:HD, s.parity, 0, :], kT[0:HD, s.parity, :], 1.0, 0.0, ALU.mult,
                                            ALU.add).then_inc(pool_done, 1)
                pool.wait_ge(pool_done, at("km1", "km1") - 1)
                pool.wait_ge(pe_done, at("km1", "QK1", 2))
                pool.sem_inc(pool_passed, 1)
                if on("km1"):
                    nc.gpsimd.tensor_scalar(km[HD:2 * HD, s.parity, 1, :], kT[HD:2 * HD, s.parity, :], 1.0, 0.0, ALU.mult,
                                            ALU.add).then_inc(pool_done, 1)
                pool.wait_ge(pool_done, at("nm11", "nm11") - 1)
                pool.wait_ge(dve_done, at("nm11", "rec1"))
                pool.sem_inc(pool_passed, 1)
                if on("nm11"):
                    nc.gpsimd.tensor_scalar(pr[:, s.parity, 1, 1, :], pr[:, s.parity, 1, 1, :],
                                            rec[:, s.parity, 1, 1:2], 0.0, ALU.mult, ALU.add).then_inc(pool_done, 1)
                pool.wait_ge(pool_done, at("nm10", "nm10") - 1)
                pool.sem_inc(pool_passed, 1)
                if on("nm10"):
                    nc.gpsimd.tensor_scalar(pr[:, s.parity, 1, 0, :], pr[:, s.parity, 1, 0, :],
                                            rec[:, s.parity, 1, 0:1], 0.0, ALU.mult, ALU.add).then_inc(pool_done, 1)
                pool.wait_ge(pool_done, at("km2", "km2") - 1)
                pool.wait_ge(pe_done, at("km2", "QK2", 2))
                pool.sem_inc(pool_passed, 1)
                if on("km2"):
                    nc.gpsimd.tensor_scalar(km[2 * HD:3 * HD, s.parity, 2, :], kT[2 * HD:3 * HD, s.parity, :], 1.0, 0.0, ALU.mult,
                                            ALU.add).then_inc(pool_done, 1)
            pool.sem_inc(pool_done, 1)
            ATTENTION.run(pool, slot)

        @block.vector
        def _(dve):
            dve.wait_ge(bias_in, 16 * HALF)

            def lowest(scores, h, jc, parity):
                return nc.vector.tensor_tensor_reduce(out=sc[:, h, jc, :], in0=scores[:, jc, :], in1=bias[:, jc, h, :], scale=1.0,
                                                      scalar=3.0e38, op0=ALU.add, op1=ALU.min,
                                                      accum_out=low[:, parity, h, jc:jc + 1])

            def slot(half, r):
                s = Slot(ATTENTION, dve, dve_done, half, r)
                at, on = s.at, s.on
                dve.wait_ge(pe_done, at("lo10", "QK1"))
                dve.wait_ge(act_done, at("lo10", "ex10", 1))
                dve.sem_inc(dve_passed, 1)
                if on("lo10"):
                    lowest(SC[1], 1, 0, s.parity).then_inc(dve_done, 1)
                dve.wait_ge(act_done, at("rec2", "ex20"))
                if on("rec2"):
                    nc.vector.reciprocal(rec[:, s.parity, 2, :], tot[:, s.parity, 2, :]).then_inc(dve_done, 1)
                dve.wait_ge(pe_done, at("xo", "mO"))
                if s.runs("xo"):
                    dve.wait_ge(x_in[s.side("xo")], s.moved("xo", 16))
                if s.runs("xo", 2):
                    dve.wait_ge(x_out[s.side("xo", 2)], s.moved("xo", 16, 2))
                if on("xo"):
                    nc.vector.scalar_tensor_tensor(xo[:, s.parity, :], PWO, W["bo"][:, 0:1], x[:, s.parity, :], ALU.add,
                                                   ALU.add).then_inc(dve_done, 1)
                if on("lo11"):
                    lowest(SC[1], 1, 1, s.parity).then_inc(dve_done, 1)
                dve.wait_ge(dve_done, at("nm20", "rec2"))
                if on("nm20"):
                    nc.vector.tensor_scalar(pr[:, s.parity, 2, 0, :], pr[:, s.parity, 2, 0, :],
                                            rec[:, s.parity, 2, 0:1], None, ALU.mult).then_inc(dve_done, 1)
                dve.wait_ge(pe_done, at("lo20", "QK2"))
                dve.sem_inc(dve_passed, 1)
                if on("lo20"):
                    lowest(SC[0], 2, 0, s.parity).then_inc(dve_done, 1)
                if on("nm30"):
                    nc.vector.tensor_scalar(pr[:, s.parity, 3, 0, :], pr[:, s.parity, 3, 0, :],
                                            rec[:, s.parity, 3, 0:1], None, ALU.mult).then_inc(dve_done, 1)
                dve.wait_ge(act_done, at("rec1", "ex11"))
                dve.wait_ge(pool_done, at("rec1", "nm10", 2))
                if on("rec1"):
                    nc.vector.reciprocal(rec[:, s.parity, 1, :], tot[:, s.parity, 1, :]).then_inc(dve_done, 1)
                if on("nm21"):
                    nc.vector.tensor_scalar(pr[:, s.parity, 2, 1, :], pr[:, s.parity, 2, 1, :],
                                            rec[:, s.parity, 2, 1:2], None, ALU.mult).then_inc(dve_done, 1)
                if on("rec0"):
                    nc.vector.reciprocal(rec[:, s.parity, 0, :], tot[:, s.parity, 0, :]).then_inc(dve_done, 1)
                if on("cp0"):
                    nc.vector.tensor_copy(pT[:, s.parity, 0, :, :], PT[0]).then_inc(dve_done, 1)
                if on("lo21"):
                    lowest(SC[0], 2, 1, s.parity).then_inc(dve_done, 1)
                dve.wait_ge(pe_done, at("v", "mV"))
                if on("v"):
                    nc.vector.tensor_tensor(v[:, s.parity, :, :].rearrange("p c d -> p (c d)"), PVV,
                                             W["v_off"][:, :, :].rearrange("p c d -> p (c d)"), ALU.add).then_inc(dve_done, 1)
                if on("lo31"):
                    lowest(SC[1], 3, 1, s.parity).then_inc(dve_done, 1)
                dve.wait_ge(dve_done, at("nm00", "rec0"))
                if on("nm00"):
                    nc.vector.tensor_scalar(pr[:, s.parity, 0, 0, :], pr[:, s.parity, 0, 0, :],
                                            rec[:, s.parity, 0, 0:1], None, ALU.mult).then_inc(dve_done, 1)
                if on("lo30"):
                    lowest(SC[1], 3, 0, s.parity).then_inc(dve_done, 1)
                dve.wait_ge(pe_done, at("lo00", "QK0"))
                dve.sem_inc(dve_passed, 1)
                if on("lo00"):
                    lowest(SC[0], 0, 0, s.parity).then_inc(dve_done, 1)
                if on("bn"):
                    nc.vector.bn_stats(stats[:, bass.ds(half * 12 + (r + ATTENTION.ahead["bn"]) * 6, 6)],
                                       xo[:, s.parity, :]).then_inc(dve_done, 1)
                if on("nm01"):
                    nc.vector.tensor_scalar(pr[:, s.parity, 0, 1, :], pr[:, s.parity, 0, 1, :],
                                            rec[:, s.parity, 0, 1:2], None, ALU.mult).then_inc(dve_done, 1)
                if on("lo01"):
                    lowest(SC[0], 0, 1, s.parity).then_inc(dve_done, 1)
                dve.wait_ge(pe_done, at("gated", "PV1"))
                if on("gated"):
                    nc.vector.scalar_tensor_tensor(gated[:, :], tg[:, s.parity, :], 1.0, PV[s.parity], ALU.add,
                                                   ALU.mult).then_inc(dve_done, 1)
                dve.wait_ge(act_done, at("rec3", "ex31"))
                dve.wait_ge(pool_done, at("rec3", "nm31", 2))
                if on("rec3"):
                    nc.vector.reciprocal(rec[:, s.parity, 3, :], tot[:, s.parity, 3, :]).then_inc(dve_done, 1)
            dve.sem_inc(dve_done, 1)
            ATTENTION.run(dve, slot)


TAPS = 9
PAD = TAPS // 2


def row_scan(nc, d, x1_t, x2_t, affine, stats, ps):
    with ExitStack() as ctx:
        sb = lambda n, s: ctx.enter_context(nc.sbuf_tensor("d_" + n, s, F32))
        new_sem = ctx.enter_context(phase_semaphores(nc))
        sem = lambda n: new_sem("d_" + n)
        taps = sb("taps", [P, TAPS, P])
        x1, g, x2 = sb("x1", [P, 2, N]), sb("g", [P, 2, N]), sb("x2", [P, 2, N])
        new = sb("new", [P, 2, N + 2 * PAD])
        taps_in, pads_zero = sem("taps_in"), sem("pads_zero")
        x_in, x_out = [sem(f"x_in{r}") for r in range(2)], [sem(f"x_out{r}") for r in range(2)]
        g_done, left_conv, right_conv, left_new, right_new, x2_done, x2_counted = (
            sem("g_done"), sem("left_conv"), sem("right_conv"), sem("left_new"), sem("right_new"),
            sem("x2_done"), sem("x2_counted"))
        pool_passed = sem("pool_passed")
        block = ctx.enter_context(nc.Block())
        LEFT = [ps[:, r, 0:P] for r in range(2)]
        RIGHT = [ps[:, 2 + r, 0:P] for r in range(2)]

        def nth(half, r, c=0):
            return half * 2 + (r + c)

        def rows(eng, row):
            for R in range(4):
                row(R // 2, R % 2, R)
            with eng.Fori(2, N // 2 - 1) as half:
                for r in range(2):
                    row(half, r, None)
            for R in range(N - 2, N):
                row(R // 2, R % 2, R)

        @block.sync
        def _(sp):
            sp.dma_start(taps[:, :, :], d["L1_conv_W"]).then_inc(taps_in, 16)
            for r in range(2):
                sp.dma_start(x1[:, r, :], x1_t[:, r * N:(r + 1) * N]).then_inc(x_in[r], 16)

            def row(half, r, R):
                wait_count(sp, x2_done, nth(half, r, 1))
                sp.dma_start(x2_t[:, bass.ds(half * (2 * N) + r * N, N)], x2[:, r, :]).then_inc(x_out[r], 16)
                if R is None or R + 2 < N:
                    sp.dma_start(x1[:, r, :], x1_t[:, bass.ds(half * (2 * N) + (r + 2) * N, N)]).then_inc(x_in[r], 16)
            rows(sp, row)
            for r in range(2):
                sp.wait_ge(x_out[r], 16 * N // 2)

        @block.scalar
        def _(act):
            act.wait_ge(pads_zero, 1)

            def row(half, r, R):
                wait_count(act, x_in[r], half * 16 + 16)
                wait_count(act, right_new, nth(half, r, -2))
                if R == 0:
                    nc.scalar.activation(g[:, 0, :], x1[:, 0, :], ACT.Identity, bias=affine[:, 1:2],
                                         scale=affine[:, 0:1]).then_inc(g_done, 1)
                    act.wait_ge(g_done, 1)
                    nc.scalar.activation(new[:, 0, PAD:PAD + N], g[:, 0, :], ACT.Identity).then_inc(g_done, 1)
                    return
                nc.scalar.activation(g[:, r, :], x1[:, r, :], ACT.Identity, bias=affine[:, 1:2],
                                     scale=affine[:, 0:1]).then_inc(g_done, 1)
            rows(act, row)

        @block.tensor
        def _(pe):
            pe.wait_ge(taps_in, 16)

            def row(half, r, R):
                if R == 0:
                    return
                last = new[:, 1 - r, :]

                def tap(to, k, at, **flags):
                    return nc.tensor.matmul(to, taps[:, k, :], last[:, at + k:at + k + P], **flags)

                if R == 1:
                    pe.wait_ge(g_done, 2)
                wait_count(pe, left_new, nth(half, r, -1))
                for k in range(PAD + 1):
                    tap(LEFT[r], k, 0, start=k == 0, stop=False)
                wait_count(pe, right_new, nth(half, r, -1))
                for k in range(PAD + 1, TAPS):
                    mm = tap(LEFT[r], k, 0, start=False, stop=k == TAPS - 1)
                mm.then_inc(left_conv, 1)
                for k in range(TAPS):
                    mm = tap(RIGHT[r], k, P, start=k == 0, stop=k == TAPS - 1)
                mm.then_inc(right_conv, 1)
            rows(pe, row)

        @block.vector
        def _(dve):
            nc.vector.memset(new[:, :, :], 0.0).then_inc(pads_zero, 1)

            def row(half, r, R):
                if R == 0:
                    return
                wait_count(dve, g_done, nth(half, r, 2))
                wait_count(dve, x2_done, nth(half, r, -1))
                wait_count(dve, left_conv, nth(half, r))
                nc.vector.scalar_tensor_tensor(new[:, r, PAD:PAD + P], LEFT[r], 0.0, g[:, r, 0:P],
                                               ALU.max, ALU.add).then_inc(left_new, 1)
                wait_count(dve, x2_done, nth(half, r))
                nc.vector.bn_stats(stats[:, bass.ds(half * 12 + (r - 1) * 6, 6)], x2[:, 1 - r, :]).then_inc(x2_counted, 1)
                wait_count(dve, right_conv, nth(half, r))
                nc.vector.scalar_tensor_tensor(new[:, r, PAD + P:PAD + N], RIGHT[r], 0.0, g[:, r, P:N],
                                               ALU.max, ALU.add).then_inc(right_new, 1)
            rows(dve, row)
            dve.wait_ge(x2_done, N)
            nc.vector.bn_stats(stats[:, (N - 1) * 6:N * 6], x2[:, 1, :]).then_inc(x2_counted, 1)

        @block.gpsimd
        def _(pool):
            def row(half, r, R):
                if R == 0:
                    pool.wait_ge(g_done, 2)
                wait_count(pool, right_new, nth(half, r))
                wait_count(pool, x_in[r], half * 16 + 16)
                wait_count(pool, x_out[r], half * 16)
                wait_counts(pool, pool_passed, (x2_counted, nth(half, r, -1)))
                nc.gpsimd.tensor_tensor(x2[:, r, :], x1[:, r, :], new[:, r, PAD:PAD + N], ALU.add).then_inc(x2_done, 1)
            rows(pool, row)


HC, HW = 8, 16
W4 = ("Wa", "Wb", "Ga", "Gb")
B4 = ("ba", "bb", "bga", "bgb")


def triangle_weights(nc, d, W, ps):
    with ExitStack() as ctx:
        sb = lambda n, s, t=F32: ctx.enter_context(nc.sbuf_tensor("e_raw_" + n, s, t))
        raw4, rawg, rawo = sb("raw4", [P, 4, P]), sb("rawg", [P, P]), sb("rawo", [P, P])
        cols = {n: sb(n, [P, 1]) for n in ("ln_g", "ln_b", "lnh_g", "lnh_b", "bg", "bo")}
        row4, beta_rep = sb("row4", [P, 4, P]), sb("beta_rep", [P, P])
        new_sem = ctx.enter_context(phase_semaphores(nc))
        sem = lambda n: new_sem("e_w_" + n)
        loaded, beta_ready, offsets_done, chain = sem("loaded"), sem("beta_ready"), sem("offsets_done"), sem("chain")
        block = ctx.enter_context(nc.Block())
        LOADS = 4 + 4 + 2 + len(cols)

        @block.sync
        def _(sp):
            for n in range(4):
                sp.dma_start(raw4[:, n, :], d["L2_conv_" + W4[n]]).then_inc(loaded, 16)
                sp.dma_start(row4[:, n, :], d["L2_conv_" + B4[n]].rearrange("a b -> b a").broadcast_to([P,
                        P])).then_inc(loaded, 16)
            sp.dma_start(rawg[:, :], d["L2_conv_Wg"]).then_inc(loaded, 16)
            sp.dma_start(rawo[:, :], d["L2_conv_Wo"]).then_inc(loaded, 16)
            for n, t in cols.items():
                sp.dma_start(t[:, :], d["L2_conv_" + n]).then_inc(loaded, 16)
            sp.wait_ge(loaded, 16 * LOADS)

        @block.vector
        def _(dve):
            link = linker(dve, chain)
            dve.wait_ge(loaded, 16 * LOADS)
            link(nc.vector.memset(beta_rep[:, :], 1.0))
            nc.vector.tensor_scalar(beta_rep[:, :], beta_rep[:, :], cols["ln_b"][:, 0:1], None, ALU.mult).then_inc(beta_ready, 1)
            link(nc.vector.tensor_scalar(W["W4"][:, :], raw4[:, :, :].rearrange("p a b -> p (a b)"), cols["ln_g"][:,
                    0:1], None, ALU.mult))
            link(nc.vector.tensor_scalar(W["Wg"][:, :], rawg[:, :], cols["ln_g"][:, 0:1], None, ALU.mult))
            link(nc.vector.tensor_scalar(W["Wo"][:, :], rawo[:, :], cols["lnh_g"][:, 0:1], None, ALU.mult))
            dve.wait_ge(offsets_done, 3)
            link(nc.vector.tensor_tensor(W["g_off"][:, :], ps[:, 1, 0:1], cols["bg"][:, :], ALU.add))
            link(nc.vector.tensor_tensor(W["o_off"][:, :], ps[:, 2, 0:1], cols["bo"][:, :], ALU.add))
            link(nc.vector.tensor_tensor(W["bias4"][:, :], ps[:, 0, :], row4[:, :, :].rearrange("p a b -> p (a b)"), ALU.add))

        @block.tensor
        def _(pe):
            pe.wait_ge(loaded, 16 * LOADS)
            pe.wait_ge(beta_ready, 1)
            nc.tensor.matmul(ps[:, 0, :], beta_rep[:, :], raw4[:, :, :].rearrange("p a b -> p (a b)"), start=True,
                             stop=True).then_inc(offsets_done, 1)
            nc.tensor.matmul(ps[:, 1, 0:1], rawg[:, :], cols["ln_b"][:, :], start=True, stop=True).then_inc(offsets_done, 1)
            nc.tensor.matmul(ps[:, 2, 0:1], rawo[:, :], cols["lnh_b"][:, :], start=True, stop=True).then_inc(offsets_done, 1)


PROJECTION_STEPS = {
    "pe": [("mA13", 0), ("mM3", 1), ("mA10", 0), ("mA12", 0), ("mA11", 0), ("mC1", 2), ("mC0", 2), ("mG1", 0),
        ("mA21", 0), ("mA20", 0), ("mG2", 0), ("mA22", 0), ("mA31", 0), ("mA23", 0), ("mA32", 0), ("mG3", 0),
        ("mA30", 0), ("mA33", 0), ("mA01", 1), ("mM0", 2), ("mA00", 1), ("mA03", 1), ("mM1", 2), ("mA02", 1),
        ("mC2", 2), ("mG0", 1), ("mC3", 2), ("mM2", 2)],
    "act": [("ln3", 1), ("rs3", 1), ("sg01", 0), ("sg00", 0), ("go0", 0), ("sg03", 0), ("sg02", 0), ("sg11", 0),
        ("sg10", 0), ("go1", 0), ("sq1", 2), ("sg13", 0), ("sg12", 0), ("go2", 0), ("sg20", 0), ("sg21", 0),
        ("sg22", 0), ("sg23", 0), ("sg32", 0), ("go3", 0), ("sq0", 2), ("sg30", 0), ("sg31", 0), ("sg33", 0),
        ("ln0", 2), ("rs0", 2), ("ln1", 2), ("rs1", 2), ("sq2", 2), ("sq3", 2), ("ln2", 2), ("rs2", 2)],
    "pool": [("ml01", 0), ("ml03", 0), ("ml02", 0), ("ml11", 0), ("ml10", 0), ("ml13", 0), ("ml21", 0), ("ml20", 0),
        ("ml22", 0), ("ml23", 0), ("ml33", 0), ("ml31", 0)],
    "dve": [("ad00", 0), ("ad01", 0), ("z2", 1), ("z3", 1), ("ml00", 0), ("ad11", 0), ("ad10", 0), ("ad13", 0),
        ("ad12", 0), ("ad21", 0), ("ad20", 0), ("ml12", 0), ("ad22", 0), ("ad23", 0), ("ad32", 0), ("ad31", 0),
        ("ad30", 0), ("ad33", 0), ("ml32", 0), ("z0", 2), ("ad03", 1), ("ad02", 1), ("z1", 2), ("ml30", 0)],
    "sp": [("gs0", 0), ("gs2", 0), ("x3", 2), ("x0", 3), ("gs1", 0), ("x1", 3), ("as2", 0), ("x2", 3), ("as3", 0),
        ("as1", 0), ("as0", 0), ("gs3", 0)],
}
PROJECTION = Schedule(NCH // 4, -3, PROJECTION_STEPS)


def triangle_projections(nc, x2_t, ab_d, go_t, W, const, affine, ps):
    Q, TILES = 4, 4
    cen, cenb = affine[:, 2:2 + P], affine[:, 2 + P:3 + P]
    with ExitStack() as ctx:
        sb = lambda n, s: ctx.enter_context(nc.sbuf_tensor("e_" + n, s, F32))
        new_sem = ctx.enter_context(phase_semaphores(nc))
        sem = lambda n: new_sem("e_" + n)
        xin, z, go = sb("xin", [P, 2, Q, CH]), sb("z", [P, 2, Q, CH]), sb("go", [P, Q, CH])
        sq, lnv, rstd = sb("sq", [P, 2, CH]), sb("lnv", [P, 2, CH]), sb("rstd", [P, 2, CH])
        ab, sg = sb("ab", [P, TILES, CH]), sb("sg", [P, TILES, N])
        stage = sb("stage", [P, 2, HALF, 2 * HC, 8, HW])
        eps = sb("eps", [P, 1])
        x_in, go_out = [[[sem(f"{n}{c}{r}") for r in range(2)] for c in range(Q)] for n in ("x_in", "go_out")]
        ab_out = [sem(f"ab_out{r}") for r in range(2)]
        pe_done, act_done, pool_done, dve_done = sem("pe_done"), sem("act_done"), sem("pool_done"), sem("dve_done")
        eps_set, pool_passed, sp_passed = sem("eps_set"), sem("pool_passed"), sem("sp_passed")
        block = ctx.enter_context(nc.Block())
        CEN = [ps[:, b, :] for b in range(2)]
        VAR, GO = ps[:, 2, :], ps[:, 3, :]
        AB = [ps[:, 4 + t, :] for t in range(TILES)]

        def gated(engine, c, t, parity):
            return engine.tensor_tensor(stage[:, parity, t % HALF, :, c * 2 + t // HALF, :],
                                        ab[:, t, 0:N].rearrange("k (c h) -> k c h", h=HW),
                                        sg[:, t, :].rearrange("k (c h) -> k c h", h=HW), ALU.mult)

        @block.sync
        def _(sp):
            def slot(i, r):
                s = Slot(PROJECTION, sp, None, i, r)
                at = s.at

                def load_x(step, c):
                    if s.runs(step):
                        ahead = r + PROJECTION.ahead[step]
                        sp.dma_start(xin[:, ahead % 2, c, :], x2_t[:, bass.ds(i * (2 * Q * CH) + (ahead * Q + c) * CH, CH)]
                                     ).then_inc(x_in[c][ahead % 2], 16)

                def store_gate(step, c):
                    if s.runs(step):
                        ahead = r + PROJECTION.ahead[step]
                        sp.dma_start(go_t[:, bass.ds(i * (2 * Q * CH) + (ahead * Q + c) * CH, CH)], go[:, c, :]
                                     ).then_inc(go_out[c][ahead % 2], 16)

                def store_ab(step, kc, which):
                    if s.runs(step):
                        ahead = r + PROJECTION.ahead[step]
                        sp.dma_start(ab_d[which, :, kc, :, bass.ds(i * (16 * HW) + ahead * (8 * HW),
                                                                   8 * HW)].rearrange("c k x -> k c x"),
                                     stage[:, ahead % 2, kc, which * HC:(which + 1) * HC, :, :].rearrange("k c i h -> k c (i h)")
                                     ).then_inc(ab_out[ahead % 2], 16)

                sp.wait_ge(act_done, at("gs0", "go0"))
                sp.sem_inc(sp_passed, 1)
                store_gate("gs0", 0)
                sp.wait_ge(act_done, at("gs2", "go2"))
                sp.sem_inc(sp_passed, 1)
                store_gate("gs2", 2)
                sp.wait_ge(pe_done, at("x3", "mC3", 2))
                sp.sem_inc(sp_passed, 1)
                load_x("x3", 3)
                sp.wait_ge(pe_done, at("x0", "mC0", 2))
                sp.sem_inc(sp_passed, 1)
                load_x("x0", 0)
                store_gate("gs1", 1)
                load_x("x1", 1)
                sp.wait_ge(pool_done, at("as2", "ml31"))
                sp.sem_inc(sp_passed, 1)
                store_ab("as2", 1, 0)
                sp.wait_ge(pe_done, at("x2", "mC2", 2))
                sp.sem_inc(sp_passed, 1)
                load_x("x2", 2)
                store_ab("as3", 1, 1)
                sp.wait_ge(dve_done, at("as1", "ml30"))
                sp.sem_inc(sp_passed, 1)
                store_ab("as1", 0, 1)
                store_ab("as0", 0, 0)
                sp.wait_ge(act_done, at("gs3", "go3"))
                sp.sem_inc(sp_passed, 1)
                store_gate("gs3", 3)
            PROJECTION.run(sp, slot)
            for r in range(2):
                sp.wait_ge(ab_out[r], PROJECTION.rounds // 2 * 64)
                for c in range(Q):
                    sp.wait_ge(go_out[c][r], PROJECTION.rounds // 2 * 16)

        @block.tensor
        def _(pe):
            def slot(i, r):
                s = Slot(PROJECTION, pe, pe_done, i, r)
                at, on = s.at, s.on
                pe.wait_ge(dve_done, at("mA13", "ad03"))
                if on("mA13"):
                    nc.tensor.matmul(AB[3], z[:, s.parity, 1, 3 * P:4 * P], W["W4"][:, :], start=True, stop=True).then_inc(pe_done, 1)
                pe.wait_ge(act_done, at("mM3", "ln2"))
                if on("mM3"):
                    nc.tensor.matmul(VAR, const["mean"][:, :], sq[:, 1, :], start=True, stop=True).then_inc(pe_done, 1)
                pe.wait_ge(dve_done, at("mA10", "ad00"))
                if on("mA10"):
                    nc.tensor.matmul(AB[0], z[:, s.parity, 1, 0:P], W["W4"][:, :], start=True, stop=True).then_inc(pe_done, 1)
                if on("mA12"):
                    nc.tensor.matmul(AB[2], z[:, s.parity, 1, 2 * P:3 * P], W["W4"][:, :], start=True, stop=True).then_inc(pe_done, 1)
                pe.wait_ge(dve_done, at("mA11", "ad01"))
                if on("mA11"):
                    nc.tensor.matmul(AB[1], z[:, s.parity, 1, P:2 * P], W["W4"][:, :], start=True, stop=True).then_inc(pe_done, 1)
                pe.wait_ge(dve_done, at("mC1", "z3", 1))
                if s.runs("mC1"):
                    pe.wait_ge(x_in[1][s.side("mC1")], s.moved("mC1", 16))
                if on("mC1"):
                    nc.tensor.matmul(CEN[1], cen, xin[:, s.parity, 1, :], start=True, stop=True).then_inc(pe_done, 1)
                if s.runs("mC0"):
                    pe.wait_ge(x_in[0][s.side("mC0")], s.moved("mC0", 16))
                if on("mC0"):
                    nc.tensor.matmul(CEN[0], cen, xin[:, s.parity, 0, :], start=True, stop=True).then_inc(pe_done, 1)
                pe.wait_ge(act_done, at("mG1", "go0"))
                if on("mG1"):
                    nc.tensor.matmul(GO, W["Wg"][:, :], z[:, s.parity, 1, :], start=True, stop=True).then_inc(pe_done, 1)
                pe.wait_ge(dve_done, at("mA21", "ad11"))
                if on("mA21"):
                    nc.tensor.matmul(AB[1], z[:, s.parity, 2, P:2 * P], W["W4"][:, :], start=True, stop=True).then_inc(pe_done, 1)
                pe.wait_ge(dve_done, at("mA20", "ad10"))
                if on("mA20"):
                    nc.tensor.matmul(AB[0], z[:, s.parity, 2, 0:P], W["W4"][:, :], start=True, stop=True).then_inc(pe_done, 1)
                pe.wait_ge(act_done, at("mG2", "go1"))
                if on("mG2"):
                    nc.tensor.matmul(GO, W["Wg"][:, :], z[:, s.parity, 2, :], start=True, stop=True).then_inc(pe_done, 1)
                pe.wait_ge(dve_done, at("mA22", "ad12"))
                if on("mA22"):
                    nc.tensor.matmul(AB[2], z[:, s.parity, 2, 2 * P:3 * P], W["W4"][:, :], start=True, stop=True).then_inc(pe_done, 1)
                pe.wait_ge(dve_done, at("mA31", "ad21"))
                if on("mA31"):
                    nc.tensor.matmul(AB[1], z[:, s.parity, 3, P:2 * P], W["W4"][:, :], start=True, stop=True).then_inc(pe_done, 1)
                if on("mA23"):
                    nc.tensor.matmul(AB[3], z[:, s.parity, 2, 3 * P:4 * P], W["W4"][:, :], start=True, stop=True).then_inc(pe_done, 1)
                pe.wait_ge(dve_done, at("mA32", "ad22"))
                if on("mA32"):
                    nc.tensor.matmul(AB[2], z[:, s.parity, 3, 2 * P:3 * P], W["W4"][:, :], start=True, stop=True).then_inc(pe_done, 1)
                pe.wait_ge(act_done, at("mG3", "go2"))
                if on("mG3"):
                    nc.tensor.matmul(GO, W["Wg"][:, :], z[:, s.parity, 3, :], start=True, stop=True).then_inc(pe_done, 1)
                if on("mA30"):
                    nc.tensor.matmul(AB[0], z[:, s.parity, 3, 0:P], W["W4"][:, :], start=True, stop=True).then_inc(pe_done, 1)
                pe.wait_ge(dve_done, at("mA33", "ad23"))
                if on("mA33"):
                    nc.tensor.matmul(AB[3], z[:, s.parity, 3, 3 * P:4 * P], W["W4"][:, :], start=True, stop=True).then_inc(pe_done, 1)
                pe.wait_ge(dve_done, at("mA01", "ad31", 1))
                if on("mA01"):
                    nc.tensor.matmul(AB[1], z[:, s.parity, 0, P:2 * P], W["W4"][:, :], start=True, stop=True).then_inc(pe_done, 1)
                pe.wait_ge(act_done, at("mM0", "sq0"))
                if on("mM0"):
                    nc.tensor.matmul(VAR, const["mean"][:, :], sq[:, 0, :], start=True, stop=True).then_inc(pe_done, 1)
                pe.wait_ge(dve_done, at("mA00", "ad30", 1))
                if on("mA00"):
                    nc.tensor.matmul(AB[0], z[:, s.parity, 0, 0:P], W["W4"][:, :], start=True, stop=True).then_inc(pe_done, 1)
                pe.wait_ge(dve_done, at("mA03", "ad33", 1))
                if on("mA03"):
                    nc.tensor.matmul(AB[3], z[:, s.parity, 0, 3 * P:4 * P], W["W4"][:, :], start=True, stop=True).then_inc(pe_done, 1)
                pe.wait_ge(act_done, at("mM1", "ln0"))
                if on("mM1"):
                    nc.tensor.matmul(VAR, const["mean"][:, :], sq[:, 1, :], start=True, stop=True).then_inc(pe_done, 1)
                if on("mA02"):
                    nc.tensor.matmul(AB[2], z[:, s.parity, 0, 2 * P:3 * P], W["W4"][:, :], start=True, stop=True).then_inc(pe_done, 1)
                pe.wait_ge(dve_done, at("mC2", "z0"))
                if s.runs("mC2"):
                    pe.wait_ge(x_in[2][s.side("mC2")], s.moved("mC2", 16))
                if on("mC2"):
                    nc.tensor.matmul(CEN[0], cen, xin[:, s.parity, 2, :], start=True, stop=True).then_inc(pe_done, 1)
                if on("mG0"):
                    nc.tensor.matmul(GO, W["Wg"][:, :], z[:, s.parity, 0, :], start=True, stop=True).then_inc(pe_done, 1)
                pe.wait_ge(dve_done, at("mC3", "z1"))
                if s.runs("mC3"):
                    pe.wait_ge(x_in[3][s.side("mC3")], s.moved("mC3", 16))
                if on("mC3"):
                    nc.tensor.matmul(CEN[1], cen, xin[:, s.parity, 3, :], start=True, stop=True).then_inc(pe_done, 1)
                pe.wait_ge(act_done, at("mM2", "sq2"))
                if on("mM2"):
                    nc.tensor.matmul(VAR, const["mean"][:, :], sq[:, 0, :], start=True, stop=True).then_inc(pe_done, 1)
            pe.sem_inc(pe_done, 1)
            PROJECTION.run(pe, slot)

        @block.scalar
        def _(act):
            act.wait_ge(eps_set, 1)
            load_log_exp(nc, act)

            def slot(i, r):
                s = Slot(PROJECTION, act, act_done, i, r)
                at, on = s.at, s.on
                act.wait_ge(pe_done, at("ln3", "mM3"))
                act.wait_ge(act_done, at("ln3", "rs1"))
                if on("ln3"):
                    nc.scalar.activation(lnv[:, 1, :], VAR, ACT.Ln, bias=eps[:, 0:1]).then_inc(act_done, 1)
                act.wait_ge(act_done, at("rs3", "ln3"))
                act.wait_ge(dve_done, at("rs3", "z1"))
                if on("rs3"):
                    nc.scalar.activation(rstd[:, 1, :], lnv[:, 1, :], ACT.Exp, scale=-0.5).then_inc(act_done, 1)
                act.wait_ge(dve_done, at("sg01", "ad01"))
                act.wait_ge(pool_done, at("sg01", "ml31", 1))
                if on("sg01"):
                    nc.scalar.activation(sg[:, 1, :], ab[:, 1, N:2 * N], ACT.Sigmoid).then_inc(act_done, 1)
                if on("sg00"):
                    nc.scalar.activation(sg[:, 0, :], ab[:, 0, N:2 * N], ACT.Sigmoid).then_inc(act_done, 1)
                if s.runs("go0", 1):
                    act.wait_ge(go_out[0][s.side("go0", 1)], s.moved("go0", 16, 1))
                if on("go0"):
                    nc.scalar.activation(go[:, 0, :], GO, ACT.Sigmoid, bias=W["g_off"][:, 0:1]).then_inc(act_done, 1)
                if on("sg03"):
                    nc.scalar.activation(sg[:, 3, :], ab[:, 3, N:2 * N], ACT.Sigmoid).then_inc(act_done, 1)
                if on("sg02"):
                    nc.scalar.activation(sg[:, 2, :], ab[:, 2, N:2 * N], ACT.Sigmoid).then_inc(act_done, 1)
                act.wait_ge(dve_done, at("sg11", "ad11"))
                act.wait_ge(pool_done, at("sg11", "ml01"))
                if on("sg11"):
                    nc.scalar.activation(sg[:, 1, :], ab[:, 1, N:2 * N], ACT.Sigmoid).then_inc(act_done, 1)
                act.wait_ge(dve_done, at("sg10", "ad10"))
                if on("sg10"):
                    nc.scalar.activation(sg[:, 0, :], ab[:, 0, N:2 * N], ACT.Sigmoid).then_inc(act_done, 1)
                act.wait_ge(pe_done, at("go1", "mG1"))
                if s.runs("go1", 1):
                    act.wait_ge(go_out[1][s.side("go1", 1)], s.moved("go1", 16, 1))
                if on("go1"):
                    nc.scalar.activation(go[:, 1, :], GO, ACT.Sigmoid, bias=W["g_off"][:, 0:1]).then_inc(act_done, 1)
                if on("sq1"):
                    nc.scalar.activation(sq[:, 1, :], CEN[1], ACT.Square, bias=cenb).then_inc(act_done, 1)
                act.wait_ge(dve_done, at("sg13", "ad13"))
                act.wait_ge(pool_done, at("sg13", "ml03"))
                if on("sg13"):
                    nc.scalar.activation(sg[:, 3, :], ab[:, 3, N:2 * N], ACT.Sigmoid).then_inc(act_done, 1)
                act.wait_ge(dve_done, at("sg12", "ad12"))
                act.wait_ge(pool_done, at("sg12", "ml02"))
                if on("sg12"):
                    nc.scalar.activation(sg[:, 2, :], ab[:, 2, N:2 * N], ACT.Sigmoid).then_inc(act_done, 1)
                act.wait_ge(pe_done, at("go2", "mG2"))
                if s.runs("go2", 1):
                    act.wait_ge(go_out[2][s.side("go2", 1)], s.moved("go2", 16, 1))
                if on("go2"):
                    nc.scalar.activation(go[:, 2, :], GO, ACT.Sigmoid, bias=W["g_off"][:, 0:1]).then_inc(act_done, 1)
                act.wait_ge(dve_done, at("sg20", "ad20"))
                act.wait_ge(pool_done, at("sg20", "ml10"))
                if on("sg20"):
                    nc.scalar.activation(sg[:, 0, :], ab[:, 0, N:2 * N], ACT.Sigmoid).then_inc(act_done, 1)
                if on("sg21"):
                    nc.scalar.activation(sg[:, 1, :], ab[:, 1, N:2 * N], ACT.Sigmoid).then_inc(act_done, 1)
                act.wait_ge(dve_done, at("sg22", "ad22"))
                if on("sg22"):
                    nc.scalar.activation(sg[:, 2, :], ab[:, 2, N:2 * N], ACT.Sigmoid).then_inc(act_done, 1)
                act.wait_ge(dve_done, at("sg23", "ad23"))
                act.wait_ge(pool_done, at("sg23", "ml13"))
                if on("sg23"):
                    nc.scalar.activation(sg[:, 3, :], ab[:, 3, N:2 * N], ACT.Sigmoid).then_inc(act_done, 1)
                act.wait_ge(dve_done, at("sg32", "ad32"))
                act.wait_ge(pool_done, at("sg32", "ml22"))
                if on("sg32"):
                    nc.scalar.activation(sg[:, 2, :], ab[:, 2, N:2 * N], ACT.Sigmoid).then_inc(act_done, 1)
                act.wait_ge(pe_done, at("go3", "mG3"))
                if s.runs("go3", 1):
                    act.wait_ge(go_out[3][s.side("go3", 1)], s.moved("go3", 16, 1))
                if on("go3"):
                    nc.scalar.activation(go[:, 3, :], GO, ACT.Sigmoid, bias=W["g_off"][:, 0:1]).then_inc(act_done, 1)
                if on("sq0"):
                    nc.scalar.activation(sq[:, 0, :], CEN[0], ACT.Square, bias=cenb).then_inc(act_done, 1)
                act.wait_ge(dve_done, at("sg30", "ad30"))
                if on("sg30"):
                    nc.scalar.activation(sg[:, 0, :], ab[:, 0, N:2 * N], ACT.Sigmoid).then_inc(act_done, 1)
                if on("sg31"):
                    nc.scalar.activation(sg[:, 1, :], ab[:, 1, N:2 * N], ACT.Sigmoid).then_inc(act_done, 1)
                act.wait_ge(dve_done, at("sg33", "ad33"))
                act.wait_ge(pool_done, at("sg33", "ml23"))
                if on("sg33"):
                    nc.scalar.activation(sg[:, 3, :], ab[:, 3, N:2 * N], ACT.Sigmoid).then_inc(act_done, 1)
                load_log_exp(nc, act)
                act.wait_ge(pe_done, at("ln0", "mM0"))
                if on("ln0"):
                    nc.scalar.activation(lnv[:, 0, :], VAR, ACT.Ln, bias=eps[:, 0:1]).then_inc(act_done, 1)
                act.wait_ge(act_done, at("rs0", "ln0"))
                if on("rs0"):
                    nc.scalar.activation(rstd[:, 0, :], lnv[:, 0, :], ACT.Exp, scale=-0.5).then_inc(act_done, 1)
                act.wait_ge(pe_done, at("ln1", "mM1"))
                if on("ln1"):
                    nc.scalar.activation(lnv[:, 1, :], VAR, ACT.Ln, bias=eps[:, 0:1]).then_inc(act_done, 1)
                act.wait_ge(act_done, at("rs1", "ln1"))
                if on("rs1"):
                    nc.scalar.activation(rstd[:, 1, :], lnv[:, 1, :], ACT.Exp, scale=-0.5).then_inc(act_done, 1)
                act.wait_ge(pe_done, at("sq2", "mC2"))
                if on("sq2"):
                    nc.scalar.activation(sq[:, 0, :], CEN[0], ACT.Square, bias=cenb).then_inc(act_done, 1)
                act.wait_ge(pe_done, at("sq3", "mC3"))
                if on("sq3"):
                    nc.scalar.activation(sq[:, 1, :], CEN[1], ACT.Square, bias=cenb).then_inc(act_done, 1)
                act.wait_ge(pe_done, at("ln2", "mM2"))
                if on("ln2"):
                    nc.scalar.activation(lnv[:, 0, :], VAR, ACT.Ln, bias=eps[:, 0:1]).then_inc(act_done, 1)
                act.wait_ge(act_done, at("rs2", "ln2"))
                act.wait_ge(dve_done, at("rs2", "z0"))
                if on("rs2"):
                    nc.scalar.activation(rstd[:, 0, :], lnv[:, 0, :], ACT.Exp, scale=-0.5).then_inc(act_done, 1)
            act.sem_inc(act_done, 1)
            PROJECTION.run(act, slot)

        @block.gpsimd
        def _(pool):
            nc.gpsimd.memset(eps[:, :], EPS).then_inc(eps_set, 1)

            def slot(i, r):
                s = Slot(PROJECTION, pool, pool_done, i, r)
                at, on = s.at, s.on
                pool.wait_ge(dve_done, at("ml01", "ad01"))
                pool.wait_ge(act_done, at("ml01", "sg01"))
                if s.runs("ml01", 2):
                    pool.wait_ge(ab_out[s.side("ml01", 2)], s.moved("ml01", 64, 2))
                pool.sem_inc(pool_passed, 1)
                if on("ml01"):
                    gated(nc.gpsimd, 0, 1, s.parity).then_inc(pool_done, 1)
                pool.wait_ge(act_done, at("ml03", "sg03"))
                if s.runs("ml03", 2):
                    pool.wait_ge(ab_out[s.side("ml03", 2)], s.moved("ml03", 64, 2))
                pool.sem_inc(pool_passed, 1)
                if on("ml03"):
                    gated(nc.gpsimd, 0, 3, s.parity).then_inc(pool_done, 1)
                pool.wait_ge(act_done, at("ml02", "sg02"))
                if s.runs("ml02", 2):
                    pool.wait_ge(ab_out[s.side("ml02", 2)], s.moved("ml02", 64, 2))
                pool.sem_inc(pool_passed, 1)
                if on("ml02"):
                    gated(nc.gpsimd, 0, 2, s.parity).then_inc(pool_done, 1)
                pool.wait_ge(dve_done, at("ml11", "ad11"))
                pool.wait_ge(act_done, at("ml11", "sg11"))
                if s.runs("ml11", 2):
                    pool.wait_ge(ab_out[s.side("ml11", 2)], s.moved("ml11", 64, 2))
                pool.sem_inc(pool_passed, 1)
                if on("ml11"):
                    gated(nc.gpsimd, 1, 1, s.parity).then_inc(pool_done, 1)
                pool.wait_ge(dve_done, at("ml10", "ad10"))
                pool.wait_ge(act_done, at("ml10", "sg10"))
                if s.runs("ml10", 2):
                    pool.wait_ge(ab_out[s.side("ml10", 2)], s.moved("ml10", 64, 2))
                pool.sem_inc(pool_passed, 1)
                if on("ml10"):
                    gated(nc.gpsimd, 1, 0, s.parity).then_inc(pool_done, 1)
                pool.wait_ge(dve_done, at("ml13", "ad13"))
                pool.wait_ge(act_done, at("ml13", "sg13"))
                if s.runs("ml13", 2):
                    pool.wait_ge(ab_out[s.side("ml13", 2)], s.moved("ml13", 64, 2))
                pool.sem_inc(pool_passed, 1)
                if on("ml13"):
                    gated(nc.gpsimd, 1, 3, s.parity).then_inc(pool_done, 1)
                pool.wait_ge(dve_done, at("ml21", "ad21"))
                pool.wait_ge(act_done, at("ml21", "sg21"))
                if s.runs("ml21", 2):
                    pool.wait_ge(ab_out[s.side("ml21", 2)], s.moved("ml21", 64, 2))
                pool.sem_inc(pool_passed, 1)
                if on("ml21"):
                    gated(nc.gpsimd, 2, 1, s.parity).then_inc(pool_done, 1)
                pool.wait_ge(dve_done, at("ml20", "ad20"))
                if s.runs("ml20", 2):
                    pool.wait_ge(ab_out[s.side("ml20", 2)], s.moved("ml20", 64, 2))
                pool.sem_inc(pool_passed, 1)
                if on("ml20"):
                    gated(nc.gpsimd, 2, 0, s.parity).then_inc(pool_done, 1)
                pool.wait_ge(dve_done, at("ml22", "ad22"))
                pool.wait_ge(act_done, at("ml22", "sg22"))
                if s.runs("ml22", 2):
                    pool.wait_ge(ab_out[s.side("ml22", 2)], s.moved("ml22", 64, 2))
                pool.sem_inc(pool_passed, 1)
                if on("ml22"):
                    gated(nc.gpsimd, 2, 2, s.parity).then_inc(pool_done, 1)
                pool.wait_ge(dve_done, at("ml23", "ad23"))
                pool.wait_ge(act_done, at("ml23", "sg23"))
                if s.runs("ml23", 2):
                    pool.wait_ge(ab_out[s.side("ml23", 2)], s.moved("ml23", 64, 2))
                pool.sem_inc(pool_passed, 1)
                if on("ml23"):
                    gated(nc.gpsimd, 2, 3, s.parity).then_inc(pool_done, 1)
                pool.wait_ge(dve_done, at("ml33", "ad33"))
                pool.wait_ge(act_done, at("ml33", "sg33"))
                if s.runs("ml33", 2):
                    pool.wait_ge(ab_out[s.side("ml33", 2)], s.moved("ml33", 64, 2))
                pool.sem_inc(pool_passed, 1)
                if on("ml33"):
                    gated(nc.gpsimd, 3, 3, s.parity).then_inc(pool_done, 1)
                if s.runs("ml31", 2):
                    pool.wait_ge(ab_out[s.side("ml31", 2)], s.moved("ml31", 64, 2))
                pool.sem_inc(pool_passed, 1)
                if on("ml31"):
                    gated(nc.gpsimd, 3, 1, s.parity).then_inc(pool_done, 1)
            pool.sem_inc(pool_done, 1)
            PROJECTION.run(pool, slot)

        @block.vector
        def _(dve):
            def slot(i, r):
                s = Slot(PROJECTION, dve, dve_done, i, r)
                at, on = s.at, s.on
                dve.wait_ge(pe_done, at("ad00", "mA00"))
                dve.wait_ge(act_done, at("ad00", "sg30", 1))
                dve.wait_ge(dve_done, at("ad00", "ml30", 1))
                if on("ad00"):
                    nc.vector.tensor_tensor(ab[:, 0, :], AB[0], W["bias4"][:, :], ALU.add).then_inc(dve_done, 1)
                dve.wait_ge(act_done, at("ad01", "sg31", 1))
                dve.wait_ge(pool_done, at("ad01", "ml31", 1))
                if on("ad01"):
                    nc.vector.tensor_tensor(ab[:, 1, :], AB[1], W["bias4"][:, :], ALU.add).then_inc(dve_done, 1)
                dve.wait_ge(pe_done, at("z2", "mC2"))
                dve.wait_ge(act_done, at("z2", "rs2"))
                if on("z2"):
                    nc.vector.scalar_tensor_tensor(z[:, s.parity, 2, :], CEN[0], cenb, rstd[:, 0, :], ALU.add,
                                                   ALU.mult).then_inc(dve_done, 1)
                dve.wait_ge(pe_done, at("z3", "mC3"))
                dve.wait_ge(act_done, at("z3", "rs3"))
                if on("z3"):
                    nc.vector.scalar_tensor_tensor(z[:, s.parity, 3, :], CEN[1], cenb, rstd[:, 1, :], ALU.add,
                                                   ALU.mult).then_inc(dve_done, 1)
                dve.wait_ge(dve_done, at("ml00", "ad00"))
                dve.wait_ge(act_done, at("ml00", "sg00"))
                if s.runs("ml00", 2):
                    dve.wait_ge(ab_out[s.side("ml00", 2)], s.moved("ml00", 64, 2))
                if on("ml00"):
                    gated(nc.vector, 0, 0, s.parity).then_inc(dve_done, 1)
                dve.wait_ge(pe_done, at("ad11", "mA11"))
                dve.wait_ge(pool_done, at("ad11", "ml01"))
                if on("ad11"):
                    nc.vector.tensor_tensor(ab[:, 1, :], AB[1], W["bias4"][:, :], ALU.add).then_inc(dve_done, 1)
                dve.wait_ge(dve_done, at("ad10", "ml00"))
                if on("ad10"):
                    nc.vector.tensor_tensor(ab[:, 0, :], AB[0], W["bias4"][:, :], ALU.add).then_inc(dve_done, 1)
                dve.wait_ge(act_done, at("ad13", "sg03"))
                dve.wait_ge(pool_done, at("ad13", "ml03"))
                if on("ad13"):
                    nc.vector.tensor_tensor(ab[:, 3, :], AB[3], W["bias4"][:, :], ALU.add).then_inc(dve_done, 1)
                dve.wait_ge(act_done, at("ad12", "sg02"))
                dve.wait_ge(pool_done, at("ad12", "ml02"))
                if on("ad12"):
                    nc.vector.tensor_tensor(ab[:, 2, :], AB[2], W["bias4"][:, :], ALU.add).then_inc(dve_done, 1)
                dve.wait_ge(pe_done, at("ad21", "mA21"))
                dve.wait_ge(act_done, at("ad21", "sg11"))
                dve.wait_ge(pool_done, at("ad21", "ml11"))
                if on("ad21"):
                    nc.vector.tensor_tensor(ab[:, 1, :], AB[1], W["bias4"][:, :], ALU.add).then_inc(dve_done, 1)
                dve.wait_ge(pe_done, at("ad20", "mA20"))
                dve.wait_ge(act_done, at("ad20", "sg10"))
                dve.wait_ge(pool_done, at("ad20", "ml10"))
                if on("ad20"):
                    nc.vector.tensor_tensor(ab[:, 0, :], AB[0], W["bias4"][:, :], ALU.add).then_inc(dve_done, 1)
                dve.wait_ge(dve_done, at("ml12", "ad12"))
                dve.wait_ge(act_done, at("ml12", "sg12"))
                if s.runs("ml12", 2):
                    dve.wait_ge(ab_out[s.side("ml12", 2)], s.moved("ml12", 64, 2))
                if on("ml12"):
                    gated(nc.vector, 1, 2, s.parity).then_inc(dve_done, 1)
                dve.wait_ge(pe_done, at("ad22", "mA22"))
                dve.wait_ge(dve_done, at("ad22", "ml12"))
                if on("ad22"):
                    nc.vector.tensor_tensor(ab[:, 2, :], AB[2], W["bias4"][:, :], ALU.add).then_inc(dve_done, 1)
                dve.wait_ge(pe_done, at("ad23", "mA23"))
                dve.wait_ge(pool_done, at("ad23", "ml13"))
                if on("ad23"):
                    nc.vector.tensor_tensor(ab[:, 3, :], AB[3], W["bias4"][:, :], ALU.add).then_inc(dve_done, 1)
                dve.wait_ge(pe_done, at("ad32", "mA32"))
                dve.wait_ge(act_done, at("ad32", "sg22"))
                dve.wait_ge(pool_done, at("ad32", "ml22"))
                if on("ad32"):
                    nc.vector.tensor_tensor(ab[:, 2, :], AB[2], W["bias4"][:, :], ALU.add).then_inc(dve_done, 1)
                if on("ad31"):
                    nc.vector.tensor_tensor(ab[:, 1, :], AB[1], W["bias4"][:, :], ALU.add).then_inc(dve_done, 1)
                dve.wait_ge(pe_done, at("ad30", "mA30"))
                if on("ad30"):
                    nc.vector.tensor_tensor(ab[:, 0, :], AB[0], W["bias4"][:, :], ALU.add).then_inc(dve_done, 1)
                dve.wait_ge(pe_done, at("ad33", "mA33"))
                dve.wait_ge(act_done, at("ad33", "sg23"))
                dve.wait_ge(pool_done, at("ad33", "ml23"))
                if on("ad33"):
                    nc.vector.tensor_tensor(ab[:, 3, :], AB[3], W["bias4"][:, :], ALU.add).then_inc(dve_done, 1)
                dve.wait_ge(dve_done, at("ml32", "ad32"))
                dve.wait_ge(act_done, at("ml32", "sg32"))
                if s.runs("ml32", 2):
                    dve.wait_ge(ab_out[s.side("ml32", 2)], s.moved("ml32", 64, 2))
                if on("ml32"):
                    gated(nc.vector, 3, 2, s.parity).then_inc(dve_done, 1)
                dve.wait_ge(act_done, at("z0", "rs0"))
                if on("z0"):
                    nc.vector.scalar_tensor_tensor(z[:, s.parity, 0, :], CEN[0], cenb, rstd[:, 0, :], ALU.add,
                                                   ALU.mult).then_inc(dve_done, 1)
                dve.wait_ge(pe_done, at("ad03", "mA03"))
                dve.wait_ge(pool_done, at("ad03", "ml33", 1))
                if on("ad03"):
                    nc.vector.tensor_tensor(ab[:, 3, :], AB[3], W["bias4"][:, :], ALU.add).then_inc(dve_done, 1)
                dve.wait_ge(pe_done, at("ad02", "mA02"))
                dve.wait_ge(dve_done, at("ad02", "ml32", 1))
                if on("ad02"):
                    nc.vector.tensor_tensor(ab[:, 2, :], AB[2], W["bias4"][:, :], ALU.add).then_inc(dve_done, 1)
                dve.wait_ge(act_done, at("z1", "rs1"))
                if on("z1"):
                    nc.vector.scalar_tensor_tensor(z[:, s.parity, 1, :], CEN[1], cenb, rstd[:, 1, :], ALU.add,
                                                   ALU.mult).then_inc(dve_done, 1)
                if s.runs("ml30", 2):
                    dve.wait_ge(ab_out[s.side("ml30", 2)], s.moved("ml30", 64, 2))
                if on("ml30"):
                    gated(nc.vector, 3, 0, s.parity).then_inc(dve_done, 1)
            dve.sem_inc(dve_done, 1)
            PROJECTION.run(dve, slot)


def triangle_products(nc, ab_d, t_t, ps):
    SLOTS = 4
    with ExitStack() as ctx:
        sb = lambda n, s: ctx.enter_context(nc.sbuf_tensor("f_" + n, s, F32))
        new_sem = ctx.enter_context(phase_semaphores(nc))
        sem = lambda n: new_sem("f_" + n)
        ab = sb("ab", [P, 2, 2, HALF, N, HW])
        t = sb("t", [P, SLOTS, 2, HALF * N])
        ab_in = [sem(f"ab_in{b}") for b in range(2)]
        t_out = [sem(f"t_out{s}") for s in range(SLOTS)]
        product, even_copied, odd_copied = sem("product"), sem("even_copied"), sem("odd_copied")
        block = ctx.enter_context(nc.Block())
        T = [ps[:, b, :] for b in range(SLOTS)]

        def chunks(eng, chunk):
            looped(eng, 0, HC // 2, 1, lambda i: [chunk(i, b) for b in range(2)], tail=1)

        def h_count(i, b, c, per=HW):
            return i * (2 * per) + (b * per + c)

        def load(sp, i, b):
            for which in range(2):
                sp.dma_start(ab[:, b, which, :, :, :].rearrange("k c i h -> k c (i h)"),
                             (ab_d[which, bass.ds(i * 2 + b, 1), :, :,
                                   :]).rearrange("o c k x -> k (o c) x")).then_inc(ab_in[b], 16)

        @block.sync
        def _(sp):
            load(sp, 0, 0)

            def chunk(i, b):
                if b == 0:
                    wait_count(sp, product, h_count(i, 0, 0))
                    load(sp, i, 1)
                elif not (isinstance(i, int) and i == HC // 2 - 1):
                    wait_count(sp, product, h_count(i, 1, 0))
                    load(sp, i + 1, 0)
                for m in range(HW // 2):
                    wait_count(sp, even_copied, h_count(i, b, m + 1, HW // 2))
                    wait_count(sp, odd_copied, h_count(i, b, m + 1, HW // 2))
                    sp.dma_start(t_t[bass.ds(i * (2 * HW) + (b * HW + 2 * m), 2), :].rearrange("h (c p j) -> p h c j",
                            c=HALF, p=P),
                                 t[:, m % SLOTS, :, :].rearrange("p h (c j) -> p h c j", c=HALF)).then_inc(t_out[m % SLOTS], 16)
            chunks(sp, chunk)
            for s in range(SLOTS):
                sp.wait_ge(t_out[s], P // 2 // SLOTS * 16)

        @block.tensor
        def _(pe):
            def chunk(i, b):
                wait_count(pe, ab_in[b], i * 32 + 32)
                for h in range(HW):
                    wait_count(pe, odd_copied if h % 2 else even_copied, h_count(i, b, h // 2 - 1, HW // 2))
                    for ic in range(HALF):
                        for kc in range(HALF):
                            mm = nc.tensor.matmul(T[h % SLOTS][:, ic * N:(ic + 1) * N], ab[:, b, 0, kc, ic * P:(ic + 1) * P, h],
                                                  ab[:, b, 1, kc, :, h], start=kc == 0, stop=kc == HALF - 1)
                    mm.then_inc(product, 1)
            chunks(pe, chunk)

        def copier(eng, copy, parity, copied):
            def chunk(i, b):
                for m in range(HW // 2):
                    h = 2 * m + parity
                    wait_count(eng, product, h_count(i, b, h + 1))
                    wait_count(eng, t_out[m % SLOTS], h_count(i, b, m // SLOTS, HW // 2 // SLOTS) * 16)
                    copy(t[:, m % SLOTS, parity, :], T[h % SLOTS]).then_inc(copied, 1)
            chunks(eng, chunk)

        @block.vector
        def _(dve):
            copier(dve, nc.vector.tensor_copy, 0, even_copied)

        @block.scalar
        def _(act):
            copier(act, lambda o, i: nc.scalar.activation(o, i, ACT.Identity), 1, odd_copied)


OUTPUT_STEPS = {
    "pe": [("mC1", 2), ("mC2", 2), ("mM1", 2), ("mM2", 2), ("mO0", 1), ("mC3", 2), ("mO3", 1), ("mO2", 1), ("mM3", 2),
        ("mC0", 3), ("mO1", 2), ("mM0", 3)],
    "act": [("ln3", 1), ("sq1", 2), ("ln0", 2), ("sq2", 2), ("rs3", 1), ("ln1", 2), ("rs0", 2), ("sq3", 2),
        ("ln2", 2), ("rs1", 2), ("sq0", 3), ("rs2", 2)],
    "pool": [("o2", 0), ("o1", 1), ("o3", 1), ("o0", 1)],
    "dve": [("y2", 0), ("tn2", 1), ("bn3", 0), ("tn3", 1), ("y1", 1), ("y0", 1), ("y3", 1), ("tn0", 2), ("tn1", 2),
        ("bn2", 0), ("bn1", 1), ("bn0", 0)],
    "sp": [("t2", 3), ("t0", 3), ("x0", 1), ("x3", 1), ("t1", 3), ("x2", 1), ("g1", 2), ("g3", 2), ("g0", 2),
        ("t3", 3), ("st3", 0), ("st1", 0), ("st0", 0), ("st2", 0), ("x1", 2), ("g2", 2)],
}
OUTPUT = Schedule(NCH // 4, -3, OUTPUT_STEPS)


def triangle_output(nc, t_t, go_t, x2_t, x3_t, W, const, stats, ps):
    Q = 4
    with ExitStack() as ctx:
        sb = lambda n, s: ctx.enter_context(nc.sbuf_tensor("g_" + n, s, F32))
        new_sem = ctx.enter_context(phase_semaphores(nc))
        sem = lambda n: new_sem("g_" + n)
        tin, gin, xin, tn, x3 = [sb(n, [P, 2, Q, CH]) for n in ("tin", "gin", "xin", "tn", "x3")]
        sq, lnv, rstd = sb("sq", [P, 2, CH]), sb("lnv", [P, 2, CH]), sb("rstd", [P, 2, CH])
        eps = sb("eps", [P, 1])
        t_in, g_in, x_in, x_out = [[[sem(f"{n}{c}{r}") for r in range(2)] for c in range(Q)] for n in ("t_in", "g_in",
                "x_in", "x_out")]
        pe_done, act_done, pool_done, dve_done = sem("pe_done"), sem("act_done"), sem("pool_done"), sem("dve_done")
        eps_set, pool_passed, sp_passed = sem("eps_set"), sem("pool_passed"), sem("sp_passed")
        block = ctx.enter_context(nc.Block())
        CEN = [ps[:, q, :] for q in range(Q)]
        VAR = [ps[:, 4 + b, :] for b in range(2)]
        OUT = [ps[:, 6 + b, :] for b in range(2)]

        @block.sync
        def _(sp):
            def slot(i, r):
                s = Slot(OUTPUT, sp, None, i, r)
                at = s.at

                def load(step, buffer, array, c, arrived):
                    if s.runs(step):
                        ahead = r + OUTPUT.ahead[step]
                        sp.dma_start(buffer[:, ahead % 2, c, :], array[:, bass.ds(i * (2 * Q * CH) + (ahead * Q + c) * CH, CH)]
                                     ).then_inc(arrived[c][ahead % 2], 16)

                def store(step, array, buffer, c, stored):
                    if s.runs(step):
                        ahead = r + OUTPUT.ahead[step]
                        sp.dma_start(array[:, bass.ds(i * (2 * Q * CH) + (ahead * Q + c) * CH, CH)], buffer[:, ahead % 2, c, :]
                                     ).then_inc(stored[c][ahead % 2], 16)

                sp.wait_ge(pe_done, at("t2", "mC2", 2))
                sp.sem_inc(sp_passed, 1)
                load("t2", tin, t_t, 2, t_in)
                load("t0", tin, t_t, 0, t_in)
                sp.wait_ge(pool_done, at("x0", "o0", 2))
                sp.sem_inc(sp_passed, 1)
                load("x0", xin, x2_t, 0, x_in)
                load("x3", xin, x2_t, 3, x_in)
                load("t1", tin, t_t, 1, t_in)
                sp.wait_ge(pool_done, at("x2", "o2", 2))
                sp.sem_inc(sp_passed, 1)
                load("x2", xin, x2_t, 2, x_in)
                sp.wait_ge(dve_done, at("g1", "y1", 2))
                sp.sem_inc(sp_passed, 1)
                load("g1", gin, go_t, 1, g_in)
                sp.wait_ge(dve_done, at("g3", "y3", 2))
                sp.sem_inc(sp_passed, 1)
                load("g3", gin, go_t, 3, g_in)
                load("g0", gin, go_t, 0, g_in)
                sp.wait_ge(pe_done, at("t3", "mC3", 2))
                sp.sem_inc(sp_passed, 1)
                load("t3", tin, t_t, 3, t_in)
                sp.wait_ge(pool_done, at("st3", "o3"))
                sp.sem_inc(sp_passed, 1)
                store("st3", x3_t, x3, 3, x_out)
                store("st1", x3_t, x3, 1, x_out)
                sp.wait_ge(pool_done, at("st0", "o0"))
                sp.sem_inc(sp_passed, 1)
                store("st0", x3_t, x3, 0, x_out)
                sp.wait_ge(pool_done, at("st2", "o2"))
                sp.sem_inc(sp_passed, 1)
                store("st2", x3_t, x3, 2, x_out)
                load("x1", xin, x2_t, 1, x_in)
                sp.wait_ge(dve_done, at("g2", "y2", 2))
                sp.sem_inc(sp_passed, 1)
                load("g2", gin, go_t, 2, g_in)
            OUTPUT.run(sp, slot)
            for stored in (x_out,):
                for c in range(Q):
                    for r in range(2):
                        sp.wait_ge(stored[c][r], OUTPUT.rounds // 2 * 16)

        @block.tensor
        def _(pe):
            def slot(i, r):
                s = Slot(OUTPUT, pe, pe_done, i, r)
                at, on = s.at, s.on
                pe.wait_ge(act_done, at("mC1", "sq1", 1))
                pe.wait_ge(dve_done, at("mC1", "tn1", 1))
                if s.runs("mC1"):
                    pe.wait_ge(t_in[1][s.side("mC1")], s.moved("mC1", 16))
                if on("mC1"):
                    nc.tensor.matmul(CEN[1], const["center"][:, :], tin[:, s.parity, 1, :], start=True,
                                     stop=True).then_inc(pe_done, 1)
                pe.wait_ge(act_done, at("mC2", "sq2", 1))
                pe.wait_ge(dve_done, at("mC2", "tn2", 1))
                if s.runs("mC2"):
                    pe.wait_ge(t_in[2][s.side("mC2")], s.moved("mC2", 16))
                if on("mC2"):
                    nc.tensor.matmul(CEN[2], const["center"][:, :], tin[:, s.parity, 2, :], start=True,
                                     stop=True).then_inc(pe_done, 1)
                pe.wait_ge(act_done, at("mM1", "sq1"))
                if on("mM1"):
                    nc.tensor.matmul(VAR[1], const["mean"][:, :], sq[:, 1, :], start=True, stop=True).then_inc(pe_done, 1)
                pe.wait_ge(act_done, at("mM2", "sq2"))
                if on("mM2"):
                    nc.tensor.matmul(VAR[0], const["mean"][:, :], sq[:, 0, :], start=True, stop=True).then_inc(pe_done, 1)
                if on("mO0"):
                    nc.tensor.matmul(OUT[0], W["Wo"][:, :], tn[:, s.parity, 0, :], start=True, stop=True).then_inc(pe_done, 1)
                pe.wait_ge(dve_done, at("mC3", "tn3", 1))
                if s.runs("mC3"):
                    pe.wait_ge(t_in[3][s.side("mC3")], s.moved("mC3", 16))
                if on("mC3"):
                    nc.tensor.matmul(CEN[3], const["center"][:, :], tin[:, s.parity, 3, :], start=True,
                                     stop=True).then_inc(pe_done, 1)
                pe.wait_ge(dve_done, at("mO3", "y1"))
                if on("mO3"):
                    nc.tensor.matmul(OUT[1], W["Wo"][:, :], tn[:, s.parity, 3, :], start=True, stop=True).then_inc(pe_done, 1)
                pe.wait_ge(dve_done, at("mO2", "y0"))
                if on("mO2"):
                    nc.tensor.matmul(OUT[0], W["Wo"][:, :], tn[:, s.parity, 2, :], start=True, stop=True).then_inc(pe_done, 1)
                pe.wait_ge(act_done, at("mM3", "sq3"))
                if on("mM3"):
                    nc.tensor.matmul(VAR[1], const["mean"][:, :], sq[:, 1, :], start=True, stop=True).then_inc(pe_done, 1)
                pe.wait_ge(dve_done, at("mC0", "tn0", 1))
                if s.runs("mC0"):
                    pe.wait_ge(t_in[0][s.side("mC0")], s.moved("mC0", 16))
                if on("mC0"):
                    nc.tensor.matmul(CEN[0], const["center"][:, :], tin[:, s.parity, 0, :], start=True,
                                     stop=True).then_inc(pe_done, 1)
                pe.wait_ge(dve_done, at("mO1", "tn1"))
                if on("mO1"):
                    nc.tensor.matmul(OUT[1], W["Wo"][:, :], tn[:, s.parity, 1, :], start=True, stop=True).then_inc(pe_done, 1)
                pe.wait_ge(act_done, at("mM0", "sq0"))
                if on("mM0"):
                    nc.tensor.matmul(VAR[0], const["mean"][:, :], sq[:, 0, :], start=True, stop=True).then_inc(pe_done, 1)
            pe.sem_inc(pe_done, 1)
            OUTPUT.run(pe, slot)

        @block.scalar
        def _(act):
            act.wait_ge(eps_set, 1)
            load_log_exp(nc, act)

            def slot(i, r):
                s = Slot(OUTPUT, act, act_done, i, r)
                at, on = s.at, s.on
                act.wait_ge(pe_done, at("ln3", "mM3"))
                act.wait_ge(act_done, at("ln3", "rs1"))
                if on("ln3"):
                    nc.scalar.activation(lnv[:, 1, :], VAR[1], ACT.Ln, bias=eps[:, 0:1]).then_inc(act_done, 1)
                act.wait_ge(pe_done, at("sq1", "mC1"))
                if on("sq1"):
                    nc.scalar.activation(sq[:, 1, :], CEN[1], ACT.Square).then_inc(act_done, 1)
                act.wait_ge(act_done, at("ln0", "rs2", 1))
                if on("ln0"):
                    nc.scalar.activation(lnv[:, 0, :], VAR[0], ACT.Ln, bias=eps[:, 0:1]).then_inc(act_done, 1)
                act.wait_ge(pe_done, at("sq2", "mC2"))
                if on("sq2"):
                    nc.scalar.activation(sq[:, 0, :], CEN[2], ACT.Square).then_inc(act_done, 1)
                act.wait_ge(act_done, at("rs3", "ln3"))
                act.wait_ge(dve_done, at("rs3", "tn1"))
                if on("rs3"):
                    nc.scalar.activation(rstd[:, 1, :], lnv[:, 1, :], ACT.Exp, scale=-0.5).then_inc(act_done, 1)
                act.wait_ge(pe_done, at("ln1", "mM1"))
                act.wait_ge(act_done, at("ln1", "rs3", 1))
                if on("ln1"):
                    nc.scalar.activation(lnv[:, 1, :], VAR[1], ACT.Ln, bias=eps[:, 0:1]).then_inc(act_done, 1)
                act.wait_ge(dve_done, at("rs0", "tn2", 1))
                if on("rs0"):
                    nc.scalar.activation(rstd[:, 0, :], lnv[:, 0, :], ACT.Exp, scale=-0.5).then_inc(act_done, 1)
                act.wait_ge(pe_done, at("sq3", "mC3"))
                if on("sq3"):
                    nc.scalar.activation(sq[:, 1, :], CEN[3], ACT.Square).then_inc(act_done, 1)
                act.wait_ge(act_done, at("ln2", "rs0"))
                if on("ln2"):
                    nc.scalar.activation(lnv[:, 0, :], VAR[0], ACT.Ln, bias=eps[:, 0:1]).then_inc(act_done, 1)
                act.wait_ge(dve_done, at("rs1", "tn3", 1))
                if on("rs1"):
                    nc.scalar.activation(rstd[:, 1, :], lnv[:, 1, :], ACT.Exp, scale=-0.5).then_inc(act_done, 1)
                act.wait_ge(pe_done, at("sq0", "mC0"))
                if on("sq0"):
                    nc.scalar.activation(sq[:, 0, :], CEN[0], ACT.Square).then_inc(act_done, 1)
                act.wait_ge(act_done, at("rs2", "ln2"))
                act.wait_ge(dve_done, at("rs2", "tn0"))
                if on("rs2"):
                    nc.scalar.activation(rstd[:, 0, :], lnv[:, 0, :], ACT.Exp, scale=-0.5).then_inc(act_done, 1)
            act.sem_inc(act_done, 1)
            OUTPUT.run(act, slot)

        @block.gpsimd
        def _(pool):
            nc.gpsimd.memset(eps[:, :], EPS).then_inc(eps_set, 1)

            def slot(i, r):
                s = Slot(OUTPUT, pool, pool_done, i, r)
                at, on = s.at, s.on
                pool.wait_ge(dve_done, at("o2", "y2"))
                if s.runs("o2"):
                    pool.wait_ge(x_in[2][s.side("o2")], s.moved("o2", 16))
                pool.sem_inc(pool_passed, 1)
                if on("o2"):
                    nc.gpsimd.tensor_tensor(x3[:, s.parity, 2, :], x3[:, s.parity, 2, :], xin[:, s.parity, 2, :],
                                            ALU.add).then_inc(pool_done, 1)
                pool.wait_ge(dve_done, at("o1", "y1"))
                if s.runs("o1"):
                    pool.wait_ge(x_in[1][s.side("o1")], s.moved("o1", 16))
                pool.sem_inc(pool_passed, 1)
                if on("o1"):
                    nc.gpsimd.tensor_tensor(x3[:, s.parity, 1, :], x3[:, s.parity, 1, :], xin[:, s.parity, 1, :],
                                            ALU.add).then_inc(pool_done, 1)
                pool.wait_ge(dve_done, at("o3", "y3"))
                if s.runs("o3"):
                    pool.wait_ge(x_in[3][s.side("o3")], s.moved("o3", 16))
                pool.sem_inc(pool_passed, 1)
                if on("o3"):
                    nc.gpsimd.tensor_tensor(x3[:, s.parity, 3, :], x3[:, s.parity, 3, :], xin[:, s.parity, 3, :],
                                            ALU.add).then_inc(pool_done, 1)
                if s.runs("o0"):
                    pool.wait_ge(x_in[0][s.side("o0")], s.moved("o0", 16))
                pool.sem_inc(pool_passed, 1)
                if on("o0"):
                    nc.gpsimd.tensor_tensor(x3[:, s.parity, 0, :], x3[:, s.parity, 0, :], xin[:, s.parity, 0, :],
                                            ALU.add).then_inc(pool_done, 1)
            pool.sem_inc(pool_done, 1)
            OUTPUT.run(pool, slot)

        @block.vector
        def _(dve):
            def slot(i, r):
                s = Slot(OUTPUT, dve, dve_done, i, r)
                at, on = s.at, s.on
                dve.wait_ge(pe_done, at("y2", "mO2"))
                dve.wait_ge(pool_done, at("y2", "o2", 2))
                dve.wait_ge(dve_done, at("y2", "bn2", 2))
                if s.runs("y2"):
                    dve.wait_ge(g_in[2][s.side("y2")], s.moved("y2", 16))
                if s.runs("y2", 2):
                    dve.wait_ge(x_out[2][s.side("y2", 2)], s.moved("y2", 16, 2))
                if on("y2"):
                    nc.vector.scalar_tensor_tensor(x3[:, s.parity, 2, :], OUT[0], W["o_off"][:, 0:1],
                                                   gin[:, s.parity, 2, :], ALU.add, ALU.mult).then_inc(dve_done, 1)
                dve.wait_ge(act_done, at("tn2", "rs2"))
                if on("tn2"):
                    nc.vector.tensor_tensor(tn[:, s.parity, 2, :], CEN[2], rstd[:, 0, :], ALU.mult).then_inc(dve_done, 1)
                dve.wait_ge(pool_done, at("bn3", "o3"))
                if on("bn3"):
                    nc.vector.bn_stats(stats[:, bass.ds(i * (2 * Q * 6) + ((r + OUTPUT.ahead["bn3"]) * Q + 3) * 6, 6)],
                                       x3[:, s.parity, 3, :]).then_inc(dve_done, 1)
                dve.wait_ge(act_done, at("tn3", "rs3"))
                if on("tn3"):
                    nc.vector.tensor_tensor(tn[:, s.parity, 3, :], CEN[3], rstd[:, 1, :], ALU.mult).then_inc(dve_done, 1)
                dve.wait_ge(pe_done, at("y1", "mO1"))
                dve.wait_ge(dve_done, at("y1", "bn1", 2))
                if s.runs("y1"):
                    dve.wait_ge(g_in[1][s.side("y1")], s.moved("y1", 16))
                if s.runs("y1", 2):
                    dve.wait_ge(x_out[1][s.side("y1", 2)], s.moved("y1", 16, 2))
                if on("y1"):
                    nc.vector.scalar_tensor_tensor(x3[:, s.parity, 1, :], OUT[1], W["o_off"][:, 0:1],
                                                   gin[:, s.parity, 1, :], ALU.add, ALU.mult).then_inc(dve_done, 1)
                dve.wait_ge(pe_done, at("y0", "mO0"))
                dve.wait_ge(dve_done, at("y0", "bn0", 2))
                if s.runs("y0"):
                    dve.wait_ge(g_in[0][s.side("y0")], s.moved("y0", 16))
                if s.runs("y0", 2):
                    dve.wait_ge(x_out[0][s.side("y0", 2)], s.moved("y0", 16, 2))
                if on("y0"):
                    nc.vector.scalar_tensor_tensor(x3[:, s.parity, 0, :], OUT[0], W["o_off"][:, 0:1],
                                                   gin[:, s.parity, 0, :], ALU.add, ALU.mult).then_inc(dve_done, 1)
                dve.wait_ge(pe_done, at("y3", "mO3"))
                if s.runs("y3"):
                    dve.wait_ge(g_in[3][s.side("y3")], s.moved("y3", 16))
                if s.runs("y3", 2):
                    dve.wait_ge(x_out[3][s.side("y3", 2)], s.moved("y3", 16, 2))
                if on("y3"):
                    nc.vector.scalar_tensor_tensor(x3[:, s.parity, 3, :], OUT[1], W["o_off"][:, 0:1],
                                                   gin[:, s.parity, 3, :], ALU.add, ALU.mult).then_inc(dve_done, 1)
                dve.wait_ge(act_done, at("tn0", "rs0"))
                if on("tn0"):
                    nc.vector.tensor_tensor(tn[:, s.parity, 0, :], CEN[0], rstd[:, 0, :], ALU.mult).then_inc(dve_done, 1)
                dve.wait_ge(act_done, at("tn1", "rs1"))
                if on("tn1"):
                    nc.vector.tensor_tensor(tn[:, s.parity, 1, :], CEN[1], rstd[:, 1, :], ALU.mult).then_inc(dve_done, 1)
                dve.wait_ge(pool_done, at("bn2", "o2"))
                if on("bn2"):
                    nc.vector.bn_stats(stats[:, bass.ds(i * (2 * Q * 6) + ((r + OUTPUT.ahead["bn2"]) * Q + 2) * 6, 6)],
                                       x3[:, s.parity, 2, :]).then_inc(dve_done, 1)
                dve.wait_ge(pool_done, at("bn1", "o1"))
                if on("bn1"):
                    nc.vector.bn_stats(stats[:, bass.ds(i * (2 * Q * 6) + ((r + OUTPUT.ahead["bn1"]) * Q + 1) * 6, 6)],
                                       x3[:, s.parity, 1, :]).then_inc(dve_done, 1)
                if on("bn0"):
                    nc.vector.bn_stats(stats[:, bass.ds(i * (2 * Q * 6) + ((r + OUTPUT.ahead["bn0"]) * Q + 0) * 6, 6)],
                                       x3[:, s.parity, 0, :]).then_inc(dve_done, 1)
            dve.sem_inc(dve_done, 1)
            OUTPUT.run(dve, slot)


PARTS3 = ("r", "i")
C2 = P // 2
GATES = ("f", "i", "d")
KAREA = 49
RECURRENCE_STEPS = {
    "pe": [("mA_i", 1), ("mi_r", 0), ("mf_i", 1), ("md_i", 1), ("md_r", 1), ("mf_r", 1), ("mi_i", 1), ("mH_r", 0),
        ("mH_i", 0), ("mB_r", 1), ("mA_r", 2), ("mB_i", 1)],
    "act": [("det4", 0), ("det8", 0), ("tau4sq", 0), ("sq_i", 1), ("sq_r", 1), ("i_r", 0), ("lnd", 0), ("tau8sq", 0),
        ("lnA", 1), ("mag", 1), ("rd", 0), ("expm", 1), ("sd_i", 1), ("sd_r", 1), ("f_i", 1), ("f_r", 1),
        ("log_r", 1), ("log_i", 1), ("lnw", 1), ("scale", 1), ("scale2", 1), ("out_r", 0), ("i_i", 1), ("tausq", 1),
        ("out_i", 0), ("det2", 1), ("tau2sq", 1)],
    "pool": [("dif", 0), ("u4", 0), ("u8", 0), ("Bx_i", 0), ("g_i", 1), ("inp_r", 0), ("P2", 0), ("P4", 0),
        ("Ah_r", 0), ("Ah_i", 0), ("ad", 0), ("h1_r", 0), ("fsum", 1), ("h1_i", 0), ("A2f", 1), ("tau", 1)],
    "dve": [("Bx1", 0), ("Bx3", 0), ("tau4", 0), ("Bx2", 0), ("Bx4", 0), ("g_r", 1), ("tau8", 0), ("Bx_r", 0),
        ("gate_r", 0), ("A2", 1), ("inp_i", 0), ("u16", 0), ("tau16", 0), ("tu", 0), ("P1", 0), ("v", 0), ("P3", 0),
        ("num", 0), ("alpha", 0), ("y_r", 0), ("magexp", 1), ("beta", 0), ("h2_r", 0), ("w", 1), ("y_i", 0),
        ("fprod", 1), ("h2_i", 0), ("sp_i", 1), ("As_r", 1), ("As_i", 1), ("det", 1), ("sp_r", 1), ("gate_i", 1),
        ("tau2", 1)],
    "sp": [("table", 2), ("x_r", 2), ("x_i", 2), ("st_r", 0), ("st_i", 0)],
}
RECURRENCE = Schedule(TOK // 2 // CH, -2, RECURRENCE_STEPS)
AHEAD = RECURRENCE.ahead


def recurrence_weights(nc, d, W, affine):
    with ExitStack() as ctx:
        sb = lambda n, s: ctx.enter_context(nc.sbuf_tensor("h_raw_" + n, s, F32))
        new_sem = ctx.enter_context(phase_semaphores(nc))
        sem = lambda n: new_sem("h_w_" + n)
        ri, ir = sb("ri", [2 * KAREA, 2, C2]), sb("ir", [2 * KAREA, 2, C2])
        sign = sb("sign", [2 * KAREA, 2])
        zeroed, loaded, chain = sem("zeroed"), sem("loaded"), sem("chain")
        block = ctx.enter_context(nc.Block())
        count = [0]

        @block.sync
        def _(sp):
            def load(to, of):
                sp.dma_start(to, of).then_inc(loaded, 16)
                count[0] += 16
            with nc.allow_non_contiguous_dma(reason="columns of one element"):
                load(sign[:, :], d["c_sign"])
                for k, name in enumerate("AB"):
                    re, im = d[f"L3_conv_{name}_real"], d[f"L3_conv_{name}_imag"]
                    load(ri[0:KAREA, k, :], re), load(ri[KAREA:2 * KAREA, k, :], im)
                    load(ir[0:KAREA, k, :], im), load(ir[KAREA:2 * KAREA, k, :], re)
                sp.wait_ge(zeroed, 1)
                for blk in range(2):
                    to = slice(blk * C2, (blk + 1) * C2)
                    for o in range(2):
                        of = slice(o * C2, (o + 1) * C2)
                        for g, gate in enumerate(GATES):
                            for s in range(2):
                                load(W["gates"][to, g, o, s, to], d["L3_conv_W" + gate][s * C2:(s + 1) * C2, of])
                            load(W["g_off"][to, 2 * g + o:2 * g + o + 1], d["L3_conv_b" + gate][of, :])
                        load(W["gn"][to, 2 * o:2 * o + 2], affine[of, 0:2])
            sp.wait_ge(loaded, count[0])

        @block.vector
        def _(dve):
            link = linker(dve, chain)
            nc.vector.memset(W["gates"][:, :, :, :, :], 0.0).then_inc(zeroed, 1)
            dve.wait_ge(loaded, count[0])
            link(nc.vector.tensor_scalar(W["g_off"][:, 0:2], W["g_off"][:, 0:2], 2.0, None, ALU.add))
            link(nc.vector.memset(W["tiny"][:, :], 1e-8))
            link(nc.vector.memset(W["floor"][:, :], 1e-36))
            link(nc.vector.tensor_scalar(W["gates"][:, 2, :, :, :], W["gates"][:, 2, :, :, :], -1.0, None, ALU.mult))
            link(nc.vector.tensor_scalar(W["g_off"][:, 4:6], W["g_off"][:, 4:6], -1.0, None, ALU.mult))
            for k in range(2):
                for part, raw in enumerate((ri, ir)):
                    own, far = W["kern"][:, 2 * k + part, 0:C2], W["kern"][:, 2 * k + part, C2:P]
                    link(nc.vector.tensor_scalar(own, raw[:, k, :], sign[:, 0:1] if part else 1.0, None, ALU.mult))
                    link(nc.vector.tensor_scalar(far, own, sign[:, 1:2], None, ALU.mult))
            link(nc.vector.tensor_scalar(W["kern"][:, 2:4, :], W["kern"][:, 2:4, :], -0.1, None, ALU.mult))


def recurrence(nc, d, x3_t, out, W, const, ps):
    F = CH
    HALFTOK = TOK // 2
    ITERS = RECURRENCE.rounds
    MUL, ADD, SUB = ALU.mult, ALU.add, ALU.subtract
    with ExitStack() as ctx:
        new_sem = ctx.enter_context(phase_semaphores(nc))
        sem = lambda n: new_sem("h_" + n)
        sb = lambda n, depth: ctx.enter_context(nc.sbuf_tensor("h_" + n, [P, depth, F], F32))
        two = ("x_r x_i g_r g_i f_r f_i i_r i_i sq_r expm As_r As_i inp_r inp_i fsum fprod tau det out_r out_i").split()
        one = ("sq_i lnA scale sd_r sd_i Bx1 Bx2 Bx3 Bx4 tausq tau2sq det2 det4 tau4sq det8 tau8sq u4 tu num dif ad "
               "P1 P2 P3 P4 h2_r h2_i").split()
        T = {n: sb(n, 2) for n in two} | {n: sb(n, 1) for n in one}
        for value, place in (("A2", "sq_r"), ("mag", "lnA"), ("magexp", "expm"), ("w", "expm"), ("lnw", "expm"),
                            ("scale2", "expm"), ("log_r", "sd_r"), ("sp_r", "sd_r"), ("gate_r", "sd_r"),
                            ("log_i", "sd_i"), ("sp_i", "sd_i"), ("gate_i", "sd_i"), ("Bx_r", "Bx1"), ("Bx_i", "Bx3"),
                            ("A2f", "fprod"), ("tau2", "tausq"), ("tau4", "tau2sq"), ("tau8", "tau4sq"),
                            ("tau16", "tau8sq"), ("u8", "u4"), ("u16", "u4"), ("v", "tu"), ("lnd", "dif"),
                            ("rd", "dif"), ("alpha", "num"), ("beta", "ad"), ("Ah_r", "P1"), ("Ah_i", "P3"),
                            ("y_r", "P1"), ("h1_r", "P1"), ("y_i", "P3"), ("h1_i", "P3")):
            T[value] = T[place]
        T["table"] = ctx.enter_context(nc.sbuf_tensor("h_table", [2 * KAREA, 2, F], F32))
        BANK = {"bd_r": 0, "bd_i": 1, "bf_r": 2, "bi_r": 2, "bf_i": 3, "bi_i": 3, "bA_r": 4, "bA_i": 5, "bB_r": 6,
                "bH_r": 6, "bB_i": 7, "bH_i": 7}
        pe_done, act_done, pool_done, dve_done = sem("pe_done"), sem("act_done"), sem("pool_done"), sem("dve_done")
        x_in, table_in, out_st = [[sem(f"{n}{r}") for r in range(2)] for n in ("x_in", "table_in", "out_st")]
        pool_passed, sp_passed = sem("pool_passed"), sem("sp_passed")
        block = ctx.enter_context(nc.Block())

        def place(slot, name):
            if name in BANK:
                return ps[:, BANK[name], :]
            return T[name][:, slot.parity if T[name].shape[1] == 2 else 0, :]

        def gate_off(g, o):
            return W["g_off"][:, 2 * g + o:2 * g + o + 1]

        @block.sync
        def _(sp):
            def slot(i, r):
                s = Slot(RECURRENCE, sp, None, i, r)
                at = s.at

                def load_x(step, o):
                    if s.runs(step):
                        for blk in range(2):
                            sp.dma_start(T[step][blk * C2:(blk + 1) * C2, (r + AHEAD[step]) % 2, :],
                                         x3_t[o * C2:(o + 1) * C2, bass.ds(i * (2 * F) + (blk * HALFTOK + (r + AHEAD[step]) * F), F)]
                                         ).then_inc(x_in[(r + AHEAD[step]) % 2], 16)

                def load_table(step):
                    if s.runs(step):
                        sp.dma_start(T["table"][:, (r + AHEAD[step]) % 2, :],
                                     d["c_table"][:, bass.ds(i * (2 * F) + (r + AHEAD[step]) * F,
                                                             F)]).then_inc(table_in[(r + AHEAD[step]) % 2], 16)

                def store(step, value, o):
                    if s.runs(step):
                        for blk in range(2):
                            sp.dma_start(out[o * C2:(o + 1) * C2,
                                             bass.ds(i * (2 * F) + (blk * HALFTOK + (r + AHEAD[step]) * F), F)],
                                         T[value][blk * C2:(blk + 1) * C2, (r + AHEAD[step]) % T[value].shape[1], :]
                                         ).then_inc(out_st[(r + AHEAD[step]) % 2], 16)

                sp.wait_ge(pe_done, at("table", "mB_i", 2))
                sp.sem_inc(sp_passed, 1)
                load_table("table")
                sp.wait_ge(dve_done, at("x_r", "g_r", 2))
                sp.sem_inc(sp_passed, 1)
                sp.wait_ge(pe_done, at("x_r", "mH_r", 2))
                sp.sem_inc(sp_passed, 1)
                load_x("x_r", 0)
                sp.wait_ge(pool_done, at("x_i", "g_i", 2))
                sp.sem_inc(sp_passed, 1)
                sp.wait_ge(pe_done, at("x_i", "mH_i", 2))
                sp.sem_inc(sp_passed, 1)
                load_x("x_i", 1)
                sp.wait_ge(act_done, at("st_r", "out_r"))
                sp.sem_inc(sp_passed, 1)
                store("st_r", "out_r", 0)
                sp.wait_ge(act_done, at("st_i", "out_i"))
                sp.sem_inc(sp_passed, 1)
                store("st_i", "out_i", 1)
            RECURRENCE.run(sp, slot)
            for r in range(2):
                sp.wait_ge(out_st[r], ITERS // 2 * 64)

        @block.tensor
        def _(pe):
            def slot(i, r):
                s = Slot(RECURRENCE, pe, pe_done, i, r)
                at, on, t = s.at, s.on, lambda name: place(s, name)
                pe.wait_ge(act_done, at("mA_i", "sq_i", 1))
                pe.wait_ge(dve_done, at("mA_i", "As_i", 1))
                if s.runs("mA_i"):
                    pe.wait_ge(table_in[s.side("mA_i")], s.moved("mA_i", 16))
                if on("mA_i"):
                    nc.tensor.matmul(t("bA_i"), W["kern"][:, 1, :], t("table"), start=True, stop=True).then_inc(pe_done, 1)
                pe.wait_ge(pool_done, at("mi_r", "g_i"))
                pe.wait_ge(act_done, at("mi_r", "f_r"))
                if on("mi_r"):
                    nc.tensor.matmul(t("bi_r"), W["gates"][:, 1, 0, 0, :], t("g_r"), start=True, stop=False)
                    nc.tensor.matmul(t("bi_r"), W["gates"][:, 1, 0, 1, :], t("g_i"), start=False, stop=True).then_inc(pe_done, 1)
                pe.wait_ge(dve_done, at("mf_i", "g_r"))
                pe.wait_ge(pool_done, at("mf_i", "g_i"))
                pe.wait_ge(act_done, at("mf_i", "i_i", 1))
                if on("mf_i"):
                    nc.tensor.matmul(t("bf_i"), W["gates"][:, 0, 1, 0, :], t("g_r"), start=True, stop=False)
                    nc.tensor.matmul(t("bf_i"), W["gates"][:, 0, 1, 1, :], t("g_i"), start=False, stop=True).then_inc(pe_done, 1)
                if on("md_i"):
                    nc.tensor.matmul(t("bd_i"), W["gates"][:, 2, 1, 0, :], t("g_r"), start=True, stop=False)
                    nc.tensor.matmul(t("bd_i"), W["gates"][:, 2, 1, 1, :], t("g_i"), start=False, stop=True).then_inc(pe_done, 1)
                if on("md_r"):
                    nc.tensor.matmul(t("bd_r"), W["gates"][:, 2, 0, 0, :], t("g_r"), start=True, stop=False)
                    nc.tensor.matmul(t("bd_r"), W["gates"][:, 2, 0, 1, :], t("g_i"), start=False, stop=True).then_inc(pe_done, 1)
                pe.wait_ge(act_done, at("mf_r", "i_r", 1))
                if on("mf_r"):
                    nc.tensor.matmul(t("bf_r"), W["gates"][:, 0, 0, 0, :], t("g_r"), start=True, stop=False)
                    nc.tensor.matmul(t("bf_r"), W["gates"][:, 0, 0, 1, :], t("g_i"), start=False, stop=True).then_inc(pe_done, 1)
                pe.wait_ge(act_done, at("mi_i", "f_i"))
                if on("mi_i"):
                    nc.tensor.matmul(t("bi_i"), W["gates"][:, 1, 1, 0, :], t("g_r"), start=True, stop=False)
                    nc.tensor.matmul(t("bi_i"), W["gates"][:, 1, 1, 1, :], t("g_i"), start=False, stop=True).then_inc(pe_done, 1)
                pe.wait_ge(pool_done, at("mH_r", "h1_r"))
                pe.wait_ge(dve_done, at("mH_r", "h2_r"))
                if s.runs("mH_r"):
                    pe.wait_ge(x_in[s.side("mH_r")], s.moved("mH_r", 64))
                if on("mH_r"):
                    nc.tensor.matmul(t("bH_r"), const["ident"][:, :], t("h1_r"), start=True, stop=False)
                    nc.tensor.matmul(t("bH_r"), const["ident"][:, :], t("h2_r"), start=False, stop=False)
                    nc.tensor.matmul(t("bH_r"), const["ident"][:, :], t("x_r"), start=False, stop=True).then_inc(pe_done, 1)
                pe.wait_ge(pool_done, at("mH_i", "h1_i"))
                pe.wait_ge(dve_done, at("mH_i", "h2_i"))
                if s.runs("mH_i"):
                    pe.wait_ge(x_in[s.side("mH_i")], s.moved("mH_i", 64))
                if on("mH_i"):
                    nc.tensor.matmul(t("bH_i"), const["ident"][:, :], t("h1_i"), start=True, stop=False)
                    nc.tensor.matmul(t("bH_i"), const["ident"][:, :], t("h2_i"), start=False, stop=False)
                    nc.tensor.matmul(t("bH_i"), const["ident"][:, :], t("x_i"), start=False, stop=True).then_inc(pe_done, 1)
                pe.wait_ge(act_done, at("mB_r", "out_r", 1))
                if s.runs("mB_r"):
                    pe.wait_ge(table_in[s.side("mB_r")], s.moved("mB_r", 16))
                if on("mB_r"):
                    nc.tensor.matmul(t("bB_r"), W["kern"][:, 2, :], t("table"), start=True, stop=True).then_inc(pe_done, 1)
                pe.wait_ge(dve_done, at("mA_r", "As_r", 1))
                if s.runs("mA_r"):
                    pe.wait_ge(table_in[s.side("mA_r")], s.moved("mA_r", 16))
                if on("mA_r"):
                    nc.tensor.matmul(t("bA_r"), W["kern"][:, 0, :], t("table"), start=True, stop=True).then_inc(pe_done, 1)
                pe.wait_ge(act_done, at("mB_i", "out_i", 1))
                if s.runs("mB_i"):
                    pe.wait_ge(table_in[s.side("mB_i")], s.moved("mB_i", 16))
                if on("mB_i"):
                    nc.tensor.matmul(t("bB_i"), W["kern"][:, 3, :], t("table"), start=True, stop=True).then_inc(pe_done, 1)
            pe.sem_inc(pe_done, 1)
            RECURRENCE.run(pe, slot)

        @block.scalar
        def _(act):
            def slot(i, r):
                s = Slot(RECURRENCE, act, act_done, i, r)
                at, on, t = s.at, s.on, lambda name: place(s, name)
                act.wait_ge(act_done, at("det4", "det2"))
                act.wait_ge(dve_done, at("det4", "tau8", 1))
                if on("det4"):
                    nc.scalar.activation(t("det4"), t("det2"), ACT.Square).then_inc(act_done, 1)
                act.wait_ge(act_done, at("det8", "det4"))
                act.wait_ge(dve_done, at("det8", "tau16", 1))
                if on("det8"):
                    nc.scalar.activation(t("det8"), t("det4"), ACT.Square).then_inc(act_done, 1)
                act.wait_ge(dve_done, at("tau4sq", "tau4"))
                if on("tau4sq"):
                    nc.scalar.activation(t("tau4sq"), t("tau4"), ACT.Square).then_inc(act_done, 1)
                act.wait_ge(pe_done, at("sq_i", "mA_i"))
                if on("sq_i"):
                    nc.scalar.activation(t("sq_i"), t("bA_i"), ACT.Square).then_inc(act_done, 1)
                act.wait_ge(pool_done, at("sq_r", "A2f", 2))
                if on("sq_r"):
                    nc.scalar.activation(t("sq_r"), t("bA_r"), ACT.Square).then_inc(act_done, 1)
                act.wait_ge(pe_done, at("i_r", "mi_r"))
                if on("i_r"):
                    nc.scalar.activation(t("i_r"), t("bi_r"), ACT.Sigmoid, bias=gate_off(1, 0)).then_inc(act_done, 1)
                load_log_exp(nc, act)
                act.wait_ge(pool_done, at("lnd", "dif"))
                if on("lnd"):
                    nc.scalar.activation(t("lnd"), t("dif"), ACT.Ln, scale=-1.0, bias=1.0).then_inc(act_done, 1)
                act.wait_ge(dve_done, at("tau8sq", "tau8"))
                if on("tau8sq"):
                    nc.scalar.activation(t("tau8sq"), t("tau8"), ACT.Square).then_inc(act_done, 1)
                act.wait_ge(dve_done, at("lnA", "A2"))
                if on("lnA"):
                    nc.scalar.activation(t("lnA"), t("A2"), ACT.Ln, bias=W["tiny"][:, 0:1]).then_inc(act_done, 1)
                act.wait_ge(act_done, at("mag", "lnA"))
                if on("mag"):
                    nc.scalar.activation(t("mag"), t("lnA"), ACT.Exp, scale=0.5).then_inc(act_done, 1)
                if on("rd"):
                    nc.scalar.activation(t("rd"), t("lnd"), ACT.Exp, scale=-1.0).then_inc(act_done, 1)
                act.wait_ge(act_done, at("expm", "mag"))
                if on("expm"):
                    nc.scalar.activation(t("expm"), t("mag"), ACT.Exp, scale=-1.0).then_inc(act_done, 1)
                act.wait_ge(pe_done, at("sd_i", "md_i"))
                act.wait_ge(dve_done, at("sd_i", "inp_i", 1))
                if on("sd_i"):
                    nc.scalar.activation(t("sd_i"), t("bd_i"), ACT.Sigmoid, bias=gate_off(2, 1)).then_inc(act_done, 1)
                act.wait_ge(pe_done, at("sd_r", "md_r"))
                act.wait_ge(pool_done, at("sd_r", "inp_r", 1))
                if on("sd_r"):
                    nc.scalar.activation(t("sd_r"), t("bd_r"), ACT.Sigmoid, bias=gate_off(2, 0)).then_inc(act_done, 1)
                if on("f_i"):
                    nc.scalar.activation(t("f_i"), t("bf_i"), ACT.Sigmoid, bias=gate_off(0, 1)).then_inc(act_done, 1)
                act.wait_ge(pe_done, at("f_r", "mf_r"))
                if on("f_r"):
                    nc.scalar.activation(t("f_r"), t("bf_r"), ACT.Sigmoid, bias=gate_off(0, 0)).then_inc(act_done, 1)
                act.wait_ge(act_done, at("log_r", "sd_r"))
                if on("log_r"):
                    nc.scalar.activation(t("log_r"), t("sd_r"), ACT.Ln, bias=W["floor"][:, 0:1]).then_inc(act_done, 1)
                if on("log_i"):
                    nc.scalar.activation(t("log_i"), t("sd_i"), ACT.Ln, bias=W["floor"][:, 0:1]).then_inc(act_done, 1)
                act.wait_ge(dve_done, at("lnw", "w"))
                if on("lnw"):
                    nc.scalar.activation(t("lnw"), t("w"), ACT.Ln).then_inc(act_done, 1)
                act.wait_ge(act_done, at("scale", "lnw"))
                if on("scale"):
                    nc.scalar.activation(t("scale"), t("lnw"), ACT.Exp, scale=-1.0).then_inc(act_done, 1)
                if on("scale2"):
                    nc.scalar.activation(t("scale2"), t("lnw"), ACT.Exp, scale=-2.0).then_inc(act_done, 1)
                act.wait_ge(pe_done, at("out_r", "mH_r"))
                if s.runs("out_r", 2):
                    act.wait_ge(out_st[s.side("out_r", 2)], s.moved("out_r", 64, 2))
                if on("out_r"):
                    nc.scalar.activation(t("out_r"), t("bH_r"), ACT.Identity).then_inc(act_done, 1)
                if on("i_i"):
                    nc.scalar.activation(t("i_i"), t("bi_i"), ACT.Sigmoid, bias=gate_off(1, 1)).then_inc(act_done, 1)
                act.wait_ge(pool_done, at("tausq", "tau"))
                if on("tausq"):
                    nc.scalar.activation(t("tausq"), t("tau"), ACT.Square).then_inc(act_done, 1)
                act.wait_ge(pe_done, at("out_i", "mH_i"))
                if s.runs("out_i", 2):
                    act.wait_ge(out_st[s.side("out_i", 2)], s.moved("out_i", 64, 2))
                if on("out_i"):
                    nc.scalar.activation(t("out_i"), t("bH_i"), ACT.Identity).then_inc(act_done, 1)
                act.wait_ge(dve_done, at("det2", "det"))
                if on("det2"):
                    nc.scalar.activation(t("det2"), t("det"), ACT.Square).then_inc(act_done, 1)
                act.wait_ge(dve_done, at("tau2sq", "tau2"))
                if on("tau2sq"):
                    nc.scalar.activation(t("tau2sq"), t("tau2"), ACT.Square).then_inc(act_done, 1)
            act.sem_inc(act_done, 1)
            RECURRENCE.run(act, slot)

        @block.gpsimd
        def _(pool):
            def slot(i, r):
                s = Slot(RECURRENCE, pool, pool_done, i, r)
                at, on, t = s.at, s.on, lambda name: place(s, name)
                pool.wait_ge(pool_done, at("dif", "tau"))
                pool.wait_ge(dve_done, at("dif", "det"))
                pool.wait_ge(act_done, at("dif", "rd", 1))
                pool.sem_inc(pool_passed, 1)
                if on("dif"):
                    nc.gpsimd.tensor_tensor(t("dif"), t("tau"), t("det"), SUB).then_inc(pool_done, 1)
                pool.wait_ge(dve_done, at("u4", "tau2"))
                pool.sem_inc(pool_passed, 1)
                if on("u4"):
                    nc.gpsimd.tensor_tensor(t("u4"), t("tau"), t("tau2"), MUL).then_inc(pool_done, 1)
                pool.wait_ge(pool_done, at("u8", "u4"))
                pool.wait_ge(dve_done, at("u8", "tau4"))
                pool.sem_inc(pool_passed, 1)
                if on("u8"):
                    nc.gpsimd.tensor_tensor(t("u8"), t("u4"), t("tau4"), MUL).then_inc(pool_done, 1)
                pool.wait_ge(dve_done, at("Bx_i", "Bx4"))
                pool.sem_inc(pool_passed, 1)
                if on("Bx_i"):
                    nc.gpsimd.tensor_tensor(t("Bx_i"), t("Bx3"), t("Bx4"), ADD).then_inc(pool_done, 1)
                pool.wait_ge(pe_done, at("g_i", "mi_r", 2))
                if s.runs("g_i"):
                    pool.wait_ge(x_in[s.side("g_i")], s.moved("g_i", 64))
                pool.sem_inc(pool_passed, 1)
                if on("g_i"):
                    nc.gpsimd.tensor_scalar(t("g_i"), t("x_i"), W["gn"][:, 2:3], W["gn"][:, 3:4], MUL, ADD).then_inc(pool_done, 1)
                pool.wait_ge(dve_done, at("inp_r", "gate_r"))
                pool.sem_inc(pool_passed, 1)
                if on("inp_r"):
                    nc.gpsimd.tensor_tensor(t("inp_r"), t("Bx_r"), t("gate_r"), MUL).then_inc(pool_done, 1)
                pool.wait_ge(dve_done, at("P2", "inp_i"))
                pool.sem_inc(pool_passed, 1)
                if on("P2"):
                    nc.gpsimd.tensor_tensor(t("P2"), t("As_i"), t("inp_i"), MUL).then_inc(pool_done, 1)
                pool.wait_ge(pool_done, at("P4", "inp_r"))
                pool.sem_inc(pool_passed, 1)
                if on("P4"):
                    nc.gpsimd.tensor_tensor(t("P4"), t("As_i"), t("inp_r"), MUL).then_inc(pool_done, 1)
                pool.wait_ge(dve_done, at("Ah_r", "P1"))
                pool.wait_ge(pool_done, at("Ah_r", "P2"))
                pool.sem_inc(pool_passed, 1)
                if on("Ah_r"):
                    nc.gpsimd.tensor_tensor(t("Ah_r"), t("P1"), t("P2"), SUB).then_inc(pool_done, 1)
                pool.wait_ge(dve_done, at("Ah_i", "P3"))
                pool.wait_ge(pool_done, at("Ah_i", "P4"))
                pool.sem_inc(pool_passed, 1)
                if on("Ah_i"):
                    nc.gpsimd.tensor_tensor(t("Ah_i"), t("P3"), t("P4"), ADD).then_inc(pool_done, 1)
                pool.wait_ge(dve_done, at("ad", "alpha"))
                pool.sem_inc(pool_passed, 1)
                if on("ad"):
                    nc.gpsimd.tensor_tensor(t("ad"), t("alpha"), t("det"), MUL).then_inc(pool_done, 1)
                pool.wait_ge(dve_done, at("h1_r", "y_r"))
                pool.sem_inc(pool_passed, 1)
                if on("h1_r"):
                    nc.gpsimd.tensor_tensor(t("h1_r"), t("y_r"), t("alpha"), MUL).then_inc(pool_done, 1)
                pool.wait_ge(act_done, at("fsum", "f_r"))
                pool.sem_inc(pool_passed, 1)
                if on("fsum"):
                    nc.gpsimd.tensor_tensor(t("fsum"), t("f_r"), t("f_i"), ADD).then_inc(pool_done, 1)
                pool.wait_ge(dve_done, at("h1_i", "y_i"))
                pool.sem_inc(pool_passed, 1)
                if on("h1_i"):
                    nc.gpsimd.tensor_tensor(t("h1_i"), t("y_i"), t("alpha"), MUL).then_inc(pool_done, 1)
                pool.wait_ge(dve_done, at("A2f", "fprod"))
                pool.sem_inc(pool_passed, 1)
                if on("A2f"):
                    nc.gpsimd.tensor_tensor(t("A2f"), t("A2"), t("fprod"), MUL).then_inc(pool_done, 1)
                pool.wait_ge(pool_done, at("tau", "fsum"))
                pool.wait_ge(dve_done, at("tau", "As_r"))
                pool.sem_inc(pool_passed, 1)
                if on("tau"):
                    nc.gpsimd.tensor_tensor(t("tau"), t("fsum"), t("As_r"), MUL).then_inc(pool_done, 1)
            pool.sem_inc(pool_done, 1)
            RECURRENCE.run(pool, slot)

        @block.vector
        def _(dve):
            def slot(i, r):
                s = Slot(RECURRENCE, dve, dve_done, i, r)
                at, on, t = s.at, s.on, lambda name: place(s, name)
                dve.wait_ge(pe_done, at("Bx1", "mB_r"))
                dve.wait_ge(dve_done, at("Bx1", "g_r"))
                dve.wait_ge(pool_done, at("Bx1", "inp_r", 1))
                if on("Bx1"):
                    nc.vector.tensor_tensor(t("Bx1"), t("bB_r"), t("g_r"), MUL).then_inc(dve_done, 1)
                if on("Bx3"):
                    nc.vector.tensor_tensor(t("Bx3"), t("bB_r"), t("g_i"), MUL).then_inc(dve_done, 1)
                dve.wait_ge(act_done, at("tau4", "tau2sq"))
                if on("tau4"):
                    nc.vector.scalar_tensor_tensor(t("tau4"), t("det2"), -2.0, t("tau2sq"), MUL, ADD).then_inc(dve_done, 1)
                dve.wait_ge(pe_done, at("Bx2", "mB_i"))
                if on("Bx2"):
                    nc.vector.tensor_tensor(t("Bx2"), t("bB_i"), t("g_i"), MUL).then_inc(dve_done, 1)
                if on("Bx4"):
                    nc.vector.tensor_tensor(t("Bx4"), t("bB_i"), t("g_r"), MUL).then_inc(dve_done, 1)
                if s.runs("g_r"):
                    dve.wait_ge(x_in[s.side("g_r")], s.moved("g_r", 64))
                if on("g_r"):
                    nc.vector.tensor_scalar(t("g_r"), t("x_r"), W["gn"][:, 0:1], W["gn"][:, 1:2], MUL, ADD).then_inc(dve_done, 1)
                dve.wait_ge(act_done, at("tau8", "tau4sq"))
                if on("tau8"):
                    nc.vector.scalar_tensor_tensor(t("tau8"), t("det4"), -2.0, t("tau4sq"), MUL, ADD).then_inc(dve_done, 1)
                dve.wait_ge(dve_done, at("Bx_r", "Bx2"))
                if on("Bx_r"):
                    nc.vector.tensor_tensor(t("Bx_r"), t("Bx1"), t("Bx2"), SUB).then_inc(dve_done, 1)
                dve.wait_ge(act_done, at("gate_r", "i_r"))
                if on("gate_r"):
                    nc.vector.tensor_tensor(t("gate_r"), t("sp_r"), t("i_r"), MUL).then_inc(dve_done, 1)
                if on("A2"):
                    nc.vector.tensor_tensor(t("A2"), t("sq_r"), t("sq_i"), ADD).then_inc(dve_done, 1)
                dve.wait_ge(pool_done, at("inp_i", "Bx_i"))
                if on("inp_i"):
                    nc.vector.tensor_tensor(t("inp_i"), t("Bx_i"), t("gate_i"), MUL).then_inc(dve_done, 1)
                dve.wait_ge(dve_done, at("u16", "tau8"))
                if on("u16"):
                    nc.vector.tensor_tensor(t("u16"), t("u8"), t("tau8"), MUL).then_inc(dve_done, 1)
                dve.wait_ge(act_done, at("tau16", "tau8sq"))
                if on("tau16"):
                    nc.vector.scalar_tensor_tensor(t("tau16"), t("det8"), -2.0, t("tau8sq"), MUL, ADD).then_inc(dve_done, 1)
                dve.wait_ge(dve_done, at("tu", "u16"))
                if on("tu"):
                    nc.vector.tensor_tensor(t("tu"), t("tau"), t("u16"), MUL).then_inc(dve_done, 1)
                dve.wait_ge(pool_done, at("P1", "inp_r"))
                if on("P1"):
                    nc.vector.tensor_tensor(t("P1"), t("As_r"), t("inp_r"), MUL).then_inc(dve_done, 1)
                dve.wait_ge(dve_done, at("v", "tu"))
                if on("v"):
                    nc.vector.tensor_tensor(t("v"), t("tu"), t("tau16"), SUB).then_inc(dve_done, 1)
                if on("P3"):
                    nc.vector.tensor_tensor(t("P3"), t("As_r"), t("inp_i"), MUL).then_inc(dve_done, 1)
                dve.wait_ge(dve_done, at("num", "v"))
                if on("num"):
                    nc.vector.scalar_tensor_tensor(t("num"), t("v"), 0.5, t("u16"), MUL, SUB).then_inc(dve_done, 1)
                dve.wait_ge(dve_done, at("alpha", "num"))
                dve.wait_ge(act_done, at("alpha", "rd"))
                if on("alpha"):
                    nc.vector.scalar_tensor_tensor(t("alpha"), t("num"), 1.0, t("rd"), ADD, MUL).then_inc(dve_done, 1)
                dve.wait_ge(pool_done, at("y_r", "Ah_r"))
                if on("y_r"):
                    nc.vector.tensor_tensor(t("y_r"), t("Ah_r"), t("f_r"), MUL).then_inc(dve_done, 1)
                dve.wait_ge(act_done, at("magexp", "expm"))
                if on("magexp"):
                    nc.vector.scalar_tensor_tensor(t("magexp"), t("mag"), 1e-8, t("expm"), ADD, MUL).then_inc(dve_done, 1)
                dve.wait_ge(pool_done, at("beta", "ad"))
                if on("beta"):
                    nc.vector.scalar_tensor_tensor(t("beta"), t("v"), 0.5, t("ad"), MUL, SUB).then_inc(dve_done, 1)
                dve.wait_ge(dve_done, at("h2_r", "beta"))
                if on("h2_r"):
                    nc.vector.scalar_tensor_tensor(t("h2_r"), t("beta"), 1.0, t("inp_r"), ADD, MUL).then_inc(dve_done, 1)
                if on("w"):
                    nc.vector.scalar_tensor_tensor(t("w"), t("mag"), 1e-8, t("magexp"), ADD, ADD).then_inc(dve_done, 1)
                if on("y_i"):
                    nc.vector.tensor_tensor(t("y_i"), t("Ah_i"), t("f_i"), MUL).then_inc(dve_done, 1)
                dve.wait_ge(act_done, at("fprod", "f_r"))
                if on("fprod"):
                    nc.vector.tensor_tensor(t("fprod"), t("f_r"), t("f_i"), MUL).then_inc(dve_done, 1)
                if on("h2_i"):
                    nc.vector.scalar_tensor_tensor(t("h2_i"), t("beta"), 1.0, t("inp_i"), ADD, MUL).then_inc(dve_done, 1)
                dve.wait_ge(pe_done, at("sp_i", "md_i"))
                dve.wait_ge(act_done, at("sp_i", "log_i"))
                if on("sp_i"):
                    nc.vector.scalar_tensor_tensor(t("sp_i"), t("bd_i"), gate_off(2, 1), t("log_i"), ADD,
                                                   ALU.min).then_inc(dve_done, 1)
                dve.wait_ge(act_done, at("As_r", "scale"))
                if on("As_r"):
                    nc.vector.scalar_tensor_tensor(t("As_r"), t("bA_r"), 0.95, t("scale"), MUL, MUL).then_inc(dve_done, 1)
                if on("As_i"):
                    nc.vector.scalar_tensor_tensor(t("As_i"), t("bA_i"), 0.95, t("scale"), MUL, MUL).then_inc(dve_done, 1)
                dve.wait_ge(pool_done, at("det", "A2f"))
                dve.wait_ge(act_done, at("det", "scale2"))
                if on("det"):
                    nc.vector.scalar_tensor_tensor(t("det"), t("A2f"), 0.95 * 0.95, t("scale2"), MUL, MUL).then_inc(dve_done, 1)
                dve.wait_ge(pe_done, at("sp_r", "md_r"))
                if on("sp_r"):
                    nc.vector.scalar_tensor_tensor(t("sp_r"), t("bd_r"), gate_off(2, 0), t("log_r"), ADD,
                                                   ALU.min).then_inc(dve_done, 1)
                dve.wait_ge(dve_done, at("gate_i", "sp_i"))
                dve.wait_ge(act_done, at("gate_i", "i_i"))
                if on("gate_i"):
                    nc.vector.tensor_tensor(t("gate_i"), t("sp_i"), t("i_i"), MUL).then_inc(dve_done, 1)
                dve.wait_ge(act_done, at("tau2", "tausq"))
                dve.wait_ge(dve_done, at("tau2", "det"))
                if on("tau2"):
                    nc.vector.scalar_tensor_tensor(t("tau2"), t("det"), -2.0, t("tausq"), MUL, ADD).then_inc(dve_done, 1)
            dve.sem_inc(dve_done, 1)
            RECURRENCE.run(dve, slot)


def layer0(nc, d, z_t, bias_d, x_t, x1_t, stats, const, affine, ps):
    input_statistics(nc, x_t, stats)
    group_norm_affine(nc, "gn0", stats[:, 0:NCH * 6], const, affine, ps)
    with ExitStack() as layer:
        wsb = lambda n, s: layer.enter_context(nc.sbuf_tensor("w0_" + n, s, F32))
        W = {n: wsb(n, [P, P]) for n in ("Wq", "Wk", "Wv", "Wg", "Wo")}
        W["Wb"] = wsb("Wb", [P, HEADS])
        W |= {n: wsb(n, [P, 1]) for n in ("q_off", "k_off", "g_off", "b_off", "bo")}
        W["v_off"] = wsb("v_off", [P, HALF, P])
        attention_weights(nc, d, W, ps)
        attention_norm(nc, x_t, z_t, bias_d, W, const, affine, ps)
        row_attention(nc, x_t, z_t, bias_d, x1_t, W, const, stats, ps)


def layer1(nc, d, x1_t, x2_t, stats, const, affine, ps):
    group_norm_affine(nc, "gn1", stats[:, :], const, affine, ps)
    row_scan(nc, d, x1_t, x2_t, affine, stats, ps)


def layer2(nc, d, ab_d, go_t, t_t, x2_t, x3_t, stats, const, affine, ps):
    with ExitStack() as layer:
        wsb = lambda n, s: layer.enter_context(nc.sbuf_tensor("w2_" + n, s, F32))
        W = {"W4": wsb("W4", [P, CH]), "Wg": wsb("Wg", [P, P]), "Wo": wsb("Wo", [P, P]), "g_off": wsb("g_off", [P, 1]),
             "o_off": wsb("o_off", [P, 1]), "bias4": wsb("bias4", [P, CH])}
        group_norm_affine(nc, "gn2", stats[:, :], const, affine, ps)
        triangle_weights(nc, d, W, ps)
        triangle_projections(nc, x2_t, ab_d, go_t, W, const, affine, ps)
        triangle_products(nc, ab_d, t_t, ps)
        triangle_output(nc, t_t, go_t, x2_t, x3_t, W, const, stats, ps)


def layer3(nc, d, x3_t, out, stats, const, affine, ps):
    with ExitStack() as layer:
        wsb = lambda n, s: layer.enter_context(nc.sbuf_tensor("w3_" + n, s, F32))
        W = {"gates": wsb("gates", [P, 3, 2, 2, P]), "g_off": wsb("g_off", [P, 6]), "gn": wsb("gn", [P, 4]),
             "kern": wsb("kern", [2 * KAREA, 4, P]), "tiny": wsb("tiny", [P, 1]), "floor": wsb("floor", [P, 1])}
        group_norm_affine(nc, "gn3", stats[:, 0:NCH * 6], const, affine, ps)
        recurrence_weights(nc, d, W, affine)
        recurrence(nc, d, x3_t, out, W, const, ps)


def layers_kernel(nc, d, out):
    scratch = lambda name, shape: nc.dram_tensor(name, shape, F32).ap()
    x_t, z_t, bias_d = d["x"], scratch("z_t", (P, TOK)), scratch("bias_d", (HEADS, TOK))
    x1_t, x2_t, x3_t, t_t, go_t = [scratch(n, (P, TOK)) for n in ("x1_t", "x2_t", "x3_t", "t_t", "go_t")]
    ab_d = scratch("ab_d", (2, HC, HALF, P, N * HW))
    with ExitStack() as ctx:
        sb = lambda n, s: ctx.enter_context(nc.sbuf_tensor(n, s, F32))
        ps = ctx.enter_context(nc.psum_tensor("ps", [P, 8, CH], F32))
        const = {n: sb("const_" + n, [P, P]) for n in ("ident", "center", "mean", "group_mean")}
        stats, affine = sb("stats", [P, N * 6]), sb("affine", [P, P + 3])
        const_in = nc.alloc_semaphore("const_in")
        with nc.Block() as block:
            @block.sync
            def _(sp):
                for n, t in const.items():
                    sp.dma_start(t[:, :], d["c_" + n]).then_inc(const_in, 16)
                sp.wait_ge(const_in, 16 * len(const))

        layer0(nc, d, z_t, bias_d, x_t, x1_t, stats, const, affine, ps)
        layer1(nc, d, x1_t, x2_t, stats, const, affine, ps)
        layer2(nc, d, ab_d, go_t, t_t, x2_t, x3_t, stats, const, affine, ps)
        layer3(nc, d, x3_t, out, stats, const, affine, ps)


def kernel(**inputs):
    import numpy as np
    import concourse.bacc as bacc
    from concourse import mybir as mb
    from concourse.bass_utils import run_bass_kernel_spmd

    nc = bacc.Bacc("TRN2", target_bir_lowering=False, num_devices=1)
    arrays, d = laid_out(inputs), {}
    for name, a in arrays.items():
        d[name] = nc.dram_tensor(name, a.shape, mb.dt.from_np(a.dtype), kind="ExternalInput").ap()
    out = nc.dram_tensor("out_t", (128, 65536), mb.dt.float32, kind="ExternalOutput").ap()
    layers_kernel(nc, d, out)
    r = run_bass_kernel_spmd(nc, [arrays], core_ids=[0])
    got = r.results[0]["out_t"]
    return np.ascontiguousarray(got.T).reshape(1, 256, 256, 128)


def laid_out(inputs):
    import numpy as np
    arrays = {}
    for name, a in inputs.items():
        a = np.asarray(a)
        if name == "x":
            a = a.reshape(-1, 128).T
        elif name == "L1_conv_W":
            a = a.transpose(1, 0, 2)
        elif a.ndim == 1:
            a = a.reshape(-1, 1)
        elif name.startswith("L2_conv_"):
            a = a.T
        elif name.startswith(("L3_conv_A", "L3_conv_B")):
            a = a.reshape(64, 49).T
        arrays[name] = np.ascontiguousarray(a)
    c = 128
    arrays["c_ident"] = np.eye(c, dtype=np.float32)
    arrays["c_center"] = (np.eye(c) - 1.0 / c).astype(np.float32)
    arrays["c_mean"] = np.full((c, c), 1.0 / c, np.float32)
    arrays["c_group_mean"] = (np.kron(np.eye(32), np.ones((4, 4))) / 4).astype(np.float32)
    k, pad, half = 7, (256 - 7) // 2, 128
    p, q = np.divmod(np.arange(k * k), k)
    turns = (p + pad)[:, None, None] * np.arange(half)[None, :, None] + (q + pad)[:, None, None] * np.arange(256)[None, None, :]
    angle = (2 * np.pi / 256) * (turns % 256).reshape(k * k, -1)
    arrays["c_table"] = np.concatenate([np.cos(angle), np.sin(angle)]).astype(np.float32)
    odd = np.tile((-1.0) ** p, 2)
    arrays["c_sign"] = np.stack([np.repeat([1.0, -1.0], k * k), odd], 1).astype(np.float32)
    return arrays
```
